# Optimizing a Trainium2 kernel written in Bass

```python
import numpy as np
import jax
import jax.numpy as jnp

def _softmax(x, axis=-1):
    return jax.nn.softmax(x, axis=axis)

def _gelu(x):
    return jax.nn.gelu(x, approximate=True)

def _silu(x):
    return jax.nn.silu(x)

def _sigmoid(x):
    return jax.nn.sigmoid(x)

def _layernorm(x, axis=-1, eps=1e-05):
    m = jnp.mean(x, axis=axis, keepdims=True)
    v = jnp.var(x, axis=axis, keepdims=True)
    return (x - m) / jnp.sqrt(v + eps)

def _scatter_add(tgt, idx, src, axis=0):
    return tgt.at[idx].add(src)

def _segment_sum(src, seg, n):
    return jax.ops.segment_sum(src, seg, n)
kernel_name = 'mk_gps_d1_gnn_r32_d2af82'

def setup_inputs(seed: int=0):
    np.random.seed(seed)
    _w = jnp.asarray

    def _rec_inputs():
        import jax
        import jax.numpy as jnp
        _gk = jax.random.key(seed)
        x = -0.0003713 + 1 * jax.random.normal(jax.random.fold_in(_gk, 1), (3125, 256), jnp.float32)
        _s = jax.random.randint(jax.random.fold_in(_gk, 2), (25000,), 0, 3125, jnp.int32)
        _d = jax.random.randint(jax.random.fold_in(_gk, 3), (25000,), 0, 3125, jnp.int32)
        _loop = jnp.arange(3125, dtype=jnp.int32)
        src = jnp.concatenate([_s, _d, _loop])
        dst = jnp.concatenate([_d, _s, _loop])
        _o = jnp.argsort(dst, stable=True)
        src = src[_o]
        dst = dst[_o]
        return (x, src, dst)
    x, src, dst = _rec_inputs()

    def _L0_gnn_setup():
        import jax, jax.numpy as jnp
        import numpy as np
        N = 50000
        E = 25000
        HEADS = 4
        C = 64
        IN = 256
        NEG_SLOPE = 0.2

        def _gat_forward(x, edge_index, W, att_src, att_dst, bias):
            n = x.shape[0]
            h = (x @ W).reshape(n, HEADS, C)
            loop = jnp.arange(n, dtype=edge_index.dtype)
            src = jnp.concatenate([edge_index[0], loop])
            dst = jnp.concatenate([edge_index[1], loop])
            a_src = jnp.einsum('nhc,hc->nh', h, att_src)
            a_dst = jnp.einsum('nhc,hc->nh', h, att_dst)
            logits = a_src[src] + a_dst[dst]
            logits = jnp.where(logits >= 0, logits, NEG_SLOPE * logits)
            seg_max = jax.ops.segment_max(logits, dst, num_segments=n)
            seg_max = jnp.where(jnp.isfinite(seg_max), seg_max, 0.0)
            ex = jnp.exp(logits - seg_max[dst])
            denom = jax.ops.segment_sum(ex, dst, num_segments=n)
            alpha = ex / (denom[dst] + 1e-16)
            msgs = alpha[:, :, None] * h[src]
            out = jax.ops.segment_sum(msgs, dst, num_segments=n)
            out = out.reshape(n, HEADS * C) + bias
            return jax.nn.relu(out)
        key = jax.random.key(seed)
        k = jax.random.split(key, 6)
        x = jax.random.normal(k[0], (N, IN), dtype=jnp.float32)
        edge_index = jax.random.randint(k[1], (2, E), 0, N, dtype=jnp.int64)
        W = jax.random.normal(k[2], (IN, HEADS * C), dtype=jnp.float32) * (1.0 / np.sqrt(IN))
        att_src = jax.random.normal(k[3], (HEADS, C), dtype=jnp.float32) * (1.0 / np.sqrt(C))
        att_dst = jax.random.normal(k[4], (HEADS, C), dtype=jnp.float32) * (1.0 / np.sqrt(C))
        bias = jax.random.normal(k[5], (HEADS * C,), dtype=jnp.float32) * 0.02
        return {'x': x, 'edge_index': edge_index, 'W': W, 'att_src': att_src, 'att_dst': att_dst, 'bias': bias}
    _L0_gnn_all = _L0_gnn_setup()
    _L0_gnn_in = {k: v for k, v in _L0_gnn_all.items() if k in ('W', 'att_src', 'att_dst', 'bias')}
    del _L0_gnn_all

    def _L0_mix_setup():
        import jax, jax.numpy as jnp
        import numpy as np
        HEADS = 4
        DIM_HEAD = 32
        key = jax.random.key(seed)
        k1, k2, k3 = jax.random.split(key, 3)
        B, L, D = (16, 256, 256)
        hidden = HEADS * DIM_HEAD
        x = jax.random.normal(k1, (B, L, D), dtype=jnp.float32)
        W_qkv = jax.random.normal(k2, (D, 3 * hidden), dtype=jnp.float32) * D ** (-0.5)
        W_out = jax.random.normal(k3, (hidden, D), dtype=jnp.float32) * hidden ** (-0.5)
        b_out = jnp.zeros((D,), dtype=jnp.float32)
        return {'x': x, 'W_qkv': W_qkv, 'W_out': W_out, 'b_out': b_out}
    _L0_mix_all = _L0_mix_setup()
    _L0_mix_in = {k: v for k, v in _L0_mix_all.items() if k in ('W_qkv', 'W_out', 'b_out')}
    del _L0_mix_all

    def _L0_ffn_setup():
        import jax, jax.numpy as jnp
        import numpy as np
        TOP_K = 2
        key = jax.random.key(seed)
        ks = jax.random.split(key, 4)
        B, L, D, H, E = (8, 128, 256, 1024, 8)
        s = 0.02
        return {'x': jax.random.normal(ks[0], (B, L, D), jnp.float32), 'Wg': jax.random.normal(ks[1], (D, E), jnp.float32) * s, 'bg': jnp.zeros((E,), jnp.float32), 'W1': jax.random.normal(ks[2], (E, D, H), jnp.float32) * s, 'b1': jnp.zeros((E, H), jnp.float32), 'W2': jax.random.normal(ks[3], (E, H, D), jnp.float32) * s, 'b2': jnp.zeros((E, D), jnp.float32)}
    _L0_ffn_all = _L0_ffn_setup()
    _L0_ffn_in = {k: v for k, v in _L0_ffn_all.items() if k in ('Wg', 'bg', 'W1', 'b1', 'W2', 'b2')}
    del _L0_ffn_all
    return {'x': x, 'src': src, 'dst': dst, 'L0_gnn_W': _L0_gnn_in['W'], 'L0_gnn_att_src': _L0_gnn_in['att_src'], 'L0_gnn_att_dst': _L0_gnn_in['att_dst'], 'L0_gnn_bias': _L0_gnn_in['bias'], 'L0_mix_W_qkv': _L0_mix_in['W_qkv'], 'L0_mix_W_out': _L0_mix_in['W_out'], 'L0_mix_b_out': _L0_mix_in['b_out'], 'L0_ffn_Wg': _L0_ffn_in['Wg'], 'L0_ffn_bg': _L0_ffn_in['bg'], 'L0_ffn_W1': _L0_ffn_in['W1'], 'L0_ffn_b1': _L0_ffn_in['b1'], 'L0_ffn_W2': _L0_ffn_in['W2'], 'L0_ffn_b2': _L0_ffn_in['b2']}

def reference(x, src, dst, L0_gnn_W, L0_gnn_att_src, L0_gnn_att_dst, L0_gnn_bias, L0_mix_W_qkv, L0_mix_W_out, L0_mix_b_out, L0_ffn_Wg, L0_ffn_bg, L0_ffn_W1, L0_ffn_b1, L0_ffn_W2, L0_ffn_b2):
    import jax
    import jax.numpy as jnp

    def _L0_gnn_ref(x, edge_index, W, att_src, att_dst, bias):
        import jax, jax.numpy as jnp
        import numpy as np
        N = 50000
        E = 25000
        HEADS = 4
        C = 64
        IN = 256
        NEG_SLOPE = 0.2

        def _gat_forward(x, edge_index, W, att_src, att_dst, bias):
            n = x.shape[0]
            h = (x @ W).reshape(n, HEADS, C)
            loop = jnp.arange(n, dtype=edge_index.dtype)
            src = jnp.concatenate([edge_index[0], loop])
            dst = jnp.concatenate([edge_index[1], loop])
            a_src = jnp.einsum('nhc,hc->nh', h, att_src)
            a_dst = jnp.einsum('nhc,hc->nh', h, att_dst)
            logits = a_src[src] + a_dst[dst]
            logits = jnp.where(logits >= 0, logits, NEG_SLOPE * logits)
            seg_max = jax.ops.segment_max(logits, dst, num_segments=n)
            seg_max = jnp.where(jnp.isfinite(seg_max), seg_max, 0.0)
            ex = jnp.exp(logits - seg_max[dst])
            denom = jax.ops.segment_sum(ex, dst, num_segments=n)
            alpha = ex / (denom[dst] + 1e-16)
            msgs = alpha[:, :, None] * h[src]
            out = jax.ops.segment_sum(msgs, dst, num_segments=n)
            out = out.reshape(n, HEADS * C) + bias
            return jax.nn.relu(out)
        return _gat_forward(x, edge_index, W, att_src, att_dst, bias)

    def _L0_mix_ref(x, W_qkv, W_out, b_out):
        import jax, jax.numpy as jnp
        import numpy as np
        HEADS = 4
        DIM_HEAD = 32
        B, L, D = x.shape
        scale = DIM_HEAD ** (-0.5)
        qkv = jnp.einsum('bld,df->blf', x, W_qkv)
        qkv = qkv.reshape(B, L, 3, HEADS, DIM_HEAD)
        q = jnp.transpose(qkv[:, :, 0], (0, 2, 1, 3)) * scale
        k = jax.nn.softmax(jnp.transpose(qkv[:, :, 1], (0, 2, 1, 3)), axis=2)
        v = jnp.transpose(qkv[:, :, 2], (0, 2, 1, 3))
        context = jnp.einsum('bhld,bhle->bhde', k, v)
        out = jnp.einsum('bhde,bhld->bhle', context, q)
        out = jnp.transpose(out, (0, 2, 1, 3)).reshape(B, L, HEADS * DIM_HEAD)
        return jnp.einsum('blf,fd->bld', out, W_out) + b_out

    def _L0_ffn_ref(x, Wg, bg, W1, b1, W2, b2):
        import jax, jax.numpy as jnp
        import numpy as np
        TOP_K = 2
        B, L, D = x.shape
        E = W1.shape[0]
        xf = x.reshape(-1, D)
        gate_logits = xf @ Wg + bg
        top_w, top_i = jax.lax.top_k(gate_logits, TOP_K)
        top_w = jax.nn.softmax(top_w, axis=-1)
        w_dense = jnp.sum(jax.nn.one_hot(top_i, E, dtype=xf.dtype) * top_w[..., None], axis=1)
        out = jnp.zeros_like(xf)
        for e in range(E):
            h = jax.nn.gelu(xf @ W1[e] + b1[e], approximate=False)
            out = out + w_dense[:, e:e + 1] * (h @ W2[e] + b2[e])
        return out.reshape(B, L, D)
    edge_index = jnp.stack([src, dst])
    xn = _layernorm(x, axis=-1)
    x = x + _L0_gnn_ref(xn, edge_index, L0_gnn_W, L0_gnn_att_src, L0_gnn_att_dst, L0_gnn_bias) + _L0_mix_ref(xn[None], L0_mix_W_qkv, L0_mix_W_out, L0_mix_b_out)[0]
    x = x + _L0_ffn_ref(_layernorm(x, axis=-1)[None], L0_ffn_Wg, L0_ffn_bg, L0_ffn_W1, L0_ffn_b1, L0_ffn_W2, L0_ffn_b2)[0]
    return x

_drawn_inputs = setup_inputs


def setup_inputs(seed=0):
    import zlib

    import numpy as np

    out = dict(_drawn_inputs(seed))
    spreads = {'L0_mix_b_out': (0.0, 0.1),
     'L0_ffn_bg': (0.0, 0.1),
     'L0_ffn_b1': (0.0, 0.312),
     'L0_ffn_b2': (0.0, 0.1)}
    factors = {'L0_gnn_bias': 3.17}
    for name, (base, spread) in spreads.items():
        noise = np.random.default_rng([zlib.crc32(name.encode()), seed]).standard_normal(out[name].shape)
        drawn = base * np.exp(spread * noise) if base else spread * noise
        out[name] = jnp.asarray(drawn.astype(out[name].dtype))
    for name, factor in factors.items():
        out[name] = (out[name] * factor).astype(out[name].dtype)
    return out
```

```python
from contextlib import ExitStack

import concourse.bass as bass
from concourse import mybir

F32 = mybir.dt.float32
BF16 = mybir.dt.bfloat16
I32 = mybir.dt.int32
U32 = mybir.dt.uint32
ALU = mybir.AluOpType
ACT = mybir.ActivationFunctionType
AX = mybir.AxisListType

P = 128
N = 3125
D = 256
NT = -(-N // P)
NPAD = NT * P
LAST = N - (NT - 1) * P
KD = D // P
HEADS = 4
C = D // HEADS
ROW = D + HEADS
HID = 128
DH = HID // HEADS
E = 53125
ET = -(-E // P)
EQ = ET // 4
NB = NT
BIG = 16384.0
CH = 448
G = 4
RING = 4
NGRP = CH // G
MAXCHUNK = -(-(ET * NB) // CH)
VCOL = 84
NX = 8
FF = 1024
KF = FF // P
NCHOICE = 2 * NT
UT = (2 * NPAD + NX * (P - 1)) // P
SLOTS = UT * P
UNROLL = 5
CONSTS = 6
EPS = 1e-5
SLOPE = 0.2
QSCALE = float(DH) ** -0.5
NEG = -3.0e38

assert ET % 4 == 0 and NT % UNROLL == 0 and P * VCOL >= MAXCHUNK * CH and NGRP % RING == 0 and EQ <= P


def flat(ap):
    return ap.rearrange("p a b -> p (a b)")


class Chain:

    def __init__(self, sem):
        self.sem, self.n = sem, 0

    def done(self, instruction):
        self.n += 1
        instruction.then_inc(self.sem, 1)


def graph_layer(nc, x, src, dst, w_gat, att_src, att_dst, gat_bias, w_qkv, w_out, b_out,
                w_gate, b_gate, w1, b1, w2, b2, out):
    h_table = nc.dram_tensor("h_table", (NPAD, ROW), F32, kind="Internal").ap()
    visit_tile = nc.dram_tensor("visit_tile", (P * VCOL,), I32, kind="Internal").ap()
    visit_block = nc.dram_tensor("visit_block", (P * VCOL,), I32, kind="Internal").ap()
    slot_x = nc.dram_tensor("slot_x", (SLOTS, D), F32, kind="Internal").ap()
    slot_y = nc.dram_tensor("slot_y", (SLOTS, D), F32, kind="Internal").ap()

    with ExitStack() as whole:
        def sem(name):
            return whole.enter_context(nc.semaphore(name))

        def sb(scope, name, shape, dtype=F32):
            return scope.enter_context(nc.sbuf_tensor(name, shape, dtype))

        bank = [whole.enter_context(nc.psum_tensor(f"bank{k}", [P, 512], F32)) for k in range(8)]

        ident = sb(whole, "ident", [P, P])
        ones = sb(whole, "ones", [P, P])
        xs = sb(whole, "xs", [P, NT, D])
        acc = sb(whole, "acc", [P, NB + 1, ROW])
        stats = sb(whole, "stats", [P, NT, 6])
        moments = sb(whole, "moments", [P, NT, 2])
        rstd = sb(whole, "rstd", [P, NT])
        gat_bias_sb = sb(whole, "gat_bias_sb", [P, D])
        iota_row = sb(whole, "iota_row", [P, P])
        adc = sb(whole, "adc", [P, NB + 1, 2 * HEADS])
        src_col = sb(whole, "src_col", [P, ET])
        dst_col = sb(whole, "dst_col", [P, ET])
        minus_base = sb(whole, "minus_base", [P, NB + 1])
        chunks_i = sb(whole, "chunks_i", [1, 1], I32)
        eps_col = sb(whole, "eps_col", [P, 1])

        weights_in = sem("weights_in")
        w1_in = sem("w1_in")
        bias_in = sem("bias_in")
        self_ready = sem("self_ready")

        with ExitStack() as early:
            xnT = sb(early, "xnT", [P, NT, D])
            hs = sb(early, "hs", [P, NT, D + 2 * HEADS])
            kv = sb(early, "kv", [P, NT, 2 * HID + 1])
            w_h = sb(early, "w_h", [P, KD, D + 2 * HEADS])
            w_kv = sb(early, "w_kv", [P, KD, 2 * HID])
            w_q = sb(early, "w_q", [P, KD, HID])
            w_o = sb(early, "w_o", [P, D])
            b_o = sb(early, "b_o", [1, D])
            tile_min = sb(early, "tile_min", [EQ, 4])
            tile_max = sb(early, "tile_max", [EQ, 4])
            with ExitStack() as scope:
                xn = sb(scope, "xn", [P, UNROLL, D])
                xnT_slot = sb(scope, "xnT_slot", [P, UNROLL, D])
                att = sb(scope, "att", [P, 2, D])
                att_w = sb(scope, "att_w", [P, KD, D])
                edge_i = sb(scope, "edge_i", [EQ, 2, 4 * P], I32)
                edge_f = sb(scope, "edge_f", [EQ, 2, 4 * P])

                x_in = [sem(f"x_in{k}") for k in range(3)]
                edges_in = sem("edges_in")
                x_padded = sem("x_padded")
                edges_padded = sem("edges_padded")
                consts = sem("consts")
                stats_ready = sem("stats_ready")
                std_ready = sem("std_ready")
                w_ready = sem("w_ready")
                xn_ready = sem("xn_ready")
                turned = sem("turned")
                xnT_kept = sem("xnT_kept")
                moments_ready = sem("moments_ready")
                xnT_ready = sem("xnT_ready")
                projected = sem("projected")
                h_copied = sem("h_copied")
                kv_copied = sem("kv_copied")
                h_stored = sem("h_stored")
                edges_f = sem("edges_f")
                edges_turned = sem("edges_turned")
                edges_done = sem("edges_done")
                v1 = Chain(sem("v1"))
                g1 = Chain(sem("g1"))

                with nc.Block() as block:
                    @block.sync
                    def _(sp):
                        half = (NT - 1) // 2
                        rows = x[0:(NT - 1) * P, :].rearrange("(t p) d -> p t d", p=P)
                        sp.dma_start(xs[:, 0:half, :], rows[:, 0:half, :]).then_inc(x_in[0], 16)
                        sp.dma_start(xs[:, half:NT - 1, :], rows[:, half:, :]).then_inc(x_in[1], 16)
                        sp.wait_ge(x_padded, 1)
                        sp.dma_start(xs[0:LAST, NT - 1, :], x[(NT - 1) * P:N, :]).then_inc(x_in[2], 16)
                        sp.wait_ge(edges_padded, 2)
                        full = E // (4 * P)
                        for j, edge in ((0, src), (1, dst)):
                            sp.dma_start(edge_i[0:full, j, :],
                                         edge[0:full * 4 * P].rearrange("(q e) -> q e", e=4 * P)).then_inc(edges_in, 16)
                            sp.dma_start(edge_i[full:full + 1, j, 0:E - full * 4 * P],
                                         edge[full * 4 * P:E].rearrange("(q e) -> q e", q=1)).then_inc(edges_in, 16)
                        with sp.Fori(0, NT) as t:
                            sp.wait_ge(h_copied, t + 1)
                            sp.dma_start(h_table.rearrange("(t p) r -> p t r", p=P)[:, bass.ds(t, 1), :],
                                         hs[:, bass.ds(t, 1), 0:ROW]).then_inc(h_stored, 16)
                        sp.wait_ge(h_stored, 16 * NT)

                    @block.gpsimd
                    def _(pool):
                        pool.memset(xs[:, NT - 1, :], 0.0).then_inc(x_padded, 1)
                        pool.memset(edge_i[:, 0, :], 0).then_inc(edges_padded, 1)
                        pool.memset(edge_i[:, 1, :], 4095).then_inc(edges_padded, 1)
                        g1.done(pool.memset(ident[:, :], 0.0))
                        pool.wait_ge(g1.sem, g1.n)
                        pool.affine_select(out=ident[:, :], in_=ident[:, :], compare_op=ALU.not_equal, fill=1.0,
                                           base=0, pattern=[[-1, P]], channel_multiplier=1).then_inc(consts, 1)
                        pool.memset(ones[:, :], 1.0).then_inc(consts, 1)
                        pool.memset(eps_col[:, :], EPS).then_inc(consts, 1)
                        pool.iota(iota_row[:, :], [[1, P]], base=0, channel_multiplier=0,
                                  allow_small_or_imprecise_dtypes=True).then_inc(consts, 1)
                        pool.iota(minus_base[:, :], [[-P, NB + 1]], base=0, channel_multiplier=0,
                                  allow_small_or_imprecise_dtypes=True).then_inc(consts, 1)
                        pool.memset(kv[:, :, 2 * HID:2 * HID + 1], 1.0).then_inc(consts, 1)

                    @block.scalar
                    def _(act):
                        act.dma_start(w_h[:, :, 0:D], w_gat.rearrange("(k p) n -> p k n", p=P)).then_inc(weights_in, 16)
                        act.dma_start(w_q[:, :, :], w_qkv[:, 0:HID].rearrange("(k p) n -> p k n", p=P)).then_inc(weights_in, 16)
                        act.dma_start(w_kv[:, :, :], w_qkv[:, HID:3 * HID].rearrange("(k p) n -> p k n", p=P)).then_inc(weights_in, 16)
                        act.dma_start(att[:, 0, :], att_src.rearrange("h c -> (h c)").partition_broadcast(P)).then_inc(weights_in, 16)
                        act.dma_start(att[:, 1, :], att_dst.rearrange("h c -> (h c)").partition_broadcast(P)).then_inc(weights_in, 16)
                        act.dma_start(w_o[:, :], w_out).then_inc(bias_in, 16)
                        act.dma_start(b_o[:, :], b_out.rearrange("(a d) -> a d", a=1)).then_inc(bias_in, 16)
                        act.dma_start(gat_bias_sb[:, :], gat_bias.partition_broadcast(P)).then_inc(bias_in, 16)
                        act.wait_ge(moments_ready, NT)
                        act.wait_ge(consts, CONSTS)
                        act.activation(rstd[:, :], moments[:, :, 1], ACT.Sqrt, bias=eps_col[:, :]).then_inc(std_ready, 1)
                        with act.Fori(0, NT // UNROLL) as i:
                            for k in range(UNROLL):
                                t = i * UNROLL + k
                                act.wait_ge(turned, t + 1 + UNROLL)
                                act.wait_ge(projected, t + 1)
                                rows_T = bank[k % 2][:, 0:D]
                                act.activation(xnT_slot[:, k, :], rows_T, ACT.Copy).then_inc(xnT_ready, 1)
                                act.activation(flat(xnT[:, bass.ds(t, 1), :]), rows_T, ACT.Copy).then_inc(xnT_kept, 1)
                                if k >= 1:
                                    act.wait_ge(projected, t + UNROLL)
                                    act.activation(flat(kv[:, bass.ds(t - 1, 1), 0:2 * HID]),
                                                   bank[4 + 2 * ((k - 1) % 2)][:, 0:2 * HID], ACT.Copy).then_inc(kv_copied, 1)
                            act.wait_ge(projected, i * UNROLL + 2 * UNROLL)
                            act.activation(flat(kv[:, bass.ds(i * UNROLL + UNROLL - 1, 1), 0:2 * HID]),
                                           bank[4 + 2 * ((UNROLL - 1) % 2)][:, 0:2 * HID], ACT.Copy).then_inc(kv_copied, 1)

                    @block.tensor
                    def _(pe):
                        pe.sem_inc(turned, UNROLL)
                        pe.sem_inc(projected, UNROLL)
                        pe.wait_ge(consts, CONSTS)
                        pe.wait_ge(w_ready, 1)
                        with pe.Fori(0, NT // UNROLL) as i:
                            def turn(k):
                                pe.wait_ge(xn_ready, i * UNROLL + k + 1)
                                pe.wait_ge(xnT_kept, i * UNROLL + (k if k == 0 else k - 1))
                                for c in range(KD):
                                    tr = pe.transpose(bank[k % 2][:, c * P:(c + 1) * P],
                                                      xn[:, k, c * P:(c + 1) * P], ident[:, :])
                                tr.then_inc(turned, 1)

                            turn(0)
                            for k in range(UNROLL):
                                t = i * UNROLL + k
                                if k + 1 < UNROLL:
                                    turn(k + 1)
                                pe.wait_ge(xnT_ready, t + 1)
                                before = t if k == 0 else t - 1
                                pe.wait_ge(h_copied, before)
                                pe.wait_ge(kv_copied, before)
                                for c in range(KD):
                                    pe.matmul(bank[3 + 2 * (k % 2)][:, 0:D + 2 * HEADS], xnT_slot[:, k, c * P:(c + 1) * P],
                                              w_h[:, c, :], start=(c == 0), stop=(c == KD - 1))
                                for c in range(KD):
                                    mm = pe.matmul(bank[4 + 2 * (k % 2)][:, 0:2 * HID], xnT_slot[:, k, c * P:(c + 1) * P],
                                                   w_kv[:, c, :], start=(c == 0), stop=(c == KD - 1))
                                mm.then_inc(projected, 1)
                        pe.wait_ge(edges_f, 2)
                        pe.wait_ge(xnT_kept, NT)
                        for j in range(2):
                            for q in range(4):
                                tr = pe.transpose(bank[j][:, q * EQ:(q + 1) * EQ], edge_f[:, j, q * P:(q + 1) * P],
                                                  ident[0:EQ, 0:EQ])
                            tr.then_inc(edges_turned, 1)

                    @block.vector
                    def _(dve):
                        dve.wait_ge(weights_in, 80)
                        for j in range(2):
                            if j:
                                dve.wait_ge(v1.sem, v1.n)
                            v1.done(dve.tensor_tensor(att_w[:, :, :], w_h[:, :, 0:D],
                                                      att[:, j:j + 1, :].broadcast_to((P, KD, D)), ALU.mult))
                            dve.wait_ge(v1.sem, v1.n)
                            v1.done(dve.tensor_reduce(w_h[:, :, D + j * HEADS:D + (j + 1) * HEADS],
                                                      att_w[:, :, :].rearrange("p k (h c) -> p k h c", c=C), AX.X, ALU.add))
                        dve.wait_ge(v1.sem, v1.n)
                        dve.sem_inc(w_ready, 1)
                        dve.wait_ge(x_in[0], 16)
                        for first, end in ((0, (NT - 1) // 2), ((NT - 1) // 2, NT)):
                            if first:
                                dve.wait_ge(x_in[1], 16)
                                dve.wait_ge(x_in[2], 16)
                            with dve.Fori(first, end) as t:
                                dve.bn_stats(flat(stats[:, bass.ds(t, 1), :]), flat(xs[:, bass.ds(t, 1), :])).then_inc(stats_ready, 1)
                        dve.wait_ge(stats_ready, NT)
                        for t in range(NT):
                            dve.bn_aggr(moments[:, t, :], stats[:, t, :]).then_inc(moments_ready, 1)
                        dve.wait_ge(std_ready, 1)
                        v1.done(dve.reciprocal(rstd[:, :], rstd[:, :]))
                        dve.wait_ge(v1.sem, v1.n)
                        with dve.Fori(0, NT // UNROLL) as i:
                            for k in range(UNROLL):
                                t = i * UNROLL + k
                                dve.wait_ge(turned, t + 1)
                                dve.tensor_scalar(xn[:, k, :], flat(xs[:, bass.ds(t, 1), :]),
                                                  flat(moments[:, bass.ds(t, 1), 0:1]),
                                                  rstd[:, bass.ds(t, 1)], ALU.subtract, ALU.mult).then_inc(xn_ready, 1)
                                if k >= 1:
                                    dve.wait_ge(projected, t + UNROLL)
                                    dve.tensor_copy(flat(hs[:, bass.ds(t - 1, 1), :]),
                                                    bank[3 + 2 * ((k - 1) % 2)][:, 0:D + 2 * HEADS]).then_inc(h_copied, 1)
                            dve.wait_ge(projected, i * UNROLL + 2 * UNROLL)
                            dve.tensor_copy(flat(hs[:, bass.ds(i * UNROLL + UNROLL - 1, 1), :]),
                                            bank[3 + 2 * ((UNROLL - 1) % 2)][:, 0:D + 2 * HEADS]).then_inc(h_copied, 1)
                        dve.wait_ge(edges_in, 64)
                        for j in range(2):
                            dve.tensor_copy(edge_f[:, j, :], edge_i[:, j, :]).then_inc(edges_f, 1)
                        dve.wait_ge(edges_f, 2)
                        by_tile = edge_f[:, 1, :].rearrange("q (k e) -> q k e", e=P)
                        dve.tensor_reduce(tile_min[:, :], by_tile, AX.X, ALU.min).then_inc(edges_done, 1)
                        dve.tensor_reduce(tile_max[:, :], by_tile, AX.X, ALU.max).then_inc(edges_done, 1)
                        for j, column in ((0, src_col), (1, dst_col)):
                            dve.wait_ge(edges_turned, j + 1)
                            dve.tensor_copy(column[:, :].rearrange("p (q k) -> p k q", k=4),
                                            bank[j][:, 0:4 * EQ].rearrange("p (k q) -> p k q", k=4)).then_inc(edges_done, 1)
                        dve.wait_ge(edges_done, 4)
                        dve.wait_ge(h_copied, NT)

            with ExitStack() as scope:
                kmax = sb(scope, "kmax", [P, HID])
                kcol = sb(scope, "kcol", [P, 1])
                kdiag = sb(scope, "kdiag", [P, P])
                head_mask = sb(scope, "head_mask", [P, HID])
                key_sum = sb(scope, "key_sum", [P, 1])
                ctx = sb(scope, "ctx", [P, HID])
                ctxT = sb(scope, "ctxT", [P, HID])
                ctx_out = sb(scope, "ctx_out", [P, D])
                w_qT = sb(scope, "w_qT", [P, D])
                w_mix = sb(scope, "w_mix", [P, KD, D])
                mix_slot = sb(scope, "mix_slot", [P, UNROLL, D])
                amax_p = sb(scope, "amax_p", [P, HEADS])
                amax_c = sb(scope, "amax_c", [HEADS, 1])
                amax_d = sb(scope, "amax_d", [HEADS, HEADS])
                amax = sb(scope, "amax", [P, HEADS])
                self_z = sb(scope, "self_z", [P, NT, HEADS])
                block_lo = sb(scope, "block_lo", [P, NB])
                tile_id = sb(scope, "tile_id", [P, 4])
                has = sb(scope, "has", [EQ, 4, NB])
                has2 = sb(scope, "has2", [EQ, 4, NB])
                first_q = sb(scope, "first_q", [EQ, NB])
                last_q = sb(scope, "last_q", [EQ, NB])
                span = sb(scope, "span", [NB, 4])
                upto = sb(scope, "upto", [P, P])
                span_rows = sb(scope, "span_rows", [NB, 3 * NB])
                rows = sb(scope, "rows", [P, 3 * NB])
                visit_id = sb(scope, "visit_id", [P, VCOL])
                past = sb(scope, "past", [P, VCOL, NB])
                within = sb(scope, "within", [P, VCOL, NB])
                vb = sb(scope, "vb", [P, VCOL])
                vt = sb(scope, "vt", [P, VCOL])
                vb_i = sb(scope, "vb_i", [P, VCOL], I32)
                vt_i = sb(scope, "vt_i", [P, VCOL], I32)
                chunk_lo = sb(scope, "chunk_lo", [1, MAXCHUNK])

                pool_ready = sem("pool_ready")
                kmax_ready = sem("kmax_ready")
                kmax_turned = sem("kmax_turned")
                kdiag_ready = sem("kdiag_ready")
                kmax_spread = sem("kmax_spread")
                keys_shifted = sem("keys_shifted")
                keys_exp = sem("keys_exp")
                ctx_summed = sem("ctx_summed")
                ctx_ready = sem("ctx_ready")
                ctx_turned = sem("ctx_turned")
                ctxT_ready = sem("ctxT_ready")
                ctx_out_summed = sem("ctx_out_summed")
                ctx_out_ready = sem("ctx_out_ready")
                w_q_turned = sem("w_q_turned")
                w_qT_ready = sem("w_qT_ready")
                w_mix_summed = sem("w_mix_summed")
                w_mix_ready = sem("w_mix_ready")
                slot_ready = sem("slot_ready")
                mixed = sem("mixed")
                mix_added = sem("mix_added")
                amax_ready = sem("amax_ready")
                amax_turned = sem("amax_turned")
                amax_diag = sem("amax_diag")
                amax_spread = sem("amax_spread")
                self_logits = sem("self_logits")
                self_exp = sem("self_exp")
                spans_ready = sem("spans_ready")
                spans_turned = sem("spans_turned")
                rows_ready = sem("rows_ready")
                rows_spread = sem("rows_spread")
                visits_ready = sem("visits_ready")
                visits_stored = sem("visits_stored")
                v2 = Chain(sem("v2"))
                g2 = Chain(sem("g2"))

                with nc.Block() as block:
                    @block.gpsimd
                    def _(pool):
                        pool.iota(block_lo[:, :], [[P, NB]], base=0, channel_multiplier=0,
                                  allow_small_or_imprecise_dtypes=True).then_inc(pool_ready, 1)
                        pool.iota(tile_id[:, :], [[1, 4]], base=0, channel_multiplier=4,
                                  allow_small_or_imprecise_dtypes=True).then_inc(pool_ready, 1)
                        pool.iota(visit_id[:, :], [[1, VCOL]], base=0, channel_multiplier=VCOL,
                                  allow_small_or_imprecise_dtypes=True).then_inc(pool_ready, 1)
                        pool.iota(chunk_lo[:, :], [[CH, MAXCHUNK]], base=0, channel_multiplier=0,
                                  allow_small_or_imprecise_dtypes=True).then_inc(pool_ready, 1)
                        g2.done(pool.memset(upto[:, :], 1.0))
                        pool.wait_ge(g2.sem, g2.n)
                        pool.affine_select(out=upto[:, :], in_=upto[:, :], compare_op=ALU.is_ge, fill=0.0,
                                           base=0, pattern=[[1, P]], channel_multiplier=-1).then_inc(pool_ready, 1)
                        g2.done(pool.memset(head_mask[:, :], 0.0))
                        pool.wait_ge(g2.sem, g2.n)
                        for h in range(HEADS):
                            g2.done(pool.memset(head_mask[h * DH:(h + 1) * DH, h * DH:(h + 1) * DH], 1.0))
                            pool.wait_ge(g2.sem, g2.n)
                        pool.memset(acc[:, NB, :], 0.0).then_inc(pool_ready, 1)
                        pool.memset(adc[:, NB, :], 0.0).then_inc(pool_ready, 1)

                    @block.vector
                    def _(dve):
                        def after(instruction):
                            v2.done(instruction)
                            dve.wait_ge(v2.sem, v2.n)

                        after(dve.tensor_reduce(kmax[:, :], kv[:, 0:NT - 1, 0:HID].rearrange("p t c -> p c t"), AX.X, ALU.max))
                        dve.tensor_tensor(kmax[0:LAST, :], kmax[0:LAST, :], kv[0:LAST, NT - 1, 0:HID], ALU.max).then_inc(kmax_ready, 1)
                        dve.tensor_reduce(amax_p[:, :], hs[:, :, D:D + HEADS].rearrange("p t h -> p h t"), AX.X, ALU.max).then_inc(amax_ready, 1)
                        dve.wait_ge(kmax_turned, 1)
                        after(dve.tensor_reduce(kcol[:, :], bank[0][:, 0:P], AX.X, ALU.max))
                        dve.tensor_scalar(kdiag[:, :], ident[:, :], kcol[:, 0:1], None, ALU.mult).then_inc(kdiag_ready, 1)
                        dve.wait_ge(amax_turned, 1)
                        after(dve.tensor_reduce(amax_c[:, :], bank[1][0:HEADS, 0:P], AX.X, ALU.max))
                        dve.tensor_scalar(amax_d[:, :], ident[0:HEADS, 0:HEADS], amax_c[:, 0:1], None, ALU.mult).then_inc(amax_diag, 1)
                        dve.wait_ge(kmax_spread, 1)
                        for i in range(NT // UNROLL):
                            keys = kv[:, i * UNROLL:(i + 1) * UNROLL, 0:HID]
                            dve.tensor_tensor(keys, keys, bank[2][:, 0:HID].unsqueeze(1).broadcast_to((P, UNROLL, HID)),
                                              ALU.subtract).then_inc(keys_shifted, 1)
                        dve.wait_ge(amax_spread, 1)
                        after(dve.tensor_copy(amax[:, :], bank[3][:, 0:HEADS]))
                        a_src, a_dst = hs[:, :, D:D + HEADS], hs[:, :, D + HEADS:D + 2 * HEADS]
                        logit, shift = adc[:, 0:NB, 0:HEADS], adc[:, 0:NB, HEADS:2 * HEADS]
                        dve.tensor_copy(logit, a_dst)
                        after(dve.tensor_tensor(shift, a_dst, amax[:, :].unsqueeze(1).broadcast_to((P, NT, HEADS)), ALU.add))
                        after(dve.scalar_tensor_tensor(out=shift, in0=shift, scalar=SLOPE, in1=shift, op0=ALU.mult, op1=ALU.max))
                        after(dve.tensor_tensor(self_z[:, :, :], a_src, a_dst, ALU.add))
                        after(dve.scalar_tensor_tensor(out=self_z[:, :, :], in0=self_z[:, :, :], scalar=SLOPE, in1=self_z[:, :, :],
                                                       op0=ALU.mult, op1=ALU.max))
                        dve.tensor_tensor(self_z[:, :, :], self_z[:, :, :], shift, ALU.subtract).then_inc(self_logits, 1)

                        dve.wait_ge(pool_ready, 7)
                        wide = (EQ, 4, NB)
                        blocks = block_lo[0:EQ, :].unsqueeze(1).broadcast_to(wide)
                        after(dve.tensor_scalar(tile_min[:, :], tile_min[:, :], -float(P - 1), None, ALU.add))
                        dve.tensor_tensor(has[:, :, :], blocks, tile_min[:, :].unsqueeze(2).broadcast_to(wide), ALU.is_ge)
                        after(dve.tensor_tensor(has2[:, :, :], blocks, tile_max[:, :].unsqueeze(2).broadcast_to(wide), ALU.is_le))
                        after(dve.tensor_tensor(has[:, :, :], has[:, :, :], has2[:, :, :], ALU.mult))
                        after(dve.tensor_scalar(tile_id[:, :], tile_id[:, :], 1.0, None, ALU.add))
                        after(dve.tensor_tensor(has2[:, :, :], has[:, :, :], tile_id[0:EQ, :].unsqueeze(2).broadcast_to(wide), ALU.mult))
                        dve.tensor_reduce(last_q[:, :], has2[:, :, :].rearrange("q k b -> q b k"), AX.X, ALU.max)
                        after(dve.tensor_scalar(has[:, :, :], has[:, :, :], -BIG, BIG - 1.0, ALU.mult, ALU.add))
                        after(dve.tensor_tensor(has2[:, :, :], has[:, :, :], tile_id[0:EQ, :].unsqueeze(2).broadcast_to(wide), ALU.add))
                        dve.tensor_reduce(first_q[:, :], has2[:, :, :].rearrange("q k b -> q b k"), AX.X, ALU.min).then_inc(spans_ready, 1)
                        dve.wait_ge(spans_turned, 1)
                        after(dve.tensor_reduce(span[:, 0:1], bank[4][0:NB, 0:EQ], AX.X, ALU.min))
                        after(dve.tensor_reduce(span[:, 1:2], bank[4][0:NB, P:P + EQ], AX.X, ALU.max))
                        after(dve.tensor_tensor(span[:, 2:3], span[:, 1:2], span[:, 0:1], ALU.subtract))
                        after(dve.tensor_scalar(span[:, 3:4], span[:, 2:3], 0.0, None, ALU.max))
                        dve.tensor_scalar(span_rows[:, 0:NB], upto[0:NB, 0:NB], span[:, 3:4], None, ALU.mult)
                        dve.tensor_scalar(span_rows[:, NB:2 * NB], ident[0:NB, 0:NB], span[:, 3:4], None, ALU.mult)
                        dve.tensor_scalar(span_rows[:, 2 * NB:3 * NB], ident[0:NB, 0:NB], span[:, 0:1], None, ALU.mult).then_inc(rows_ready, 1)
                        dve.wait_ge(rows_spread, 1)
                        after(dve.tensor_copy(rows[:, :], bank[5][:, 0:3 * NB]))
                        upto_b, of_b, first_b = rows[:, 0:NB], rows[:, NB:2 * NB], rows[:, 2 * NB:3 * NB]
                        after(dve.tensor_scalar(chunk_lo[:, :], chunk_lo[:, :], rows[0:1, NB - 1:NB], None, ALU.is_lt))
                        after(dve.tensor_reduce(key_sum[0:1, :], chunk_lo[:, :], AX.X, ALU.add))
                        after(dve.tensor_copy(chunks_i[:, :], key_sum[0:1, :]))
                        after(dve.tensor_tensor(of_b, upto_b, of_b, ALU.subtract))
                        after(dve.tensor_tensor(first_b, first_b, of_b, ALU.subtract))
                        grid = (P, VCOL, NB)
                        ids = visit_id[:, :].unsqueeze(2).broadcast_to(grid)
                        dve.tensor_tensor(past[:, :, :], ids, upto_b.unsqueeze(1).broadcast_to(grid), ALU.is_ge)
                        after(dve.tensor_tensor(within[:, :, :], ids, of_b.unsqueeze(1).broadcast_to(grid), ALU.is_ge))
                        dve.tensor_reduce(vb[:, :], past[:, :, :], AX.X, ALU.add)
                        after(dve.tensor_tensor(within[:, :, :], within[:, :, :], past[:, :, :], ALU.subtract))
                        after(dve.tensor_tensor(within[:, :, :], within[:, :, :], first_b.unsqueeze(1).broadcast_to(grid), ALU.mult))
                        after(dve.tensor_reduce(vt[:, :], within[:, :, :], AX.X, ALU.add))
                        after(dve.tensor_tensor(vt[:, :], vt[:, :], visit_id[:, :], ALU.add))
                        after(dve.tensor_scalar(vt[:, :], vt[:, :], float(ET - 1), None, ALU.min))
                        dve.tensor_copy(vt_i[:, :], vt[:, :]).then_inc(visits_ready, 1)
                        dve.tensor_copy(vb_i[:, :], vb[:, :]).then_inc(visits_ready, 1)

                        dve.wait_ge(ctx_summed, 1)
                        after(dve.reciprocal(key_sum[:, :], bank[0][:, HID:HID + 1]))
                        after(dve.tensor_scalar(ctx[:, :], bank[0][:, 0:HID], key_sum[:, 0:1], QSCALE, ALU.mult, ALU.mult))
                        dve.tensor_tensor(ctx[:, :], ctx[:, :], head_mask[:, :], ALU.mult).then_inc(ctx_ready, 1)
                        dve.wait_ge(w_q_turned, 1)
                        dve.tensor_copy(w_qT[:, :], bank[6][:, 0:D]).then_inc(w_qT_ready, 1)
                        dve.wait_ge(ctx_turned, 1)
                        dve.tensor_copy(ctxT[:, :], bank[1][:, 0:P]).then_inc(ctxT_ready, 1)
                        dve.wait_ge(ctx_out_summed, 1)
                        dve.tensor_copy(ctx_out[:, :], bank[2][:, 0:D]).then_inc(ctx_out_ready, 1)
                        dve.wait_ge(w_mix_summed, 1)
                        dve.tensor_copy(w_mix[:, :, :], bank[3][:, :].rearrange("p (k d) -> p k d", k=KD)).then_inc(w_mix_ready, 1)
                        dve.wait_ge(self_exp, 1)
                        dve.tensor_tensor(acc[:, 0:NB, 0:D].rearrange("p t (h c) -> p t h c", c=C),
                                          hs[:, :, 0:D].rearrange("p t (h c) -> p t h c", c=C),
                                          acc[:, 0:NB, D:ROW].unsqueeze(3).broadcast_to((P, NB, HEADS, C)), ALU.mult).then_inc(self_ready, 1)
                        with dve.Fori(0, NT // UNROLL) as i:
                            for k in range(UNROLL):
                                t = i * UNROLL + k
                                dve.wait_ge(mixed, t + 1 + UNROLL)
                                dve.tensor_tensor(flat(xs[:, bass.ds(t, 1), :]), flat(xs[:, bass.ds(t, 1), :]),
                                                  bank[4 + k % 4][:, 0:D], ALU.add).then_inc(mix_added, 1)
                        dve.wait_ge(mix_added, NT)

                    @block.scalar
                    def _(act):
                        for i in range(NT // UNROLL):
                            keys = kv[:, i * UNROLL:(i + 1) * UNROLL, 0:HID]
                            act.wait_ge(keys_shifted, i + 1)
                            act.activation(keys, keys, ACT.Exp).then_inc(keys_exp, 1)
                        act.wait_ge(self_logits, 1)
                        act.activation(acc[:, 0:NB, D:ROW], self_z[:, :, :], ACT.Exp).then_inc(self_exp, 1)
                        with act.Fori(0, NT // UNROLL) as i:
                            for k in range(UNROLL):
                                act.wait_ge(mixed, i * UNROLL + k + 1)
                                act.activation(mix_slot[:, k, :], flat(xnT[:, bass.ds(i * UNROLL + k, 1), :]),
                                               ACT.Copy).then_inc(slot_ready, 1)

                    @block.tensor
                    def _(pe):
                        pe.sem_inc(mixed, UNROLL)
                        pe.wait_ge(kmax_ready, 1)
                        pe.transpose(bank[0][:, 0:P], kmax[:, :], ident[:, :]).then_inc(kmax_turned, 1)
                        pe.wait_ge(amax_ready, 1)
                        pe.transpose(bank[1][0:HEADS, 0:P], amax_p[:, :], ident[:, :]).then_inc(amax_turned, 1)
                        pe.wait_ge(kdiag_ready, 1)
                        pe.matmul(bank[2][:, 0:P], ones[:, :], kdiag[:, :], start=True, stop=True).then_inc(kmax_spread, 1)
                        pe.wait_ge(amax_diag, 1)
                        pe.matmul(bank[3][:, 0:HEADS], ones[0:HEADS, :], amax_d[:, :], start=True, stop=True).then_inc(amax_spread, 1)
                        for c in range(KD):
                            tr = pe.transpose(bank[6][:, c * P:(c + 1) * P], w_q[:, c, :], ident[:, :])
                        tr.then_inc(w_q_turned, 1)
                        for t in range(NT):
                            if t % UNROLL == 0:
                                pe.wait_ge(keys_exp, t // UNROLL + 1)
                            n = P if t < NT - 1 else LAST
                            mm = pe.matmul(bank[0][:, 0:HID + 1], kv[0:n, t, 0:HID], kv[0:n, t, HID:2 * HID + 1],
                                           start=(t == 0), stop=(t == NT - 1))
                        mm.then_inc(ctx_summed, 1)
                        pe.wait_ge(spans_ready, 1)
                        pe.transpose(bank[4][0:NB, 0:EQ], first_q[:, :], ident[0:EQ, 0:EQ])
                        pe.transpose(bank[4][0:NB, P:P + EQ], last_q[:, :], ident[0:EQ, 0:EQ]).then_inc(spans_turned, 1)
                        pe.wait_ge(rows_ready, 1)
                        pe.matmul(bank[5][:, 0:3 * NB], ones[0:NB, :], span_rows[:, :], start=True, stop=True).then_inc(rows_spread, 1)
                        pe.wait_ge(ctx_ready, 1)
                        pe.transpose(bank[1][:, 0:P], ctx[:, :], ident[:, :]).then_inc(ctx_turned, 1)
                        pe.wait_ge(ctxT_ready, 1)
                        pe.wait_ge(bias_in, 48)
                        pe.matmul(bank[2][:, 0:D], ctxT[:, :], w_o[:, :], start=True, stop=True).then_inc(ctx_out_summed, 1)
                        pe.wait_ge(ctx_out_ready, 1)
                        pe.wait_ge(w_qT_ready, 1)
                        for c in range(KD):
                            mm = pe.matmul(bank[3][:, c * D:(c + 1) * D], w_qT[:, c * P:(c + 1) * P], ctx_out[:, :],
                                           start=True, stop=True)
                        mm.then_inc(w_mix_summed, 1)
                        pe.wait_ge(w_mix_ready, 1)
                        pe.wait_ge(visits_ready, 2)
                        with pe.Fori(0, NT // UNROLL) as i:
                            for k in range(UNROLL):
                                t = i * UNROLL + k
                                pe.wait_ge(slot_ready, t + 1)
                                pe.wait_ge(mix_added, i * UNROLL if k < 4 else t - 3)
                                for c in range(KD):
                                    pe.matmul(bank[4 + k % 4][:, 0:D], mix_slot[:, k, c * P:(c + 1) * P], w_mix[:, c, :],
                                              start=(c == 0), stop=False)
                                pe.matmul(bank[4 + k % 4][:, 0:D], ones[0:1, :], b_o[:, :], start=False, stop=True).then_inc(mixed, 1)

                    @block.sync
                    def _(sp):
                        sp.wait_ge(visits_ready, 2)
                        sp.dma_start(visit_tile.rearrange("(p c) -> p c", c=VCOL), vt_i[:, :]).then_inc(visits_stored, 16)
                        sp.dma_start(visit_block.rearrange("(p c) -> p c", c=VCOL), vb_i[:, :]).then_inc(visits_stored, 16)
                        sp.wait_ge(visits_stored, 32)

        w1_sb = sb(whole, "w1_sb", [P, NX * KD, FF])
        w2_in = sem("w2_in")
        slots_zeroed = sem("slots_zeroed")
        with ExitStack() as scope:
            table = sb(scope, "table", [1, 2, CH], I32)
            gathered = sb(scope, "gathered", [P, RING, G, ROW])
            index = sb(scope, "index", [P, RING, G], U32)
            local = sb(scope, "local", [P, RING, G])
            one_hot = sb(scope, "one_hot", [P, RING, G, P])
            one_hotT = sb(scope, "one_hotT", [P, 2, G, P])
            z = sb(scope, "z", [P, G, HEADS])
            turned_bank, ad_bank, sum_bank = bank[0:2], bank[2:4], bank[4:8]

            zeros = sb(scope, "zeros", [P, D])
            zeros_ready = sem("zeros_ready")
            table_in = sem("table_in")
            cols_ready = sem("cols_ready")
            gather_done = [sem(f"gather_done{r}") for r in range(RING)]
            hot_ready = sem("hot_ready")
            hot_turned = sem("hot_turned")
            hotT_ready = sem("hotT_ready")
            ad_ready = sem("ad_ready")
            logit_step = sem("logit_step")
            logits_ready = sem("logits_ready")
            exp_ready = sem("exp_ready")
            weighted = sem("weighted")
            summed = sem("summed")
            added = sem("added")
            waited = sem("waited")

            def steps(eng, c, step):
                for r in range(RING):
                    step(c * NGRP + r, r, r, RING)
                with eng.Fori(1, NGRP // RING - 1) as i:
                    for r in range(RING):
                        step(c * NGRP + i * RING + r, i * RING + r, r, RING)
                for r in range(RING):
                    step(c * NGRP + NGRP - RING + r, NGRP - RING + r, r, RING - 1 - r)

            with nc.Block() as block:
                @block.sync
                def _(sp):
                    chunks = sp.value_load(chunks_i[0:1, 0:1], min_val=1, max_val=MAXCHUNK)
                    with sp.Fori(0, chunks) as c:
                        first = sp.snap(c * CH)
                        sp.wait_ge(added, first)
                        sp.sem_inc(waited, 1)
                        sp.dma_start(table[0:1, 0, :], visit_tile[bass.ds(first, CH)].unsqueeze(0)).then_inc(table_in, 16)
                        sp.dma_start(table[0:1, 1, :], visit_block[bass.ds(first, CH)].unsqueeze(0)).then_inc(table_in, 16)
                    sp.dma_start(w1_sb[:, :, :], w1.rearrange("e (k p) f -> p (e k) f", p=P)).then_inc(w1_in, 16)
                    sp.wait_ge(zeros_ready, 1)
                    sp.dma_start(slot_x.rearrange("(u p) d -> p u d", p=P),
                                 zeros[:, :].unsqueeze(1).broadcast_to((P, UT, D))).then_inc(slots_zeroed, 16)
                    sp.wait_ge(slots_zeroed, 16)

                @block.gpsimd
                def _(pool):
                    pool.memset(zeros[:, :], 0.0).then_inc(zeros_ready, 1)
                    chunks = pool.value_load(chunks_i[0:1, 0:1], min_val=1, max_val=MAXCHUNK)
                    with pool.Fori(0, chunks) as c:
                        with pool.Fori(0, NGRP // RING) as i:
                            for r in range(RING):
                                pool.wait_ge(cols_ready, c * NGRP + i * RING + r + 1)
                                pool.sem_inc(waited, 1)
                                for j in range(G):
                                    pool.indirect_dma_start(gathered[:, r, j, :], None, h_table,
                                                            bass.IndirectOffsetOnAxis(ap=index[:, r, j:j + 1], axis=0)
                                                            ).then_inc(gather_done[r], 16)

                @block.scalar
                def _(act):
                    chunks = act.value_load(chunks_i[0:1, 0:1], min_val=1, max_val=MAXCHUNK)
                    tile_regs = [act.alloc_register(f"act_tile{j}") for j in range(G)]
                    block_regs = [act.alloc_register(f"act_block{j}") for j in range(G)]

                    def columns(s, r, free):
                        act.load(tile_regs, table[0:1, 0, bass.ds(s * G, G)])
                        act.load(block_regs, table[0:1, 1, bass.ds(s * G, G)])
                        act.wait_ge(summed, free)
                        for j in range(G):
                            t = act.snap(tile_regs[j], min_val=0, max_val=ET - 1)
                            b = act.snap(block_regs[j], min_val=0, max_val=NB)
                            act.activation(index[:, r, j:j + 1], src_col[:, bass.ds(t, 1)], ACT.Copy)
                            op = act.activation(local[:, r, j:j + 1], dst_col[:, bass.ds(t, 1)], ACT.Identity,
                                                bias=minus_base[:, bass.ds(b, 1)])
                        op.then_inc(cols_ready, 1)

                    def turned_out(n, half):
                        act.wait_ge(hot_turned, n)
                        act.activation(one_hotT[:, half, :, :].rearrange("p a b -> p (a b)"), turned_bank[half][:, :],
                                       ACT.Copy).then_inc(hotT_ready, 1)

                    def exps(n, r):
                        act.wait_ge(logits_ready, n)
                        act.activation(gathered[:, r, :, D:ROW], z[:, :, :], ACT.Exp).then_inc(exp_ready, 1)

                    def step(n, s, r, ahead):
                        if ahead >= 1:
                            act.wait_ge(ad_ready, n)
                            turned_out(n + 2, (r + 1) % 2)
                        if ahead >= 3:
                            columns(s + 3, (r + 3) % RING, n)
                        if ahead >= 1:
                            exps(n + 2, (r + 1) % RING)

                    with act.Fori(0, chunks) as c:
                        act.wait_ge(table_in, c * 32 + 32)
                        act.sem_inc(waited, 1)
                        for r in range(3):
                            columns(r, r, c * NGRP)
                        turned_out(c * NGRP + 1, 0)
                        exps(c * NGRP + 1, 0)
                        steps(act, c, step)

                @block.tensor
                def _(pe):
                    chunks = pe.value_load(chunks_i[0:1, 0:1], min_val=1, max_val=MAXCHUNK)
                    block_regs = [pe.alloc_register(f"pe_block{j}") for j in range(G)]

                    def turn(n, r, half):
                        pe.wait_ge(hot_ready, n)
                        for j in range(G):
                            tr = pe.transpose(turned_bank[half][:, j * P:(j + 1) * P], one_hot[:, r, j, :], ident[:, :])
                        tr.then_inc(hot_turned, 1)

                    def spread(n, half):
                        pe.wait_ge(hotT_ready, n)
                        for j in range(G):
                            b = pe.snap(block_regs[j], min_val=0, max_val=NB)
                            mm = pe.matmul(ad_bank[half][:, j * 2 * HEADS:(j + 1) * 2 * HEADS], one_hotT[:, half, j, :],
                                           flat(adc[:, bass.ds(b, 1), :]), start=True, stop=True)
                        mm.then_inc(ad_ready, 1)

                    def step(n, s, r, ahead):
                        if ahead >= 1:
                            pe.load(block_regs, table[0:1, 1, bass.ds((s + 1) * G, G)])
                            pe.wait_ge(logits_ready, n)
                            spread(n + 2, (r + 1) % 2)
                        pe.wait_ge(weighted, n + 1)
                        for j in range(G):
                            pe.wait_ge(added, (n - 1) * G + j + 1 if not isinstance(s, int) or s > 0 else n * G)
                            mm = pe.matmul(sum_bank[j][:, 0:ROW], one_hot[:, r, j, :], gathered[:, r, j, :],
                                           start=True, stop=True)
                        mm.then_inc(summed, 1)
                        if ahead >= 2:
                            turn(n + 3, (r + 2) % RING, r % 2)

                    with pe.Fori(0, chunks) as c:
                        pe.wait_ge(table_in, c * 32 + 32)
                        pe.sem_inc(waited, 1)
                        pe.load(block_regs, table[0:1, 1, 0:G])
                        turn(c * NGRP + 1, 0, 0)
                        spread(c * NGRP + 1, 0)
                        turn(c * NGRP + 2, 1, 1)
                        steps(pe, c, step)

                @block.vector
                def _(dve):
                    chunks = dve.value_load(chunks_i[0:1, 0:1], min_val=1, max_val=MAXCHUNK)
                    block_regs = [dve.alloc_register(f"dve_block{j}") for j in range(G)]

                    def hot(r, j):
                        return dve.tensor_scalar(one_hot[:, r, j, :], iota_row[:, :], local[:, r, j:j + 1], None, ALU.is_equal)

                    def add_sum(n, j):
                        b = dve.snap(block_regs[j], min_val=0, max_val=NB)
                        dve.wait_ge(added, n * G + j)
                        dve.tensor_tensor(flat(acc[:, bass.ds(b, 1), :]), flat(acc[:, bass.ds(b, 1), :]),
                                          sum_bank[j][:, 0:ROW], ALU.add).then_inc(added, 1)

                    def logits(n, r, half, part):
                        ad = ad_bank[half][:, 0:G * 2 * HEADS].rearrange("p (j a) -> p j a", j=G)
                        if part == 0:
                            dve.wait_ge(ad_ready, n + 1)
                            dve.tensor_tensor(z[:, :, :], gathered[:, r, :, D:ROW], ad[:, :, 0:HEADS], ALU.add).then_inc(logit_step, 1)
                        elif part == 1:
                            dve.wait_ge(logit_step, n * 2 + 1)
                            dve.scalar_tensor_tensor(out=z[:, :, :], in0=z[:, :, :], scalar=SLOPE, in1=z[:, :, :],
                                                     op0=ALU.mult, op1=ALU.max).then_inc(logit_step, 1)
                        else:
                            dve.wait_ge(logit_step, n * 2 + 2)
                            dve.tensor_tensor(z[:, :, :], z[:, :, :], ad[:, :, HEADS:2 * HEADS], ALU.subtract).then_inc(logits_ready, 1)

                    def weigh(n, r):
                        dve.wait_ge(exp_ready, n + 1)
                        message = gathered[:, r, :, 0:D].rearrange("p j (h c) -> p j h c", c=C)
                        dve.tensor_tensor(message, message,
                                          gathered[:, r, :, D:ROW].unsqueeze(3).broadcast_to((P, G, HEADS, C)),
                                          ALU.mult).then_inc(weighted, 1)

                    with dve.Fori(0, chunks) as c:
                        rounds = c * (NGRP // RING)

                        def step(n, s, r, ahead):
                            before = not isinstance(s, int) or s > 0
                            if before:
                                dve.load(block_regs, table[0:1, 1, bass.ds(s * G - G, G)])
                            weigh(n, r)
                            if ahead >= 2:
                                dve.wait_ge(cols_ready, n + 3)
                            if before:
                                dve.wait_ge(summed, n)
                            for j in range(G):
                                if before:
                                    add_sum(n - 1, j)
                                if j == 3 and ahead >= 1:
                                    logits(n + 1, (r + 1) % RING, (r + 1) % 2, 2)
                                if ahead >= 2:
                                    op = hot((r + 2) % RING, j)
                                if j == 1 and ahead >= 1:
                                    dve.wait_ge(gather_done[(r + 1) % RING], ring_count(n, s, r))
                                    logits(n + 1, (r + 1) % RING, (r + 1) % 2, 0)
                                if j == 2 and ahead >= 1:
                                    logits(n + 1, (r + 1) % RING, (r + 1) % 2, 1)
                            if ahead >= 2:
                                op.then_inc(hot_ready, 1)

                        def ring_count(n, s, r):
                            uses = (n + 1 - (r + 1) % RING)
                            return uses * (16 * G // RING) + 16 * G

                        dve.wait_ge(table_in, c * 32 + 32)
                        for r in range(2):
                            dve.wait_ge(cols_ready, c * NGRP + r + 1)
                            for j in range(G):
                                op = hot(r, j)
                            op.then_inc(hot_ready, 1)
                        dve.wait_ge(gather_done[0], rounds * 16 * G + 16 * G)
                        for part in range(3):
                            logits(c * NGRP, 0, 0, part)
                        steps(dve, c, step)
                        dve.load(block_regs, table[0:1, 1, CH - G:CH])
                        dve.wait_ge(summed, c * NGRP + NGRP)
                        for j in range(G):
                            add_sum(c * NGRP + NGRP - 1, j)
        w2_sb = sb(whole, "w2_sb", [P, NX * KF, D])
        b1_sb = sb(whole, "b1_sb", [NX, FF])
        b2_sb = sb(whole, "b2_sb", [NX, D])
        slot_of = sb(whole, "slot_of", [P, NCHOICE], U32)
        share = sb(whole, "share", [P, 2, NT])
        tile_expert = sb(whole, "tile_expert", [P, UT], I32)
        chosen = sb(whole, "chosen", [NX, UT])
        with ExitStack() as scope:
            w_g = sb(scope, "w_g", [P, KD, NX])
            b_g = sb(scope, "b_g", [1, NX])
            rden = sb(scope, "rden", [P, NT, HEADS])
            xn = sb(scope, "xn2", [P, UNROLL, D])
            xnT_slot = sb(scope, "xn2T_slot", [P, 2, D])
            gate = sb(scope, "gate", [P, NT, NX])
            top = sb(scope, "top", [P, NT, NX])
            top_i = sb(scope, "top_i", [P, NT, NX], U32)
            top_f = sb(scope, "top_f", [P, 2, NT])
            expert_id = sb(scope, "expert_id", [P, NX])
            row_id = sb(scope, "row_id", [P, 1])
            tile_no = sb(scope, "tile_no", [P, UT])
            before_row = sb(scope, "before_row", [P, P])
            choice = sb(scope, "choice", [P, NCHOICE, NX])
            count = src_col[:, 0:NCHOICE * NX].rearrange("p (n e) -> p n e", e=NX)
            upto_count = dst_col[:, 0:NCHOICE * NX].rearrange("p (n e) -> p n e", e=NX)
            room = sb(scope, "room", [P, NX])
            room_i = sb(scope, "room_i", [P, NX], I32)
            tiles_upto = sb(scope, "tiles_upto", [P, NX])
            start = sb(scope, "start", [P, NX])
            slot_f = sb(scope, "slot_f", [P, NCHOICE])
            past_e = xnT_slot[:, :, :].rearrange("p a b -> p (a b)")[:, 0:UT * NX].rearrange("p (u e) -> p u e", e=NX)
            expert_f = sb(scope, "expert_f", [P, UT])
            ratio = sb(scope, "ratio", [P, NT])

            gate_in = sem("gate_in")
            ffn_bias_in = sem("ffn_bias_in")
            den_ready = sem("den_ready")
            gat_step = sem("gat_step")
            gat_ready = sem("gat_ready")
            x_step = sem("x_step")
            moments2_ready = sem("moments2_ready")
            std2_ready = sem("std2_ready")
            xn2_ready = sem("xn2_ready")
            xn2_kept = sem("xn2_kept")
            turned2 = sem("turned2")
            xn2T_ready = sem("xn2T_ready")
            gated = sem("gated")
            pool3 = sem("pool3")
            ratio_ready = sem("ratio_ready")
            exp2_ready = sem("exp2_ready")
            choice_ready = sem("choice_ready")
            counted = sem("counted")
            slots_ready = sem("slots_ready")
            scattered = sem("scattered")
            v3 = Chain(sem("v3"))
            g3 = Chain(sem("g3"))

            with nc.Block() as block:
                @block.sync
                def _(sp):
                    sp.dma_start(w_g[:, :, :], w_gate.rearrange("(k p) e -> p k e", p=P)).then_inc(gate_in, 16)
                    sp.dma_start(b_g[:, :], b_gate.rearrange("(a e) -> a e", a=1)).then_inc(gate_in, 16)
                    sp.dma_start(b1_sb[:, :], b1).then_inc(ffn_bias_in, 16)
                    sp.dma_start(b2_sb[:, :], b2).then_inc(ffn_bias_in, 16)
                    sp.dma_start(w2_sb[:, :, :], w2.rearrange("e (k p) d -> p (e k) d", p=P)).then_inc(w2_in, 16)

                @block.gpsimd
                def _(pool):
                    pool.iota(expert_id[:, :], [[1, NX]], base=0, channel_multiplier=0,
                              allow_small_or_imprecise_dtypes=True).then_inc(pool3, 1)
                    pool.iota(row_id[:, :], [[0, 1]], base=0, channel_multiplier=1,
                              allow_small_or_imprecise_dtypes=True).then_inc(pool3, 1)
                    pool.iota(tile_no[:, :], [[1, UT]], base=0, channel_multiplier=0,
                              allow_small_or_imprecise_dtypes=True).then_inc(pool3, 1)
                    g3.done(pool.memset(before_row[:, :], 1.0))
                    pool.wait_ge(g3.sem, g3.n)
                    pool.affine_select(out=before_row[:, :], in_=before_row[:, :], compare_op=ALU.is_ge, fill=0.0,
                                       base=-1, pattern=[[1, P]], channel_multiplier=-1).then_inc(pool3, 1)
                    pool.wait_ge(den_ready, 1)
                    with pool.Fori(0, NT) as t:
                        sums = acc[:, bass.ds(t, 1), 0:D].rearrange("p a (h c) -> p (a h) c", c=C)
                        pool.tensor_tensor(sums, sums, flat(rden[:, bass.ds(t, 1), :]).unsqueeze(2).broadcast_to((P, HEADS, C)),
                                           ALU.mult).then_inc(gat_step, 1)
                        pool.wait_ge(gat_step, t + 1)
                        pool.sem_inc(waited, 1)
                        pool.tensor_tensor(flat(acc[:, bass.ds(t, 1), 0:D]), flat(acc[:, bass.ds(t, 1), 0:D]),
                                           gat_bias_sb[:, :], ALU.add).then_inc(gat_ready, 1)
                    with pool.Fori(0, NT // UNROLL) as i:
                        for k in range(UNROLL):
                            pool.wait_ge(xn2_ready, i * UNROLL + k + 1)
                            pool.tensor_copy(flat(acc[:, bass.ds(i * UNROLL + k, 1), 0:D]), xn[:, k, :]).then_inc(xn2_kept, 1)
                    pool.wait_ge(xn2_kept, NT)
                    pool.wait_ge(slots_ready, 1)
                    for n in range(NCHOICE):
                        pool.indirect_dma_start(slot_x, bass.IndirectOffsetOnAxis(ap=slot_of[:, n:n + 1], axis=0),
                                                acc[:, n % NT, 0:D], None).then_inc(scattered, 16)
                    pool.wait_ge(scattered, 16 * NCHOICE)

                @block.scalar
                def _(act):
                    act.wait_ge(moments2_ready, NT)
                    act.activation(rstd[:, :], moments[:, :, 1], ACT.Sqrt, bias=eps_col[:, :]).then_inc(std2_ready, 1)
                    with act.Fori(0, NT // UNROLL) as i:
                        for k in range(UNROLL):
                            t = i * UNROLL + k
                            act.wait_ge(turned2, t + 1)
                            act.wait_ge(gated, t if k == 0 else t - 1)
                            act.activation(xnT_slot[:, k % 2, :], bank[k % 2][:, 0:D], ACT.Copy).then_inc(xn2T_ready, 1)
                    act.wait_ge(ratio_ready, 1)
                    act.activation(ratio[:, :], ratio[:, :], ACT.Exp).then_inc(exp2_ready, 1)

                @block.tensor
                def _(pe):
                    pe.wait_ge(gate_in, 32)
                    with pe.Fori(0, NT // UNROLL) as i:
                        def turn(k):
                            pe.wait_ge(xn2_ready, i * UNROLL + k + 1)
                            pe.wait_ge(xn2T_ready, i * UNROLL + (k if k == 0 else k - 1))
                            for c in range(KD):
                                tr = pe.transpose(bank[k % 2][:, c * P:(c + 1) * P], xn[:, k, c * P:(c + 1) * P], ident[:, :])
                            tr.then_inc(turned2, 1)

                        turn(0)
                        for k in range(UNROLL):
                            t = i * UNROLL + k
                            if k + 1 < UNROLL:
                                turn(k + 1)
                            pe.wait_ge(xn2T_ready, t + 1)
                            logits = bank[7][:, bass.ds(t * NX, NX)]
                            for c in range(KD):
                                pe.matmul(logits, xnT_slot[:, k % 2, c * P:(c + 1) * P], w_g[:, c, :], start=(c == 0), stop=False)
                            pe.matmul(logits, ones[0:1, :], b_g[:, :], start=False, stop=True).then_inc(gated, 1)
                    pe.wait_ge(choice_ready, 1)
                    flat_choice = choice[:, :, :].rearrange("p n e -> p (n e)")
                    pe.matmul(bank[0][:, 0:NCHOICE * NX], before_row[:, :], flat_choice, start=True, stop=True)
                    pe.matmul(bank[1][:, 0:NCHOICE * NX], ones[:, :], flat_choice, start=True, stop=True).then_inc(counted, 1)

                @block.vector
                def _(dve):
                    def after(instruction):
                        v3.done(instruction)
                        dve.wait_ge(v3.sem, v3.n)

                    dve.reciprocal(rden[:, :, :], acc[:, 0:NB, D:ROW]).then_inc(den_ready, 1)
                    with dve.Fori(0, NT) as t:
                        dve.wait_ge(gat_ready, t + 1)
                        row = flat(xs[:, bass.ds(t, 1), :])
                        dve.scalar_tensor_tensor(out=row, in0=flat(acc[:, bass.ds(t, 1), 0:D]), scalar=0.0, in1=row,
                                                 op0=ALU.max, op1=ALU.add).then_inc(x_step, 1)
                        dve.wait_ge(x_step, 2 * t + 1)
                        dve.bn_stats(flat(stats[:, bass.ds(t, 1), :]), row).then_inc(x_step, 1)
                    dve.wait_ge(x_step, 2 * NT)
                    for t in range(NT):
                        dve.bn_aggr(moments[:, t, :], stats[:, t, :]).then_inc(moments2_ready, 1)
                    dve.wait_ge(std2_ready, 1)
                    after(dve.reciprocal(rstd[:, :], rstd[:, :]))
                    with dve.Fori(0, NT // UNROLL) as i:
                        for k in range(UNROLL):
                            t = i * UNROLL + k
                            dve.wait_ge(turned2, i * UNROLL)
                            dve.wait_ge(xn2_kept, i * UNROLL)
                            dve.tensor_scalar(xn[:, k, :], flat(xs[:, bass.ds(t, 1), :]), flat(moments[:, bass.ds(t, 1), 0:1]),
                                              rstd[:, bass.ds(t, 1)], ALU.subtract, ALU.mult).then_inc(xn2_ready, 1)
                    dve.wait_ge(gated, NT)
                    after(dve.tensor_copy(gate[:, :, :], bank[7][:, 0:NT * NX].rearrange("p (t e) -> p t e", e=NX)))
                    for t in range(NT):
                        dve.max(top[:, t, :], gate[:, t, :]).then_inc(v3.sem, 1)
                    v3.n += NT
                    dve.wait_ge(v3.sem, v3.n)
                    for t in range(NT):
                        dve.max_index(top_i[:, t, :], top[:, t, :], gate[:, t, :]).then_inc(v3.sem, 1)
                    v3.n += NT
                    dve.tensor_tensor(ratio[:, :], top[:, :, 1], top[:, :, 0], ALU.subtract).then_inc(ratio_ready, 1)
                    dve.wait_ge(v3.sem, v3.n)
                    after(dve.tensor_copy(top_f[:, :, :], top_i[:, :, 0:2].rearrange("p t k -> p k t")))
                    dve.wait_ge(pool3, 4)
                    for k in range(2):
                        op = dve.tensor_tensor(choice[:, k * NT:(k + 1) * NT, :], top_f[:, k, :].unsqueeze(2).broadcast_to((P, NT, NX)),
                                               expert_id[:, :].unsqueeze(1).broadcast_to((P, NT, NX)), ALU.is_equal)
                    op.then_inc(choice_ready, 1)
                    dve.wait_ge(exp2_ready, 1)
                    after(dve.tensor_scalar(share[:, 1, :], ratio[:, :], 1.0, None, ALU.add))
                    after(dve.reciprocal(share[:, 0, :], share[:, 1, :]))
                    after(dve.tensor_tensor(share[:, 1, :], ratio[:, :], share[:, 0, :], ALU.mult))
                    dve.wait_ge(counted, 1)
                    after(dve.tensor_copy(count[:, :, :], bank[1][:, 0:NCHOICE * NX].rearrange("p (n e) -> p n e", e=NX)))
                    for e in range(NX):
                        op = dve.tensor_tensor_scan(upto_count[:, :, e], ones[:, 0:NCHOICE], count[:, :, e], 0.0, ALU.mult, ALU.add)
                    after(op)
                    after(dve.tensor_scalar(room_i[:, :], upto_count[:, NCHOICE - 1, :], float(P - 1), None, ALU.add))
                    after(dve.tensor_scalar(room_i[:, :], room_i[:, :], P.bit_length() - 1, None, ALU.arith_shift_right))
                    after(dve.tensor_copy(room[:, :], room_i[:, :]))
                    after(dve.tensor_tensor_scan(tiles_upto[:, :], ones[:, 0:NX], room[:, :], 0.0, ALU.mult, ALU.add))
                    after(dve.tensor_tensor(start[:, :], tiles_upto[:, :], room[:, :], ALU.subtract))
                    after(dve.tensor_scalar(start[:, :], start[:, :], float(P), None, ALU.mult))
                    after(dve.tensor_tensor(upto_count[:, :, :], upto_count[:, :, :], count[:, :, :], ALU.subtract))
                    after(dve.tensor_tensor(upto_count[:, :, :], upto_count[:, :, :],
                                            start[:, :].unsqueeze(1).broadcast_to((P, NCHOICE, NX)), ALU.add))
                    after(dve.tensor_tensor(upto_count[:, :, :], upto_count[:, :, :],
                                            bank[0][:, 0:NCHOICE * NX].rearrange("p (n e) -> p n e", e=NX), ALU.add))
                    after(dve.tensor_tensor(upto_count[:, :, :], upto_count[:, :, :], choice[:, :, :], ALU.mult))
                    after(dve.tensor_reduce(slot_f[:, :], upto_count[:, :, :], AX.X, ALU.add))
                    dve.tensor_copy(slot_of[:, :], slot_f[:, :]).then_inc(slots_ready, 1)
                    grid = (P, UT, NX)
                    after(dve.tensor_tensor(past_e[:, :, :], tile_no[:, :].unsqueeze(2).broadcast_to(grid),
                                            tiles_upto[:, :].unsqueeze(1).broadcast_to(grid), ALU.is_ge))
                    after(dve.tensor_reduce(expert_f[:, :], past_e[:, :, :], AX.X, ALU.add))
                    after(dve.tensor_scalar(expert_f[:, :], expert_f[:, :], float(NX - 1), None, ALU.min))
                    after(dve.tensor_copy(tile_expert[:, :], expert_f[:, :]))
                    after(dve.tensor_scalar(chosen[:, :], expert_f[0:NX, :], row_id[0:NX, :], None, ALU.is_equal))

        with ExitStack() as scope:
            xg = sb(scope, "xg", [P, 2, D])
            xgT = sb(scope, "xgT", [P, 2, D])
            hidden = sb(scope, "hidden", [P, FF])
            hiddenT = sb(scope, "hiddenT", [P, FF])
            y = sb(scope, "y", [P, 2, D])
            picked = acc[0:NX, 0:2, 0:P]

            xg_in = [sem(f"xg_in{k}") for k in range(2)]
            xg_turned = sem("xg_turned")
            xgT_ready = sem("xgT_ready")
            picked_ready = sem("picked_ready")
            hidden_summed = sem("hidden_summed")
            hidden_ready = sem("hidden_ready")
            hidden_turned = sem("hidden_turned")
            hiddenT_ready = sem("hiddenT_ready")
            y_summed = sem("y_summed")
            y_ready = sem("y_ready")
            y_out = [sem(f"y_out{k}") for k in range(2)]
            slot_rows = slot_x.rearrange("(u p) d -> u p d", p=P)
            y_rows = slot_y.rearrange("(u p) d -> u p d", p=P)

            def tiles(eng, step):
                rounds = UT // 2
                for u in range(2):
                    step(u, u, 9)
                with eng.Fori(1, rounds - 1) as i:
                    for k in range(2):
                        step(i * 2 + k, k, 9)
                for u in range(2 * rounds - 2, UT):
                    step(u, u % 2, UT - 1 - u)

            with nc.Block() as block:
                @block.sync
                def _(sp):
                    def load(u, k):
                        sp.dma_start(xg[:, k, :], slot_rows[bass.ds(u, 1), :, :].rearrange("a p d -> p (a d)")).then_inc(xg_in[k], 16)

                    def step(u, k, ahead):
                        if ahead >= 2:
                            sp.wait_ge(xg_turned, u + 1)
                            load(u + 2, k)
                        sp.wait_ge(y_ready, u + 1)
                        sp.dma_start(y_rows[bass.ds(u, 1), :, :].rearrange("a p d -> p (a d)"), y[:, k, :]).then_inc(y_out[k], 16)

                    load(0, 0)
                    load(1, 1)
                    tiles(sp, step)
                    for k in range(2):
                        sp.wait_ge(y_out[k], 16 * ((UT + 1 - k) // 2))

                @block.scalar
                def _(act):
                    def turned_in(u, k):
                        act.wait_ge(xg_turned, u + 1)
                        act.activation(xgT[:, k, :], bank[0][:, 0:D], ACT.Copy).then_inc(xgT_ready, 1)

                    def gelu(u, k):
                        for half in range(2):
                            act.wait_ge(hidden_summed, 2 * u + half + 1)
                            act.activation(hidden[:, half * 512:(half + 1) * 512], bank[1 + 2 * k + half][:, :],
                                           ACT.Gelu).then_inc(hidden_ready, 1)

                    def step(u, k, ahead):
                        if ahead >= 1:
                            gelu(u + 1, 1 - k)
                        if ahead >= 2:
                            turned_in(u + 2, k)

                    turned_in(0, 0)
                    gelu(0, 0)
                    turned_in(1, 1)
                    tiles(act, step)

                @block.tensor
                def _(pe):
                    expert_reg = pe.alloc_register("pe_expert")
                    pe.wait_ge(w1_in, 16)
                    pe.wait_ge(w2_in, 16)
                    pe.wait_ge(ffn_bias_in, 32)

                    def turn_in(u, k):
                        pe.wait_ge(xg_in[k], tile_count(u, k) * 16)
                        for c in range(KD):
                            tr = pe.transpose(bank[0][:, c * P:(c + 1) * P], xg[:, k, c * P:(c + 1) * P], ident[:, :])
                        tr.then_inc(xg_turned, 1)

                    def tile_count(u, k):
                        return u // 2 + 1 if isinstance(u, int) else (u - k) // 2 + 1

                    def widen(u, k):
                        e = pe.value_load(tile_expert[0:1, bass.ds(u, 1)], min_val=0, max_val=NX - 1)
                        pe.wait_ge(xgT_ready, u + 1)
                        pe.wait_ge(picked_ready, u + 1)
                        for half in range(2):
                            into = bank[1 + 2 * k + half][:, :]
                            cols = slice(half * 512, (half + 1) * 512)
                            pe.matmul(into, picked[:, k, :], b1_sb[:, cols], start=True, stop=False)
                            for c in range(KD):
                                mm = pe.matmul(into, xgT[:, k, c * P:(c + 1) * P], flat(w1_sb[:, bass.ds(e * KD + c, 1), cols]),
                                               start=False, stop=(c == KD - 1))
                            mm.then_inc(hidden_summed, 1)

                    def step(u, k, ahead):
                        for half in range(2):
                            pe.wait_ge(hidden_ready, 2 * u + half + 1)
                            for f in range(4):
                                tr = pe.transpose(bank[5 + half][:, f * P:(f + 1) * P],
                                                  hidden[:, (half * 4 + f) * P:(half * 4 + f + 1) * P], ident[:, :])
                            tr.then_inc(hidden_turned, 1)
                        if ahead >= 1:
                            widen(u + 1, 1 - k)
                        if ahead >= 2:
                            turn_in(u + 2, k)
                        e = pe.value_load(tile_expert[0:1, bass.ds(u, 1)], min_val=0, max_val=NX - 1)
                        pe.wait_ge(y_ready, u)
                        pe.matmul(bank[7][:, 0:D], picked[:, k, :], b2_sb[:, :], start=True, stop=False)
                        for f in range(KF):
                            if f % 4 == 0:
                                pe.wait_ge(hiddenT_ready, 2 * u + f // 4 + 1)
                            mm = pe.matmul(bank[7][:, 0:D], hiddenT[:, f * P:(f + 1) * P], flat(w2_sb[:, bass.ds(e * KF + f, 1), :]),
                                           start=False, stop=(f == KF - 1))
                        mm.then_inc(y_summed, 1)

                    turn_in(0, 0)
                    widen(0, 0)
                    turn_in(1, 1)
                    tiles(pe, step)

                @block.vector
                def _(dve):
                    def pick(u, k, free):
                        dve.wait_ge(y_summed, free)
                        dve.tensor_copy(picked[:, k, :], chosen[:, bass.ds(u, 1)].broadcast_to((NX, P))).then_inc(picked_ready, 1)

                    def step(u, k, ahead):
                        for half in range(2):
                            dve.wait_ge(hidden_turned, 2 * u + half + 1)
                            dve.tensor_copy(hiddenT[:, half * 512:(half + 1) * 512], bank[5 + half][:, :]).then_inc(hiddenT_ready, 1)
                        dve.wait_ge(y_summed, u + 1)
                        if not isinstance(u, int) or u >= 2:
                            dve.wait_ge(y_out[k], ((u - k) // 2) * 16)
                        dve.tensor_copy(y[:, k, :], bank[7][:, 0:D]).then_inc(y_ready, 1)
                        if ahead >= 2:
                            pick(u + 2, k, u + 1)

                    pick(0, 0, 0)
                    pick(1, 1, 0)
                    tiles(dve, step)

        with ExitStack() as scope:
            DEPTH = 8
            yg = sb(scope, "yg", [P, DEPTH, D])
            yg_in = [sem(f"yg_in{k}") for k in range(DEPTH)]
            taken = sem("taken")
            out_stored = sem("out_stored")

            with nc.Block() as block:
                @block.gpsimd
                def _(pool):
                    for n in range(NCHOICE):
                        t, k = n // 2, n % 2
                        if n >= DEPTH:
                            pool.wait_ge(taken, n - DEPTH + 1)
                        pool.indirect_dma_start(yg[:, n % DEPTH, :], None, slot_y,
                                                bass.IndirectOffsetOnAxis(ap=slot_of[:, k * NT + t:k * NT + t + 1], axis=0)
                                                ).then_inc(yg_in[n % DEPTH], 16)

                @block.vector
                def _(dve):
                    for n in range(NCHOICE):
                        t, k = n // 2, n % 2
                        dve.wait_ge(yg_in[n % DEPTH], 16 * (n // DEPTH + 1))
                        if k:
                            dve.wait_ge(taken, n)
                        dve.scalar_tensor_tensor(out=xs[:, t, :], in0=yg[:, n % DEPTH, :], scalar=share[:, k, t:t + 1],
                                                 in1=xs[:, t, :], op0=ALU.mult, op1=ALU.add).then_inc(taken, 1)

                @block.sync
                def _(sp):
                    for t in range(NT):
                        rows_t = P if t < NT - 1 else LAST
                        sp.wait_ge(taken, 2 * t + 2)
                        sp.dma_start(out[t * P:t * P + rows_t, :], xs[0:rows_t, t, :]).then_inc(out_stored, 16)
                    sp.wait_ge(out_stored, 16 * NT)


_INS = ['x', 'src', 'dst', 'L0_gnn_W', 'L0_gnn_att_src', 'L0_gnn_att_dst', 'L0_gnn_bias', 'L0_mix_W_qkv', 'L0_mix_W_out',
        'L0_mix_b_out', 'L0_ffn_Wg', 'L0_ffn_bg', 'L0_ffn_W1', 'L0_ffn_b1', 'L0_ffn_W2', 'L0_ffn_b2']


def kernel(**inputs):
    import numpy as np
    import concourse.bacc as bacc
    from concourse.bass_utils import run_bass_kernel_spmd

    nc = bacc.Bacc("TRN2", target_bir_lowering=False, num_devices=1)
    arrays, args = {}, []
    for name in _INS:
        a = np.ascontiguousarray(inputs[name])
        arrays[f"in_{name}"] = a
        args.append(nc.dram_tensor(f"in_{name}", a.shape, mybir.dt.from_np(a.dtype), kind="ExternalInput").ap())
    out = nc.dram_tensor("out", (N, D), F32, kind="ExternalOutput").ap()
    graph_layer(nc, *args, out)
    result = run_bass_kernel_spmd(nc, [arrays], core_ids=[0])
    return result.results[0]["out"]
```

```python
from contextlib import ExitStack

import concourse.bass as bass
from concourse import mybir

F32 = mybir.dt.float32
BF16 = mybir.dt.bfloat16
I32 = mybir.dt.int32
U32 = mybir.dt.uint32
ALU = mybir.AluOpType
ACT = mybir.ActivationFunctionType
AX = mybir.AxisListType

P = 128
N = 3125
D = 256
NT = -(-N // P)
NPAD = NT * P
LAST = N - (NT - 1) * P
KD = D // P
HEADS = 4
C = D // HEADS
ROW = D + HEADS
HID = 128
DH = HID // HEADS
E = 53125
ET = -(-E // P)
EQ = ET // 4
NB = NT
BIG = 16384.0
CH = 448
G = 4
RING = 4
NGRP = CH // G
MAXCHUNK = -(-(ET * NB) // CH)
VCOL = 84
NX = 8
FF = 1024
KF = FF // P
NCHOICE = 2 * NT
UT = (2 * N + NX * (P - 1)) // P
SPARE = P
UNROLL = 5
CONSTS = 6
EPS = 1e-5
SLOPE = 0.2
QSCALE = float(DH) ** -0.5
NEG = -3.0e38

assert UT % 2 == 0 and ET % 4 == 0 and NT % UNROLL == 0 and P * VCOL >= MAXCHUNK * CH and NGRP % RING == 0 and EQ <= P


def flat(ap):
    return ap.rearrange("p a b -> p (a b)")


def ahead(n):
    return n + UNROLL


def from_one(n):
    return n + 1


class Chain:

    def __init__(self, sem):
        self.sem, self.n = sem, 0

    def done(self, instruction):
        self.n += 1
        instruction.then_inc(self.sem, 1)


def graph_layer(nc, x, src, dst, w_gat, att_src, att_dst, gat_bias, w_qkv, w_out, b_out,
                w_gate, b_gate, w1, b1, w2, b2, out):
    h_table = nc.dram_tensor("h_table", (NPAD, ROW), F32, kind="Internal").ap()
    visit_tile = nc.dram_tensor("visit_tile", (P * VCOL,), I32, kind="Internal").ap()
    visit_block = nc.dram_tensor("visit_block", (P * VCOL,), I32, kind="Internal").ap()
    xn_table = nc.dram_tensor("xn_table", (NPAD, D), F32, kind="Internal").ap()

    with ExitStack() as whole:
        def sem(name):
            return whole.enter_context(nc.semaphore(name))

        def sb(scope, name, shape, dtype=F32):
            return scope.enter_context(nc.sbuf_tensor(name, shape, dtype))

        bank = [whole.enter_context(nc.psum_tensor(f"bank{k}", [P, 512], F32)) for k in range(8)]

        ident = sb(whole, "ident", [P, P])
        ones = sb(whole, "ones", [P, P])
        xs = sb(whole, "xs", [P, NT, D])
        acc = sb(whole, "acc", [P, NB + 1, ROW])
        stats = sb(whole, "stats", [P, NT, 6])
        moments = sb(whole, "moments", [P, NT, 2])
        rstd = sb(whole, "rstd", [P, NT])
        gat_bias_sb = sb(whole, "gat_bias_sb", [P, D])
        iota_row = sb(whole, "iota_row", [P, P])
        adc = sb(whole, "adc", [P, NB + 1, 2 * HEADS])
        src_col = sb(whole, "src_col", [P, ET])
        dst_col = sb(whole, "dst_col", [P, ET])
        minus_base = sb(whole, "minus_base", [P, NB + 1])
        chunks_i = sb(whole, "chunks_i", [1, 1], I32)
        eps_col = sb(whole, "eps_col", [P, 1])
        xnT = sb(whole, "xnT", [P, NT, D])
        w_mix = sb(whole, "w_mix", [P, KD, D])
        b_o = sb(whole, "b_o", [1, D])

        weights_in = sem("weights_in")
        bias_in = sem("bias_in")
        self_ready = sem("self_ready")
        waited = sem("waited")

        with ExitStack() as early:
            hs = sb(early, "hs", [P, NT, D + 2 * HEADS])
            kv = sb(early, "kv", [P, NT, 2 * HID + 1])
            w_h = sb(early, "w_h", [P, KD, D + 2 * HEADS])
            w_kv = sb(early, "w_kv", [P, KD, 2 * HID])
            w_q = sb(early, "w_q", [P, KD, HID])
            w_o = sb(early, "w_o", [P, D])
            tile_min = sb(early, "tile_min", [EQ, 4])
            tile_max = sb(early, "tile_max", [EQ, 4])
            with ExitStack() as scope:
                xn = sb(scope, "xn", [P, UNROLL, D])
                xnT_slot = sb(scope, "xnT_slot", [P, UNROLL, D])
                att = sb(scope, "att", [P, 2, D])
                att_w = sb(scope, "att_w", [P, KD, D])
                edge_i = sb(scope, "edge_i", [EQ, 2, 4 * P], I32)
                edge_f = sb(scope, "edge_f", [EQ, 2, 4 * P])

                x_in = [sem(f"x_in{k}") for k in range(3)]
                edges_in = sem("edges_in")
                x_padded = sem("x_padded")
                edges_padded = sem("edges_padded")
                consts = sem("consts")
                stats_ready = sem("stats_ready")
                std_ready = sem("std_ready")
                rstd_ready = sem("rstd_ready")
                w_ready = sem("w_ready")
                xn_ready = sem("xn_ready")
                turned = sem("turned")
                xnT_kept = sem("xnT_kept")
                moments_ready = sem("moments_ready")
                xnT_ready = sem("xnT_ready")
                projected = sem("projected")
                h_copied = sem("h_copied")
                kv_copied = sem("kv_copied")
                h_stored = sem("h_stored")
                edges_f = sem("edges_f")
                edges_turned = sem("edges_turned")
                edges_done = sem("edges_done")
                v1 = Chain(sem("v1"))
                g1 = Chain(sem("g1"))

                PAIRS = ((3, 4), (5, 6), (2, 7), (3, 4), (5, 6))

                def rounds(eng, step):
                    with eng.Fori(0, NT // UNROLL - 1) as i:
                        for k in range(UNROLL):
                            step(i, k, False)
                    for k in range(UNROLL):
                        step(NT // UNROLL - 1, k, True)

                with nc.Block() as block:
                    @block.sync
                    def _(sp):
                        rows = x[0:(NT - 1) * P, :].rearrange("(t p) d -> p t d", p=P)
                        sp.dma_start(xs[:, 0:UNROLL, :], rows[:, 0:UNROLL, :]).then_inc(x_in[0], 16)
                        sp.wait_ge(edges_padded, 2)
                        full = E // (4 * P)
                        for j, edge in ((0, src), (1, dst)):
                            sp.dma_start(edge_i[0:full, j, :],
                                         edge[0:full * 4 * P].rearrange("(q e) -> q e", e=4 * P)).then_inc(edges_in, 16)
                            sp.dma_start(edge_i[full:full + 1, j, 0:E - full * 4 * P],
                                         edge[full * 4 * P:E].rearrange("(q e) -> q e", q=1)).then_inc(edges_in, 16)
                        sp.dma_start(xs[:, UNROLL:NT - 1, :], rows[:, UNROLL:, :]).then_inc(x_in[1], 16)
                        sp.wait_ge(x_padded, 1)
                        sp.dma_start(xs[0:LAST, NT - 1, :], x[(NT - 1) * P:N, :]).then_inc(x_in[2], 16)
                        with sp.Fori(0, NT) as t:
                            sp.wait_ge(h_copied, ahead(t + 1))
                            sp.dma_start(h_table.rearrange("(t p) r -> p t r", p=P)[:, bass.ds(t, 1), :],
                                         hs[:, bass.ds(t, 1), 0:ROW]).then_inc(h_stored, 16)
                        sp.wait_ge(h_stored, 16 * NT)

                    @block.gpsimd
                    def _(pool):
                        for counts in (xnT_kept, h_copied, kv_copied, turned, projected):
                            pool.sem_inc(counts, UNROLL)
                        pool.memset(edge_i[:, 0, :], 0).then_inc(edges_padded, 1)
                        pool.memset(edge_i[:, 1, :], 4095).then_inc(edges_padded, 1)
                        pool.memset(xs[:, NT - 1, :], 0.0).then_inc(x_padded, 1)
                        g1.done(pool.memset(ident[:, :], 0.0))
                        pool.wait_ge(g1.sem, g1.n)
                        pool.affine_select(out=ident[:, :], in_=ident[:, :], compare_op=ALU.not_equal, fill=1.0,
                                           base=0, pattern=[[-1, P]], channel_multiplier=1).then_inc(consts, 1)
                        pool.memset(ones[:, :], 1.0).then_inc(consts, 1)
                        pool.memset(eps_col[:, :], EPS).then_inc(consts, 1)
                        pool.iota(iota_row[:, :], [[1, P]], base=0, channel_multiplier=0,
                                  allow_small_or_imprecise_dtypes=True).then_inc(consts, 1)
                        pool.iota(minus_base[:, :], [[-P, NB + 1]], base=0, channel_multiplier=0,
                                  allow_small_or_imprecise_dtypes=True).then_inc(consts, 1)
                        pool.memset(kv[:, :, 2 * HID:2 * HID + 1], 1.0).then_inc(consts, 1)

                    @block.scalar
                    def _(act):
                        act.dma_start(w_h[:, :, 0:D], w_gat.rearrange("(k p) n -> p k n", p=P)).then_inc(weights_in, 16)
                        act.dma_start(w_q[:, :, :], w_qkv[:, 0:HID].rearrange("(k p) n -> p k n", p=P)).then_inc(weights_in, 16)
                        act.dma_start(w_kv[:, :, :], w_qkv[:, HID:3 * HID].rearrange("(k p) n -> p k n", p=P)).then_inc(weights_in, 16)
                        act.dma_start(att[:, 0, :], att_src.rearrange("h c -> (h c)").partition_broadcast(P)).then_inc(weights_in, 16)
                        act.dma_start(att[:, 1, :], att_dst.rearrange("h c -> (h c)").partition_broadcast(P)).then_inc(weights_in, 16)
                        act.dma_start(w_o[:, :], w_out).then_inc(bias_in, 16)
                        act.dma_start(b_o[:, :], b_out.rearrange("(a d) -> a d", a=1)).then_inc(bias_in, 16)
                        act.dma_start(gat_bias_sb[:, :], gat_bias.partition_broadcast(P)).then_inc(bias_in, 16)
                        act.wait_ge(consts, CONSTS)

                        def deviations(i):
                            act.wait_ge(moments_ready, i * UNROLL + UNROLL)
                            act.activation(rstd[:, 0:UNROLL], moments[:, 0:UNROLL, 1], ACT.Sqrt, bias=eps_col[:, :]).then_inc(std_ready, 1)

                        def keep(t, k):
                            act.wait_ge(turned, ahead(t + 1))
                            rows_T = bank[k % 2][:, 0:D]
                            act.activation(xnT_slot[:, k, :], rows_T, ACT.Copy).then_inc(xnT_ready, 1)
                            act.activation(flat(xnT[:, bass.ds(t, 1), :]), rows_T, ACT.Copy).then_inc(xnT_kept, 1)

                        def step(i, k, last):
                            t = i * UNROLL + k
                            if not (last and k == UNROLL - 1):
                                keep(t + 1, (k + 1) % UNROLL)
                            act.wait_ge(projected, ahead(t + 1))
                            act.activation(flat(kv[:, bass.ds(t, 1), 0:2 * HID]), bank[PAIRS[k][1]][:, 0:2 * HID],
                                           ACT.Copy).then_inc(kv_copied, 1)
                            if k == 2 and not last:
                                deviations(i + 1)

                        deviations(0)
                        keep(0, 0)
                        rounds(act, step)

                    @block.tensor
                    def _(pe):
                        pe.wait_ge(consts, CONSTS)
                        pe.wait_ge(edges_f, 2)
                        for j in range(2):
                            for q in range(4):
                                tr = pe.transpose(bank[j][:, q * EQ:(q + 1) * EQ], edge_f[:, j, q * P:(q + 1) * P],
                                                  ident[0:EQ, 0:EQ])
                            tr.then_inc(edges_turned, 1)

                        def turn(t, k):
                            pe.wait_ge(xn_ready, t + 1)
                            pe.wait_ge(xnT_kept, ahead(t if k == 0 else t - 1))
                            for c in range(KD):
                                tr = pe.transpose(bank[k % 2][:, c * P:(c + 1) * P],
                                                  xn[:, k, c * P:(c + 1) * P], ident[:, :])
                            tr.then_inc(turned, 1)

                        def step(i, k, last):
                            t = i * UNROLL + k
                            if not (last and k == UNROLL - 1):
                                turn(t + 1, (k + 1) % UNROLL)
                            pe.wait_ge(xnT_ready, t + 1)
                            pe.wait_ge(h_copied, ahead(t - 1))
                            pe.wait_ge(kv_copied, ahead(t - 1))
                            for c in range(KD):
                                pe.matmul(bank[PAIRS[k][0]][:, 0:D + 2 * HEADS], xnT_slot[:, k, c * P:(c + 1) * P],
                                          w_h[:, c, :], start=(c == 0), stop=(c == KD - 1))
                            for c in range(KD):
                                mm = pe.matmul(bank[PAIRS[k][1]][:, 0:2 * HID], xnT_slot[:, k, c * P:(c + 1) * P],
                                               w_kv[:, c, :], start=(c == 0), stop=(c == KD - 1))
                            mm.then_inc(projected, 1)

                        pe.wait_ge(edges_done, 4)
                        turn(0, 0)
                        pe.wait_ge(w_ready, 1)
                        rounds(pe, step)

                    @block.vector
                    def _(dve):

                        def statistics(i, k):
                            dve.bn_stats(stats[:, k, :], flat(xs[:, bass.ds(i * UNROLL + k, 1), :])).then_inc(stats_ready, 1)

                        def averages(i):
                            dve.wait_ge(stats_ready, i * UNROLL + UNROLL)
                            if not isinstance(i, int) or i > 0:
                                dve.wait_ge(xn_ready, i * UNROLL)
                                dve.sem_inc(waited, 1)
                            for k in range(UNROLL):
                                dve.bn_aggr(moments[:, k, :], stats[:, k, :]).then_inc(moments_ready, 1)

                        def invert(i):
                            dve.wait_ge(std_ready, i + 1)
                            dve.reciprocal(rstd[:, 0:UNROLL], rstd[:, 0:UNROLL]).then_inc(rstd_ready, 1)
                            dve.wait_ge(rstd_ready, i + 1)

                        def normalise(t, k):
                            dve.wait_ge(turned, ahead(t + 1 - UNROLL))
                            dve.tensor_scalar(xn[:, k, :], flat(xs[:, bass.ds(t, 1), :]), moments[:, k, 0:1],
                                              rstd[:, k:k + 1], ALU.subtract, ALU.mult).then_inc(xn_ready, 1)

                        dve.wait_ge(x_in[0], 16)
                        for k in range(UNROLL):
                            statistics(0, k)
                        averages(0)
                        dve.wait_ge(edges_in, 64)
                        for j in range(2):
                            dve.tensor_copy(edge_f[:, j, :], edge_i[:, j, :]).then_inc(edges_f, 1)
                        dve.wait_ge(edges_f, 2)
                        by_tile = edge_f[:, 1, :].rearrange("q (k e) -> q k e", e=P)
                        dve.tensor_reduce(tile_min[:, :], by_tile, AX.X, ALU.min).then_inc(edges_done, 1)
                        dve.tensor_reduce(tile_max[:, :], by_tile, AX.X, ALU.max).then_inc(edges_done, 1)
                        for j, column in ((0, src_col), (1, dst_col)):
                            dve.wait_ge(edges_turned, j + 1)
                            dve.tensor_copy(column[:, :].rearrange("p (q k) -> p k q", k=4),
                                            bank[j][:, 0:4 * EQ].rearrange("p (k q) -> p k q", k=4)).then_inc(edges_done, 1)
                        invert(0)
                        normalise(0, 0)
                        normalise(1, 1)
                        dve.wait_ge(weights_in, 80)
                        for j in range(2):
                            if j:
                                dve.wait_ge(v1.sem, v1.n)
                            v1.done(dve.tensor_tensor(att_w[:, :, :], w_h[:, :, 0:D],
                                                      att[:, j:j + 1, :].broadcast_to((P, KD, D)), ALU.mult))
                            dve.wait_ge(v1.sem, v1.n)
                            v1.done(dve.tensor_reduce(w_h[:, :, D + j * HEADS:D + (j + 1) * HEADS],
                                                      att_w[:, :, :].rearrange("p k (h c) -> p k h c", c=C), AX.X, ALU.add))
                        dve.wait_ge(v1.sem, v1.n)
                        dve.sem_inc(w_ready, 1)
                        dve.wait_ge(x_in[1], 16)
                        dve.wait_ge(x_in[2], 16)

                        def step(i, k, last):
                            t = i * UNROLL + k
                            if not last and k == UNROLL - 2:
                                invert(i + 1)
                            if not (last and k >= UNROLL - 2):
                                normalise(t + 2, (k + 2) % UNROLL)
                            if not last:
                                for n in {0: (0, 1), 1: (2, 3), 2: (4,)}.get(k, ()):
                                    statistics(i + 1, n)
                                if k == 2:
                                    averages(i + 1)
                            dve.wait_ge(projected, ahead(t + 1))
                            dve.tensor_copy(flat(hs[:, bass.ds(t, 1), :]), bank[PAIRS[k][0]][:, 0:D + 2 * HEADS]).then_inc(h_copied, 1)

                        rounds(dve, step)
                        dve.wait_ge(h_copied, ahead(NT))

            with ExitStack() as scope:
                kmax = sb(scope, "kmax", [P, HID])
                kcol = sb(scope, "kcol", [P, 1])
                kdiag = sb(scope, "kdiag", [P, P])
                head_mask = sb(scope, "head_mask", [P, HID])
                key_sum = sb(scope, "key_sum", [P, 1])
                ctx = sb(scope, "ctx", [P, HID])
                ctxT = sb(scope, "ctxT", [P, HID])
                ctx_out = sb(scope, "ctx_out", [P, D])
                w_qT = sb(scope, "w_qT", [P, D])
                amax_p = sb(scope, "amax_p", [P, HEADS])
                amax_c = sb(scope, "amax_c", [HEADS, 1])
                amax_d = sb(scope, "amax_d", [HEADS, HEADS])
                amax = sb(scope, "amax", [P, HEADS])
                self_z = sb(scope, "self_z", [P, NT, HEADS])
                block_lo = sb(scope, "block_lo", [P, NB])
                tile_id = sb(scope, "tile_id", [P, 4])
                has = sb(scope, "has", [EQ, 4, NB])
                has2 = sb(scope, "has2", [EQ, 4, NB])
                first_q = sb(scope, "first_q", [EQ, NB])
                last_q = sb(scope, "last_q", [EQ, NB])
                span = sb(scope, "span", [NB, 4])
                upto = sb(scope, "upto", [P, P])
                span_rows = sb(scope, "span_rows", [NB, 3 * NB])
                rows = sb(scope, "rows", [P, 3 * NB])
                visit_id = sb(scope, "visit_id", [P, VCOL])
                past = sb(scope, "past", [P, VCOL, NB])
                within = sb(scope, "within", [P, VCOL, NB])
                from_visit = sb(scope, "from_visit", [P, NB + 1])
                change = sb(scope, "change", [P, NB])
                vb = sb(scope, "vb", [P, VCOL])
                vt = sb(scope, "vt", [P, VCOL])
                vb_i = sb(scope, "vb_i", [P, VCOL], I32)
                vt_i = sb(scope, "vt_i", [P, VCOL], I32)
                chunk_lo = sb(scope, "chunk_lo", [1, MAXCHUNK])

                pool_ready = sem("pool_ready")
                kmax_ready = sem("kmax_ready")
                kmax_turned = sem("kmax_turned")
                kdiag_ready = sem("kdiag_ready")
                kmax_spread = sem("kmax_spread")
                keys_shifted = sem("keys_shifted")
                keys_exp = sem("keys_exp")
                ctx_summed = sem("ctx_summed")
                ctx_ready = sem("ctx_ready")
                ctx_turned = sem("ctx_turned")
                ctxT_ready = sem("ctxT_ready")
                ctx_out_summed = sem("ctx_out_summed")
                ctx_out_ready = sem("ctx_out_ready")
                w_q_turned = sem("w_q_turned")
                w_qT_ready = sem("w_qT_ready")
                w_mix_summed = sem("w_mix_summed")
                w_mix_ready = sem("w_mix_ready")
                amax_ready = sem("amax_ready")
                amax_turned = sem("amax_turned")
                amax_diag = sem("amax_diag")
                amax_spread = sem("amax_spread")
                self_logits = sem("self_logits")
                self_exp = sem("self_exp")
                spans_ready = sem("spans_ready")
                spans_turned = sem("spans_turned")
                rows_ready = sem("rows_ready")
                rows_spread = sem("rows_spread")
                visits_ready = sem("visits_ready")
                visits_stored = sem("visits_stored")
                v2 = Chain(sem("v2"))
                g2 = Chain(sem("g2"))

                with nc.Block() as block:
                    @block.gpsimd
                    def _(pool):
                        pool.iota(block_lo[:, :], [[P, NB]], base=0, channel_multiplier=0,
                                  allow_small_or_imprecise_dtypes=True).then_inc(pool_ready, 1)
                        pool.iota(tile_id[:, :], [[1, 4]], base=0, channel_multiplier=4,
                                  allow_small_or_imprecise_dtypes=True).then_inc(pool_ready, 1)
                        pool.iota(visit_id[:, :], [[1, VCOL]], base=0, channel_multiplier=VCOL,
                                  allow_small_or_imprecise_dtypes=True).then_inc(pool_ready, 1)
                        pool.iota(chunk_lo[:, :], [[CH, MAXCHUNK]], base=0, channel_multiplier=0,
                                  allow_small_or_imprecise_dtypes=True).then_inc(pool_ready, 1)
                        g2.done(pool.memset(upto[:, :], 1.0))
                        pool.wait_ge(g2.sem, g2.n)
                        pool.affine_select(out=upto[:, :], in_=upto[:, :], compare_op=ALU.is_ge, fill=0.0,
                                           base=0, pattern=[[1, P]], channel_multiplier=-1).then_inc(pool_ready, 1)
                        g2.done(pool.memset(head_mask[:, :], 0.0))
                        pool.wait_ge(g2.sem, g2.n)
                        for h in range(HEADS):
                            g2.done(pool.memset(head_mask[h * DH:(h + 1) * DH, h * DH:(h + 1) * DH], 1.0))
                            pool.wait_ge(g2.sem, g2.n)
                        pool.memset(acc[:, NB, :], 0.0).then_inc(pool_ready, 1)
                        pool.memset(adc[:, NB, :], 0.0).then_inc(pool_ready, 1)
                        pool.memset(from_visit[:, NB:NB + 1], 0.0).then_inc(pool_ready, 1)
                        pool.wait_ge(self_exp, 1)
                        pool.tensor_tensor(acc[:, 0:NB, 0:D].rearrange("p t (h c) -> p t h c", c=C),
                                           hs[:, :, 0:D].rearrange("p t (h c) -> p t h c", c=C),
                                           acc[:, 0:NB, D:ROW].unsqueeze(3).broadcast_to((P, NB, HEADS, C)), ALU.mult).then_inc(self_ready, 1)

                    @block.vector
                    def _(dve):
                        def after(instruction):
                            v2.done(instruction)
                            dve.wait_ge(v2.sem, v2.n)

                        after(dve.tensor_reduce(kmax[:, :], kv[:, 0:NT - 1, 0:HID].rearrange("p t c -> p c t"), AX.X, ALU.max))
                        dve.tensor_tensor(kmax[0:LAST, :], kmax[0:LAST, :], kv[0:LAST, NT - 1, 0:HID], ALU.max).then_inc(kmax_ready, 1)
                        dve.tensor_reduce(amax_p[:, :], hs[:, :, D:D + HEADS].rearrange("p t h -> p h t"), AX.X, ALU.max).then_inc(amax_ready, 1)
                        dve.wait_ge(kmax_turned, 1)
                        after(dve.tensor_reduce(kcol[:, :], bank[0][:, 0:P], AX.X, ALU.max))
                        dve.tensor_scalar(kdiag[:, :], ident[:, :], kcol[:, 0:1], None, ALU.mult).then_inc(kdiag_ready, 1)
                        dve.wait_ge(amax_turned, 1)
                        after(dve.tensor_reduce(amax_c[:, :], bank[1][0:HEADS, 0:P], AX.X, ALU.max))
                        dve.tensor_scalar(amax_d[:, :], ident[0:HEADS, 0:HEADS], amax_c[:, 0:1], None, ALU.mult).then_inc(amax_diag, 1)
                        dve.wait_ge(amax_spread, 1)
                        after(dve.tensor_copy(amax[:, :], bank[3][:, 0:HEADS]))
                        a_src, a_dst = hs[:, :, D:D + HEADS], hs[:, :, D + HEADS:D + 2 * HEADS]
                        logit, shift = adc[:, 0:NB, 0:HEADS], adc[:, 0:NB, HEADS:2 * HEADS]
                        dve.tensor_copy(logit, a_dst)
                        after(dve.tensor_tensor(shift, a_dst, amax[:, :].unsqueeze(1).broadcast_to((P, NT, HEADS)), ALU.add))
                        after(dve.scalar_tensor_tensor(out=shift, in0=shift, scalar=SLOPE, in1=shift, op0=ALU.mult, op1=ALU.max))
                        after(dve.tensor_tensor(self_z[:, :, :], a_src, a_dst, ALU.add))
                        after(dve.scalar_tensor_tensor(out=self_z[:, :, :], in0=self_z[:, :, :], scalar=SLOPE, in1=self_z[:, :, :],
                                                       op0=ALU.mult, op1=ALU.max))
                        dve.tensor_tensor(self_z[:, :, :], self_z[:, :, :], shift, ALU.subtract).then_inc(self_logits, 1)

                        dve.wait_ge(kmax_spread, 1)
                        for i in range(NT // UNROLL):
                            keys = kv[:, i * UNROLL:(i + 1) * UNROLL, 0:HID]
                            dve.tensor_tensor(keys, keys, bank[2][:, 0:HID].unsqueeze(1).broadcast_to((P, UNROLL, HID)),
                                              ALU.subtract).then_inc(keys_shifted, 1)

                        dve.wait_ge(pool_ready, 8)
                        wide = (EQ, 4, NB)
                        blocks = block_lo[0:EQ, :].unsqueeze(1).broadcast_to(wide)
                        after(dve.tensor_scalar(tile_min[:, :], tile_min[:, :], -float(P - 1), None, ALU.add))
                        dve.tensor_tensor(has[:, :, :], blocks, tile_min[:, :].unsqueeze(2).broadcast_to(wide), ALU.is_ge)
                        after(dve.tensor_tensor(has2[:, :, :], blocks, tile_max[:, :].unsqueeze(2).broadcast_to(wide), ALU.is_le))
                        after(dve.tensor_tensor(has[:, :, :], has[:, :, :], has2[:, :, :], ALU.mult))
                        after(dve.tensor_scalar(tile_id[:, :], tile_id[:, :], 1.0, None, ALU.add))
                        after(dve.tensor_tensor(has2[:, :, :], has[:, :, :], tile_id[0:EQ, :].unsqueeze(2).broadcast_to(wide), ALU.mult))
                        dve.tensor_reduce(last_q[:, :], has2[:, :, :].rearrange("q k b -> q b k"), AX.X, ALU.max)
                        after(dve.tensor_scalar(has[:, :, :], has[:, :, :], -BIG, BIG - 1.0, ALU.mult, ALU.add))
                        after(dve.tensor_tensor(has2[:, :, :], has[:, :, :], tile_id[0:EQ, :].unsqueeze(2).broadcast_to(wide), ALU.add))
                        dve.tensor_reduce(first_q[:, :], has2[:, :, :].rearrange("q k b -> q b k"), AX.X, ALU.min).then_inc(spans_ready, 1)
                        dve.wait_ge(spans_turned, 1)
                        after(dve.tensor_reduce(span[:, 0:1], bank[4][0:NB, 0:EQ], AX.X, ALU.min))
                        after(dve.tensor_reduce(span[:, 1:2], bank[4][0:NB, P:P + EQ], AX.X, ALU.max))
                        after(dve.tensor_tensor(span[:, 2:3], span[:, 1:2], span[:, 0:1], ALU.subtract))
                        after(dve.tensor_scalar(span[:, 3:4], span[:, 2:3], 0.0, None, ALU.max))
                        dve.tensor_scalar(span_rows[:, 0:NB], upto[0:NB, 0:NB], span[:, 3:4], None, ALU.mult)
                        dve.tensor_scalar(span_rows[:, NB:2 * NB], ident[0:NB, 0:NB], span[:, 3:4], None, ALU.mult)
                        dve.tensor_scalar(span_rows[:, 2 * NB:3 * NB], ident[0:NB, 0:NB], span[:, 0:1], None, ALU.mult).then_inc(rows_ready, 1)
                        dve.wait_ge(rows_spread, 1)
                        after(dve.tensor_copy(rows[:, :], bank[5][:, 0:3 * NB]))
                        upto_b, of_b, first_b = rows[:, 0:NB], rows[:, NB:2 * NB], rows[:, 2 * NB:3 * NB]
                        after(dve.tensor_scalar(chunk_lo[:, :], chunk_lo[:, :], rows[0:1, NB - 1:NB], None, ALU.is_lt))
                        after(dve.tensor_reduce(key_sum[0:1, :], chunk_lo[:, :], AX.X, ALU.add))
                        after(dve.tensor_copy(chunks_i[:, :], key_sum[0:1, :]))
                        after(dve.tensor_tensor(of_b, upto_b, of_b, ALU.subtract))
                        after(dve.tensor_tensor(from_visit[:, 0:NB], first_b, of_b, ALU.subtract))
                        after(dve.tensor_tensor(change[:, :], from_visit[:, 1:NB + 1], from_visit[:, 0:NB], ALU.subtract))
                        grid = (P, VCOL, NB)
                        ids = visit_id[:, :].unsqueeze(2).broadcast_to(grid)
                        after(dve.tensor_tensor(past[:, :, :], ids, upto_b.unsqueeze(1).broadcast_to(grid), ALU.is_ge))
                        dve.tensor_reduce(vb[:, :], past[:, :, :], AX.X, ALU.add)
                        after(dve.tensor_tensor(within[:, :, :], past[:, :, :], change[:, :].unsqueeze(1).broadcast_to(grid), ALU.mult))
                        after(dve.tensor_reduce(vt[:, :], within[:, :, :], AX.X, ALU.add))
                        after(dve.tensor_tensor(vt[:, :], vt[:, :], visit_id[:, :], ALU.add))
                        after(dve.tensor_scalar(vt[:, :], vt[:, :], from_visit[:, 0:1], None, ALU.add))
                        after(dve.tensor_scalar(vt[:, :], vt[:, :], float(ET - 1), None, ALU.min))
                        dve.tensor_copy(vt_i[:, :], vt[:, :]).then_inc(visits_ready, 1)
                        dve.tensor_copy(vb_i[:, :], vb[:, :]).then_inc(visits_ready, 1)

                        dve.wait_ge(ctx_summed, 1)
                        after(dve.reciprocal(key_sum[:, :], bank[0][:, HID:HID + 1]))
                        after(dve.tensor_scalar(ctx[:, :], bank[0][:, 0:HID], key_sum[:, 0:1], QSCALE, ALU.mult, ALU.mult))
                        dve.tensor_tensor(ctx[:, :], ctx[:, :], head_mask[:, :], ALU.mult).then_inc(ctx_ready, 1)
                        dve.wait_ge(w_q_turned, 1)
                        dve.tensor_copy(w_qT[:, :], bank[6][:, 0:D]).then_inc(w_qT_ready, 1)
                        dve.wait_ge(ctx_turned, 1)
                        dve.tensor_copy(ctxT[:, :], bank[1][:, 0:P]).then_inc(ctxT_ready, 1)
                        dve.wait_ge(ctx_out_summed, 1)
                        dve.tensor_copy(ctx_out[:, :], bank[2][:, 0:D]).then_inc(ctx_out_ready, 1)
                        dve.wait_ge(w_mix_summed, 1)
                        dve.tensor_copy(w_mix[:, :, :], bank[3][:, :].rearrange("p (k d) -> p k d", k=KD)).then_inc(w_mix_ready, 1)
                        dve.wait_ge(w_mix_ready, 1)

                    @block.scalar
                    def _(act):
                        act.wait_ge(self_logits, 1)
                        act.activation(acc[:, 0:NB, D:ROW], self_z[:, :, :], ACT.Exp).then_inc(self_exp, 1)
                        for i in range(NT // UNROLL):
                            keys = kv[:, i * UNROLL:(i + 1) * UNROLL, 0:HID]
                            act.wait_ge(keys_shifted, i + 1)
                            act.activation(keys, keys, ACT.Exp).then_inc(keys_exp, 1)

                    @block.tensor
                    def _(pe):
                        pe.wait_ge(kmax_ready, 1)
                        pe.transpose(bank[0][:, 0:P], kmax[:, :], ident[:, :]).then_inc(kmax_turned, 1)
                        pe.wait_ge(amax_ready, 1)
                        pe.transpose(bank[1][0:HEADS, 0:P], amax_p[:, :], ident[:, :]).then_inc(amax_turned, 1)
                        pe.wait_ge(kdiag_ready, 1)
                        pe.matmul(bank[2][:, 0:P], ones[:, :], kdiag[:, :], start=True, stop=True).then_inc(kmax_spread, 1)
                        pe.wait_ge(amax_diag, 1)
                        pe.matmul(bank[3][:, 0:HEADS], ones[0:HEADS, :], amax_d[:, :], start=True, stop=True).then_inc(amax_spread, 1)
                        for c in range(KD):
                            tr = pe.transpose(bank[6][:, c * P:(c + 1) * P], w_q[:, c, :], ident[:, :])
                        tr.then_inc(w_q_turned, 1)
                        for t in range(NT):
                            if t % UNROLL == 0:
                                pe.wait_ge(keys_exp, t // UNROLL + 1)
                            n = P if t < NT - 1 else LAST
                            mm = pe.matmul(bank[0][:, 0:HID + 1], kv[0:n, t, 0:HID], kv[0:n, t, HID:2 * HID + 1],
                                           start=(t == 0), stop=(t == NT - 1))
                        mm.then_inc(ctx_summed, 1)
                        pe.wait_ge(spans_ready, 1)
                        pe.transpose(bank[4][0:NB, 0:EQ], first_q[:, :], ident[0:EQ, 0:EQ])
                        pe.transpose(bank[4][0:NB, P:P + EQ], last_q[:, :], ident[0:EQ, 0:EQ]).then_inc(spans_turned, 1)
                        pe.wait_ge(rows_ready, 1)
                        pe.matmul(bank[5][:, 0:3 * NB], ones[0:NB, :], span_rows[:, :], start=True, stop=True).then_inc(rows_spread, 1)
                        pe.wait_ge(ctx_ready, 1)
                        pe.transpose(bank[1][:, 0:P], ctx[:, :], ident[:, :]).then_inc(ctx_turned, 1)
                        pe.wait_ge(ctxT_ready, 1)
                        pe.wait_ge(bias_in, 48)
                        pe.matmul(bank[2][:, 0:D], ctxT[:, :], w_o[:, :], start=True, stop=True).then_inc(ctx_out_summed, 1)
                        pe.wait_ge(ctx_out_ready, 1)
                        pe.wait_ge(w_qT_ready, 1)
                        for c in range(KD):
                            mm = pe.matmul(bank[3][:, c * D:(c + 1) * D], w_qT[:, c * P:(c + 1) * P], ctx_out[:, :],
                                           start=True, stop=True)
                        mm.then_inc(w_mix_summed, 1)

                    @block.sync
                    def _(sp):
                        sp.wait_ge(visits_ready, 2)
                        sp.dma_start(visit_tile.rearrange("(p c) -> p c", c=VCOL), vt_i[:, :]).then_inc(visits_stored, 16)
                        sp.dma_start(visit_block.rearrange("(p c) -> p c", c=VCOL), vb_i[:, :]).then_inc(visits_stored, 16)
                        sp.wait_ge(visits_stored, 32)

        w2_in = sem("w2_in")
        w2_sb = sb(whole, "w2_sb", [P, NX * KF, D])
        with ExitStack() as scope:
            table = sb(scope, "table", [1, 2, CH], I32)
            gathered = sb(scope, "gathered", [P, RING, G, ROW])
            index = sb(scope, "index", [P, RING, G], U32)
            local = sb(scope, "local", [P, RING, G])
            one_hot = sb(scope, "one_hot", [P, RING, G, P])
            one_hotT = sb(scope, "one_hotT", [P, 2, G, P])
            z = sb(scope, "z", [P, G, HEADS])
            turned_bank, ad_bank, sum_bank = bank[0:2], bank[2:4], bank[4:8]

            table_in = sem("table_in")
            cols_ready = sem("cols_ready")
            gather_done = [sem(f"gather_done{r}") for r in range(RING)]
            hot_ready = sem("hot_ready")
            hot_turned = sem("hot_turned")
            hotT_ready = sem("hotT_ready")
            ad_ready = sem("ad_ready")
            logit_step = sem("logit_step")
            logits_ready = sem("logits_ready")
            exp_ready = sem("exp_ready")
            weighted = sem("weighted")
            summed = sem("summed")
            added = sem("added")

            def steps(eng, c, step):
                for r in range(RING):
                    step(c * NGRP + r, r, r, RING)
                with eng.Fori(1, NGRP // RING - 1) as i:
                    for r in range(RING):
                        step(c * NGRP + i * RING + r, i * RING + r, r, RING)
                for r in range(RING):
                    step(c * NGRP + NGRP - RING + r, NGRP - RING + r, r, RING - 1 - r)

            with nc.Block() as block:
                @block.sync
                def _(sp):
                    chunks = sp.value_load(chunks_i[0:1, 0:1], min_val=1, max_val=MAXCHUNK)
                    with sp.Fori(0, chunks) as c:
                        first = sp.snap(c * CH)
                        sp.wait_ge(added, from_one(first))
                        sp.sem_inc(waited, 1)
                        sp.dma_start(table[0:1, 0, :], visit_tile[bass.ds(first, CH)].unsqueeze(0)).then_inc(table_in, 16)
                        sp.dma_start(table[0:1, 1, :], visit_block[bass.ds(first, CH)].unsqueeze(0)).then_inc(table_in, 16)
                        with sp.If(c == 0):
                            for e in range(NX):
                                sp.wait_ge(added, from_one(2 * G * (e + 1)))
                                sp.dma_start(w2_sb[:, e * KF:(e + 1) * KF, :],
                                             w2[e:e + 1, :, :].rearrange("e (k p) d -> p (e k) d", p=P)).then_inc(w2_in, 16)

                @block.gpsimd
                def _(pool):
                    for counts in (summed, added, ad_ready, logits_ready):
                        pool.sem_inc(counts, 1)
                    chunks = pool.value_load(chunks_i[0:1, 0:1], min_val=1, max_val=MAXCHUNK)
                    with pool.Fori(0, chunks) as c:
                        with pool.Fori(0, NGRP // RING) as i:
                            for r in range(RING):
                                pool.wait_ge(cols_ready, c * NGRP + i * RING + r + 1)
                                pool.sem_inc(waited, 1)
                                for j in range(G):
                                    pool.indirect_dma_start(gathered[:, r, j, :], None, h_table,
                                                            bass.IndirectOffsetOnAxis(ap=index[:, r, j:j + 1], axis=0)
                                                            ).then_inc(gather_done[r], 16)

                @block.scalar
                def _(act):
                    chunks = act.value_load(chunks_i[0:1, 0:1], min_val=1, max_val=MAXCHUNK)
                    tile_regs = [act.alloc_register(f"act_tile{j}") for j in range(G)]
                    block_regs = [act.alloc_register(f"act_block{j}") for j in range(G)]

                    def columns(s, r, free):
                        act.load(tile_regs, table[0:1, 0, bass.ds(s * G, G)])
                        act.load(block_regs, table[0:1, 1, bass.ds(s * G, G)])
                        act.wait_ge(summed, from_one(free))
                        for j in range(G):
                            t = act.snap(tile_regs[j], min_val=0, max_val=ET - 1)
                            b = act.snap(block_regs[j], min_val=0, max_val=NB)
                            act.activation(index[:, r, j:j + 1], src_col[:, bass.ds(t, 1)], ACT.Copy)
                            op = act.activation(local[:, r, j:j + 1], dst_col[:, bass.ds(t, 1)], ACT.Identity,
                                                bias=minus_base[:, bass.ds(b, 1)])
                        op.then_inc(cols_ready, 1)

                    def turned_out(n, half):
                        act.wait_ge(hot_turned, n)
                        act.activation(one_hotT[:, half, :, :].rearrange("p a b -> p (a b)"), turned_bank[half][:, :],
                                       ACT.Copy).then_inc(hotT_ready, 1)

                    def exps(n, r):
                        act.wait_ge(logits_ready, from_one(n))
                        act.activation(gathered[:, r, :, D:ROW], z[:, :, :], ACT.Exp).then_inc(exp_ready, 1)

                    def step(n, s, r, ahead):
                        if ahead >= 1:
                            act.wait_ge(ad_ready, from_one(n))
                            turned_out(n + 2, (r + 1) % 2)
                        if ahead >= 3:
                            columns(s + 3, (r + 3) % RING, n)
                        if ahead >= 1:
                            exps(n + 2, (r + 1) % RING)

                    with act.Fori(0, chunks) as c:
                        act.wait_ge(table_in, c * 32 + 32)
                        act.sem_inc(waited, 1)
                        for r in range(3):
                            columns(r, r, c * NGRP)
                        turned_out(c * NGRP + 1, 0)
                        exps(c * NGRP + 1, 0)
                        steps(act, c, step)

                @block.tensor
                def _(pe):
                    chunks = pe.value_load(chunks_i[0:1, 0:1], min_val=1, max_val=MAXCHUNK)
                    block_regs = [pe.alloc_register(f"pe_block{j}") for j in range(G)]

                    def turn(n, r, half):
                        pe.wait_ge(hot_ready, n)
                        for j in range(G):
                            tr = pe.transpose(turned_bank[half][:, j * P:(j + 1) * P], one_hot[:, r, j, :], ident[:, :])
                        tr.then_inc(hot_turned, 1)

                    def spread(n, half):
                        pe.wait_ge(hotT_ready, n)
                        for j in range(G):
                            b = pe.snap(block_regs[j], min_val=0, max_val=NB)
                            mm = pe.matmul(ad_bank[half][:, j * 2 * HEADS:(j + 1) * 2 * HEADS], one_hotT[:, half, j, :],
                                           flat(adc[:, bass.ds(b, 1), :]), start=True, stop=True)
                        mm.then_inc(ad_ready, 1)

                    def step(n, s, r, ahead):
                        if ahead >= 1:
                            pe.load(block_regs, table[0:1, 1, bass.ds((s + 1) * G, G)])
                            pe.wait_ge(logits_ready, from_one(n))
                            spread(n + 2, (r + 1) % 2)
                        pe.wait_ge(weighted, n + 1)
                        for j in range(G):
                            pe.wait_ge(added, from_one((n - 1) * G + j + 1 if not isinstance(s, int) or s > 0 else n * G))
                            mm = pe.matmul(sum_bank[j][:, 0:ROW], one_hot[:, r, j, :], gathered[:, r, j, :],
                                           start=True, stop=True)
                        mm.then_inc(summed, 1)
                        if ahead >= 2:
                            turn(n + 3, (r + 2) % RING, r % 2)

                    with pe.Fori(0, chunks) as c:
                        pe.wait_ge(table_in, c * 32 + 32)
                        pe.sem_inc(waited, 1)
                        pe.load(block_regs, table[0:1, 1, 0:G])
                        turn(c * NGRP + 1, 0, 0)
                        spread(c * NGRP + 1, 0)
                        turn(c * NGRP + 2, 1, 1)
                        steps(pe, c, step)

                @block.vector
                def _(dve):
                    chunks = dve.value_load(chunks_i[0:1, 0:1], min_val=1, max_val=MAXCHUNK)
                    block_regs = [dve.alloc_register(f"dve_block{j}") for j in range(G)]

                    def hot(r, j):
                        return dve.tensor_scalar(one_hot[:, r, j, :], iota_row[:, :], local[:, r, j:j + 1], None, ALU.is_equal)

                    def add_sum(n, j):
                        b = dve.snap(block_regs[j], min_val=0, max_val=NB)
                        dve.wait_ge(added, from_one(n * G + j))
                        dve.tensor_tensor(flat(acc[:, bass.ds(b, 1), :]), flat(acc[:, bass.ds(b, 1), :]),
                                          sum_bank[j][:, 0:ROW], ALU.add).then_inc(added, 1)

                    def logits(n, r, half, part):
                        ad = ad_bank[half][:, 0:G * 2 * HEADS].rearrange("p (j a) -> p j a", j=G)
                        if part == 0:
                            dve.wait_ge(ad_ready, from_one(n + 1))
                            dve.tensor_tensor(z[:, :, :], gathered[:, r, :, D:ROW], ad[:, :, 0:HEADS], ALU.add).then_inc(logit_step, 1)
                        elif part == 1:
                            dve.wait_ge(logit_step, n * 2 + 1)
                            dve.scalar_tensor_tensor(out=z[:, :, :], in0=z[:, :, :], scalar=SLOPE, in1=z[:, :, :],
                                                     op0=ALU.mult, op1=ALU.max).then_inc(logit_step, 1)
                        else:
                            dve.wait_ge(logit_step, n * 2 + 2)
                            dve.tensor_tensor(z[:, :, :], z[:, :, :], ad[:, :, HEADS:2 * HEADS], ALU.subtract).then_inc(logits_ready, 1)

                    def weigh(n, r):
                        dve.wait_ge(exp_ready, n + 1)
                        message = gathered[:, r, :, 0:D].rearrange("p j (h c) -> p j h c", c=C)
                        dve.tensor_tensor(message, message,
                                          gathered[:, r, :, D:ROW].unsqueeze(3).broadcast_to((P, G, HEADS, C)),
                                          ALU.mult).then_inc(weighted, 1)

                    with dve.Fori(0, chunks) as c:
                        rounds = c * (NGRP // RING)

                        def step(n, s, r, ahead):
                            before = not isinstance(s, int) or s > 0
                            if before:
                                dve.load(block_regs, table[0:1, 1, bass.ds(s * G - G, G)])
                            weigh(n, r)
                            if ahead >= 2:
                                dve.wait_ge(cols_ready, n + 3)
                            if before:
                                dve.wait_ge(summed, from_one(n))
                            for j in range(G):
                                if before:
                                    add_sum(n - 1, j)
                                if j == 3 and ahead >= 1:
                                    logits(n + 1, (r + 1) % RING, (r + 1) % 2, 2)
                                if ahead >= 2:
                                    op = hot((r + 2) % RING, j)
                                if j == 1 and ahead >= 1:
                                    dve.wait_ge(gather_done[(r + 1) % RING], ring_count(n, s, r))
                                    logits(n + 1, (r + 1) % RING, (r + 1) % 2, 0)
                                if j == 2 and ahead >= 1:
                                    logits(n + 1, (r + 1) % RING, (r + 1) % 2, 1)
                            if ahead >= 2:
                                op.then_inc(hot_ready, 1)

                        def ring_count(n, s, r):
                            uses = (n + 1 - (r + 1) % RING)
                            return uses * (16 * G // RING) + 16 * G

                        dve.wait_ge(table_in, c * 32 + 32)
                        for r in range(2):
                            dve.wait_ge(cols_ready, c * NGRP + r + 1)
                            for j in range(G):
                                op = hot(r, j)
                            op.then_inc(hot_ready, 1)
                        dve.wait_ge(gather_done[0], rounds * 16 * G + 16 * G)
                        for part in range(3):
                            logits(c * NGRP, 0, 0, part)
                        steps(dve, c, step)
                        dve.load(block_regs, table[0:1, 1, CH - G:CH])
                        dve.wait_ge(summed, from_one(c * NGRP + NGRP))
                        for j in range(G):
                            add_sum(c * NGRP + NGRP - 1, j)
        b1_cols = sb(whole, "b1_cols", [P, NX * KF])
        b2_sb = sb(whole, "b2_sb", [P, NX, D])
        tile_expert = sb(whole, "tile_expert", [P, UT], I32)
        slot_token = sb(whole, "slot_token", [P, UT])
        slot_read = sb(whole, "slot_read", [P, UT])
        slot_share = sb(whole, "slot_share", [P, UT])
        with ExitStack() as scope:
            w_g = sb(scope, "w_g", [P, KD, NX])
            b_g = sb(scope, "b_g", [1, NX])
            rden = sb(scope, "rden", [P, NT, HEADS])
            xn = sb(scope, "xn2", [P, UNROLL, D])
            xnT_slot = sb(scope, "xn2T_slot", [P, 2, D])
            gate = sb(scope, "gate", [P, NT, NX])
            top = sb(scope, "top", [P, NT, NX])
            top_i = sb(scope, "top_i", [P, NT, NX], U32)
            top_f = sb(scope, "top_f", [P, 2, NT])
            expert_id = sb(scope, "expert_id", [P, NX])
            row_id = sb(scope, "row_id", [P, 1])
            node_id = sb(scope, "node_id", [P, NT])
            valid = sb(scope, "valid", [P, 1])
            absent = sb(scope, "absent", [P, 1])
            b1_rows = sb(scope, "b1_rows", [NX * KF, P])
            zeros = sb(scope, "zeros", [P, D])
            share = sb(scope, "share", [P, 2, NT])
            slot_i = sb(scope, "slot_i", [P, 2, NCHOICE], I32)
            slot_at = sb(scope, "slot_at", [P, 2, NCHOICE])
            place = sb(scope, "place", [P, 2, P])
            what = sb(scope, "what", [P, 2, 2, UT])
            empty = sb(scope, "empty", [P, UT])
            tile_no = sb(scope, "tile_no", [P, UT])
            before_row = sb(scope, "before_row", [P, P])
            choice = sb(scope, "choice", [P, NCHOICE, NX])
            count = src_col[:, 0:NCHOICE * NX].rearrange("p (n e) -> p n e", e=NX)
            upto_count = dst_col[:, 0:NCHOICE * NX].rearrange("p (n e) -> p n e", e=NX)
            room = sb(scope, "room", [P, NX])
            room_i = sb(scope, "room_i", [P, NX], I32)
            tiles_upto = sb(scope, "tiles_upto", [P, NX])
            start = sb(scope, "start", [P, NX])
            slot_f = sb(scope, "slot_f", [P, NCHOICE])
            past_e = xnT_slot[:, :, :].rearrange("p a b -> p (a b)")[:, 0:UT * NX].rearrange("p (u e) -> p u e", e=NX)
            expert_f = sb(scope, "expert_f", [P, UT])
            ratio = sb(scope, "ratio", [P, NT])

            mix_slot = sb(scope, "mix_slot", [P, UNROLL, D])

            slot_ready = sem("slot_ready")
            mixed = sem("mixed")
            mix_added = sem("mix_added")
            gat_scaled = sem("gat_scaled")
            gate_in = sem("gate_in")
            ffn_bias_in = sem("ffn_bias_in")
            den_ready = sem("den_ready")
            gat_ready = sem("gat_ready")
            stats2_ready = sem("stats2_ready")
            x_step = sem("x_step")
            moments2_ready = sem("moments2_ready")
            std2_ready = sem("std2_ready")
            xn2_ready = sem("xn2_ready")
            xn2_kept = sem("xn2_kept")
            turned2 = sem("turned2")
            xn2T_ready = sem("xn2T_ready")
            gated = sem("gated")
            pool3 = sem("pool3")
            ratio_ready = sem("ratio_ready")
            exp2_ready = sem("exp2_ready")
            choice_ready = sem("choice_ready")
            b1_in = sem("b1_in")
            b1_turned = sem("b1_turned")
            xn_stored = sem("xn_stored")
            out_started = sem("out_started")
            places_ready = sem("places_ready")
            placed = sem("placed")
            zeros_ready = sem("zeros_ready")
            counted = sem("counted")
            v3 = Chain(sem("v3"))
            g3 = Chain(sem("g3"))

            with nc.Block() as block:
                @block.sync
                def _(sp):
                    sp.dma_start(w_g[:, :, :], w_gate.rearrange("(k p) e -> p k e", p=P)).then_inc(gate_in, 16)
                    sp.dma_start(b_g[:, :], b_gate.rearrange("(a e) -> a e", a=1)).then_inc(gate_in, 16)
                    sp.dma_start(b1_rows[:, :], b1.rearrange("e (k p) -> (e k) p", p=P)).then_inc(b1_in, 16)
                    sp.dma_start(b2_sb[:, :, :], b2.partition_broadcast(P)).then_inc(ffn_bias_in, 16)
                    sp.wait_ge(zeros_ready, 1)
                    sp.dma_start(out[N:N + SPARE, :], zeros[:, :]).then_inc(out_started, 16)
                    sp.wait_ge(x_step, NT // UNROLL)
                    sp.dma_start(out[0:(NT - 1) * P, :].rearrange("(t p) d -> p t d", p=P), xs[:, 0:NT - 1, :]).then_inc(out_started, 16)
                    sp.dma_start(out[(NT - 1) * P:N, :], xs[0:LAST, NT - 1, :]).then_inc(out_started, 16)
                    for i in range(NT // UNROLL):
                        sp.wait_ge(xn2_kept, from_one((i + 1) * UNROLL))
                        sp.dma_start(xn_table[i * UNROLL * P:(i + 1) * UNROLL * P, :].rearrange("(t p) d -> p t d", p=P),
                                     acc[:, i * UNROLL:(i + 1) * UNROLL, 0:D]).then_inc(xn_stored, 16)
                    sp.wait_ge(xn_stored, 16 * (NT // UNROLL))
                    sp.wait_ge(out_started, 48)

                @block.gpsimd
                def _(pool):
                    for counts in (gated, xn2T_ready, turned2, xn2_kept, mix_added):
                        pool.sem_inc(counts, 1)
                    pool.sem_inc(mixed, UNROLL)
                    pool.memset(zeros[:, :], 0.0).then_inc(zeros_ready, 1)
                    pool.iota(node_id[:, :], [[P, NT]], base=1, channel_multiplier=1,
                              allow_small_or_imprecise_dtypes=True).then_inc(pool3, 1)
                    pool.iota(expert_id[:, :], [[1, NX]], base=0, channel_multiplier=0,
                              allow_small_or_imprecise_dtypes=True).then_inc(pool3, 1)
                    pool.iota(row_id[:, :], [[0, 1]], base=N + 1, channel_multiplier=1,
                              allow_small_or_imprecise_dtypes=True).then_inc(pool3, 1)
                    pool.iota(tile_no[:, :], [[1, UT]], base=0, channel_multiplier=0,
                              allow_small_or_imprecise_dtypes=True).then_inc(pool3, 1)
                    g3.done(pool.memset(before_row[:, :], 1.0))
                    pool.wait_ge(g3.sem, g3.n)
                    pool.affine_select(out=before_row[:, :], in_=before_row[:, :], compare_op=ALU.is_ge, fill=0.0,
                                       base=-1, pattern=[[1, P]], channel_multiplier=-1).then_inc(pool3, 1)
                    pool.wait_ge(den_ready, 1)
                    pool.wait_ge(bias_in, 48)
                    for i in range(NT // UNROLL):
                        tiles = slice(i * UNROLL, (i + 1) * UNROLL)
                        sums = acc[:, tiles, 0:D].rearrange("p t (h c) -> p t h c", c=C)
                        pool.tensor_tensor(sums, sums, rden[:, tiles, :].unsqueeze(3).broadcast_to((P, UNROLL, HEADS, C)),
                                           ALU.mult).then_inc(gat_scaled, 1)
                        pool.wait_ge(gat_scaled, i + 1)
                        sums = acc[:, tiles, 0:D]
                        pool.tensor_tensor(sums, sums, gat_bias_sb[:, :].unsqueeze(1).broadcast_to((P, UNROLL, D)),
                                           ALU.add).then_inc(gat_ready, 1)
                    with pool.Fori(0, NT // UNROLL) as i:
                        for k in range(UNROLL):
                            pool.wait_ge(xn2_ready, i * UNROLL + k + 1)
                            pool.tensor_copy(flat(acc[:, bass.ds(i * UNROLL + k, 1), 0:D]), xn[:, k, :]).then_inc(xn2_kept, 1)

                @block.scalar
                def _(act):
                    with act.Fori(0, NT // UNROLL) as i:
                        for k in range(UNROLL):
                            act.wait_ge(mixed, i * UNROLL + k + 1)
                            act.activation(mix_slot[:, k, :], flat(xnT[:, bass.ds(i * UNROLL + k, 1), :]),
                                           ACT.Copy).then_inc(slot_ready, 1)
                    act.wait_ge(moments2_ready, NT)
                    act.activation(rstd[:, :], moments[:, :, 1], ACT.Sqrt, bias=eps_col[:, :]).then_inc(std2_ready, 1)
                    with act.Fori(0, NT // UNROLL) as i:
                        for k in range(UNROLL):
                            t = i * UNROLL + k
                            act.wait_ge(turned2, from_one(t + 1))
                            act.wait_ge(gated, from_one(t if k == 0 else t - 1))
                            act.activation(xnT_slot[:, k % 2, :], bank[k % 2][:, 0:D], ACT.Copy).then_inc(xn2T_ready, 1)
                    act.wait_ge(ratio_ready, 1)
                    act.activation(ratio[:, :], ratio[:, :], ACT.Exp).then_inc(exp2_ready, 1)

                @block.tensor
                def _(pe):
                    with pe.Fori(0, NT // UNROLL) as i:
                        for k in range(UNROLL):
                            t = i * UNROLL + k
                            pe.wait_ge(slot_ready, t + 1)
                            pe.wait_ge(mix_added, from_one(i * UNROLL if k < 4 else t - 3))
                            for c in range(KD):
                                pe.matmul(bank[3 + k % 4][:, 0:D], mix_slot[:, k, c * P:(c + 1) * P], w_mix[:, c, :],
                                          start=(c == 0), stop=False)
                            pe.matmul(bank[3 + k % 4][:, 0:D], ones[0:1, :], b_o[:, :], start=False, stop=True).then_inc(mixed, 1)
                    pe.wait_ge(gate_in, 32)
                    with pe.Fori(0, NT // UNROLL) as i:
                        def turn(k):
                            pe.wait_ge(xn2_ready, i * UNROLL + k + 1)
                            pe.wait_ge(xn2T_ready, from_one(i * UNROLL + (k if k == 0 else k - 1)))
                            for c in range(KD):
                                tr = pe.transpose(bank[k % 2][:, c * P:(c + 1) * P], xn[:, k, c * P:(c + 1) * P], ident[:, :])
                            tr.then_inc(turned2, 1)

                        turn(0)
                        for k in range(UNROLL):
                            t = i * UNROLL + k
                            if k + 1 < UNROLL:
                                turn(k + 1)
                            pe.wait_ge(xn2T_ready, from_one(t + 1))
                            logits = bank[7][:, bass.ds(t * NX, NX)]
                            for c in range(KD):
                                pe.matmul(logits, xnT_slot[:, k % 2, c * P:(c + 1) * P], w_g[:, c, :], start=(c == 0), stop=False)
                            pe.matmul(logits, ones[0:1, :], b_g[:, :], start=False, stop=True).then_inc(gated, 1)
                    pe.wait_ge(choice_ready, 1)
                    pe.wait_ge(b1_in, 16)
                    pe.transpose(bank[2][:, 0:NX * KF], b1_rows[:, :], ident[0:NX * KF, 0:NX * KF]).then_inc(b1_turned, 1)
                    flat_choice = choice[:, :, :].rearrange("p n e -> p (n e)")
                    pe.matmul(bank[0][:, 0:NCHOICE * NX], before_row[:, :], flat_choice, start=True, stop=True)
                    pe.matmul(bank[1][:, 0:NCHOICE * NX], ones[:, :], flat_choice, start=True, stop=True).then_inc(counted, 1)
                    for n in range(NCHOICE):
                        pe.wait_ge(places_ready, n + 1)
                        pe.matmul(bank[3][:, 0:2 * UT], place[:, n % 2, :], what[:, n % 2, :, :].rearrange("p a b -> p (a b)"),
                                  start=(n == 0), stop=(n == NCHOICE - 1)).then_inc(placed, 1)

                @block.vector
                def _(dve):
                    def after(instruction):
                        v3.done(instruction)
                        dve.wait_ge(v3.sem, v3.n)

                    dve.reciprocal(rden[:, :, :], acc[:, 0:NB, D:ROW]).then_inc(den_ready, 1)
                    with dve.Fori(0, NT // UNROLL) as i:
                        for k in range(UNROLL):
                            t = i * UNROLL + k
                            dve.wait_ge(mixed, ahead(t + 1))
                            row = flat(xs[:, bass.ds(t, 1), :])
                            dve.tensor_tensor(row, row, bank[3 + k % 4][:, 0:D], ALU.add).then_inc(mix_added, 1)
                        dve.wait_ge(gat_ready, i + 1)
                        dve.wait_ge(mix_added, from_one(i * UNROLL + UNROLL))
                        some = xs[:, bass.ds(i * UNROLL, UNROLL), :]
                        dve.scalar_tensor_tensor(out=some, in0=acc[:, bass.ds(i * UNROLL, UNROLL), 0:D], scalar=0.0, in1=some,
                                                 op0=ALU.max, op1=ALU.add).then_inc(x_step, 1)
                        dve.wait_ge(x_step, i + 1)
                        for k in range(UNROLL):
                            t = i * UNROLL + k
                            dve.bn_stats(flat(stats[:, bass.ds(t, 1), :]), flat(xs[:, bass.ds(t, 1), :])).then_inc(stats2_ready, 1)
                    dve.wait_ge(stats2_ready, NT)
                    for t in range(NT):
                        dve.bn_aggr(moments[:, t, :], stats[:, t, :]).then_inc(moments2_ready, 1)
                    dve.wait_ge(std2_ready, 1)
                    after(dve.reciprocal(rstd[:, :], rstd[:, :]))
                    with dve.Fori(0, NT // UNROLL) as i:
                        for k in range(UNROLL):
                            t = i * UNROLL + k
                            dve.wait_ge(turned2, from_one(i * UNROLL))
                            dve.wait_ge(xn2_kept, from_one(i * UNROLL))
                            dve.tensor_scalar(xn[:, k, :], flat(xs[:, bass.ds(t, 1), :]), flat(moments[:, bass.ds(t, 1), 0:1]),
                                              rstd[:, bass.ds(t, 1)], ALU.subtract, ALU.mult).then_inc(xn2_ready, 1)
                    dve.wait_ge(gated, from_one(NT))
                    after(dve.tensor_copy(gate[:, :, :], bank[7][:, 0:NT * NX].rearrange("p (t e) -> p t e", e=NX)))
                    for t in range(NT):
                        dve.max(top[:, t, :], gate[:, t, :]).then_inc(v3.sem, 1)
                    v3.n += NT
                    dve.wait_ge(v3.sem, v3.n)
                    for t in range(NT):
                        dve.max_index(top_i[:, t, :], top[:, t, :], gate[:, t, :]).then_inc(v3.sem, 1)
                    v3.n += NT
                    dve.tensor_tensor(ratio[:, :], top[:, :, 1], top[:, :, 0], ALU.subtract).then_inc(ratio_ready, 1)
                    dve.wait_ge(v3.sem, v3.n)
                    after(dve.tensor_copy(top_f[:, :, :], top_i[:, :, 0:2].rearrange("p t k -> p k t")))
                    dve.wait_ge(pool3, 5)
                    for k in range(2):
                        after(dve.tensor_tensor(choice[:, k * NT:(k + 1) * NT, :], top_f[:, k, :].unsqueeze(2).broadcast_to((P, NT, NX)),
                                                expert_id[:, :].unsqueeze(1).broadcast_to((P, NT, NX)), ALU.is_equal))
                    after(dve.tensor_scalar(valid[:, :], node_id[:, NT - 1:NT], float(N), None, ALU.is_le))
                    both = choice[:, NT - 1:NCHOICE:NT, :]
                    dve.tensor_scalar(both, both, valid[:, 0:1], None, ALU.mult).then_inc(choice_ready, 1)
                    dve.tensor_scalar(absent[:, :], valid[:, :], -float(UT * P), float(UT * P), ALU.mult, ALU.add)
                    dve.wait_ge(exp2_ready, 1)
                    after(dve.tensor_scalar(share[:, 1, :], ratio[:, :], 1.0, None, ALU.add))
                    after(dve.reciprocal(share[:, 0, :], share[:, 1, :]))
                    after(dve.tensor_tensor(share[:, 1, :], ratio[:, :], share[:, 0, :], ALU.mult))
                    dve.wait_ge(counted, 1)
                    after(dve.tensor_copy(count[:, :, :], bank[1][:, 0:NCHOICE * NX].rearrange("p (n e) -> p n e", e=NX)))
                    for e in range(NX):
                        op = dve.tensor_tensor_scan(upto_count[:, :, e], ones[:, 0:NCHOICE], count[:, :, e], 0.0, ALU.mult, ALU.add)
                    after(op)
                    after(dve.tensor_scalar(room_i[:, :], upto_count[:, NCHOICE - 1, :], float(P - 1), None, ALU.add))
                    after(dve.tensor_scalar(room_i[:, :], room_i[:, :], P.bit_length() - 1, None, ALU.arith_shift_right))
                    after(dve.tensor_copy(room[:, :], room_i[:, :]))
                    after(dve.tensor_tensor_scan(tiles_upto[:, :], ones[:, 0:NX], room[:, :], 0.0, ALU.mult, ALU.add))
                    after(dve.tensor_tensor(start[:, :], tiles_upto[:, :], room[:, :], ALU.subtract))
                    after(dve.tensor_scalar(start[:, :], start[:, :], float(P), None, ALU.mult))
                    after(dve.tensor_tensor(upto_count[:, :, :], upto_count[:, :, :], count[:, :, :], ALU.subtract))
                    after(dve.tensor_tensor(upto_count[:, :, :], upto_count[:, :, :],
                                            start[:, :].unsqueeze(1).broadcast_to((P, NCHOICE, NX)), ALU.add))
                    after(dve.tensor_tensor(upto_count[:, :, :], upto_count[:, :, :],
                                            bank[0][:, 0:NCHOICE * NX].rearrange("p (n e) -> p n e", e=NX), ALU.add))
                    after(dve.tensor_tensor(upto_count[:, :, :], upto_count[:, :, :], choice[:, :, :], ALU.mult))
                    after(dve.tensor_reduce(slot_f[:, :], upto_count[:, :, :], AX.X, ALU.add))
                    last = slot_f[:, NT - 1:NCHOICE:NT]
                    after(dve.tensor_scalar(last, last, absent[:, 0:1], None, ALU.add))
                    after(dve.tensor_copy(slot_i[:, 0, :], slot_f[:, :]))
                    after(dve.tensor_scalar(slot_i[:, 1, :], slot_i[:, 0, :], P.bit_length() - 1, None, ALU.arith_shift_right))
                    after(dve.tensor_scalar(slot_i[:, 0, :], slot_i[:, 0, :], P - 1, None, ALU.bitwise_and))
                    after(dve.tensor_copy(slot_at[:, :, :], slot_i[:, :, :]))
                    for n in range(NCHOICE):
                        if n >= 2:
                            dve.wait_ge(placed, n - 1)
                        dve.tensor_scalar(place[:, n % 2, :], iota_row[:, :], slot_at[:, 0, n:n + 1], None, ALU.is_equal)
                        dve.tensor_scalar(what[:, n % 2, 0, :], tile_no[:, :], slot_at[:, 1, n:n + 1],
                                          node_id[:, n % NT:n % NT + 1], ALU.is_equal, ALU.mult)
                        dve.tensor_scalar(what[:, n % 2, 1, :], tile_no[:, :], slot_at[:, 1, n:n + 1],
                                          share[:, n // NT, n % NT:n % NT + 1], ALU.is_equal, ALU.mult).then_inc(places_ready, 1)
                    grid = (P, UT, NX)
                    after(dve.tensor_tensor(past_e[:, :, :], tile_no[:, :].unsqueeze(2).broadcast_to(grid),
                                            tiles_upto[:, :].unsqueeze(1).broadcast_to(grid), ALU.is_ge))
                    after(dve.tensor_reduce(expert_f[:, :], past_e[:, :, :], AX.X, ALU.add))
                    after(dve.tensor_scalar(expert_f[:, :], expert_f[:, :], float(NX - 1), None, ALU.min))
                    after(dve.tensor_copy(tile_expert[:, :], expert_f[:, :]))
                    dve.wait_ge(b1_turned, 1)
                    dve.tensor_copy(b1_cols[:, :], bank[2][:, 0:NX * KF])
                    dve.wait_ge(placed, NCHOICE)
                    after(dve.tensor_copy(slot_token[:, :], bank[3][:, 0:UT]))
                    dve.tensor_copy(slot_share[:, :], bank[3][:, UT:2 * UT])
                    after(dve.tensor_scalar(empty[:, :], slot_token[:, :], 0.0, None, ALU.is_equal))
                    after(dve.tensor_scalar(empty[:, :], empty[:, :], row_id[:, 0:1], -1.0, ALU.mult, ALU.add))
                    after(dve.tensor_tensor(slot_token[:, :], slot_token[:, :], empty[:, :], ALU.add))
                    after(dve.tensor_scalar(slot_read[:, :], slot_token[:, :], float(N - 1), None, ALU.min))

        with ExitStack() as scope:
            w1_slot = sb(scope, "w1_slot", [P, 2, KD, FF])
            xg = sb(scope, "xg", [P, 2, D])
            xgT = sb(scope, "xgT", [P, 2, D])
            hiddenT = sb(scope, "hiddenT", [P, 2, FF])
            y = sb(scope, "y", [P, 2, D])
            b1_slot = sb(scope, "b1_slot", [P, 2, KF])
            read_index = sb(scope, "read_index", [P, 2], U32)
            add_index = sb(scope, "add_index", [P, 2], U32)

            w1_in = [sem(f"w1_in{k}") for k in range(2)]
            xg_in = [sem(f"xg_in{k}") for k in range(2)]
            read_ready = sem("read_ready")
            xg_turned = sem("xg_turned")
            xgT_ready = sem("xgT_ready")
            b1_ready = sem("b1_ready")
            hidden_summed = sem("hidden_summed")
            hidden_ready = sem("hidden_ready")
            y_summed = sem("y_summed")
            y_biased = sem("y_biased")
            y_ready = sem("y_ready")
            y_added = sem("y_added")

            def tiles(eng, step):
                rounds = UT // 2
                for u in range(2):
                    step(u, u, 9)
                with eng.Fori(1, rounds - 2) as i:
                    for k in range(2):
                        step(i * 2 + k, k, 9)
                for u in range(UT - 4, UT):
                    step(u, u % 2, UT - 1 - u)

            def uses(u, k):
                return u // 2 + 1 if isinstance(u, int) else (u - k) // 2 + 1

            with nc.Block() as block:
                @block.sync
                def _(sp):
                    def load(u, k):
                        e = sp.value_load(tile_expert[0:1, bass.ds(u, 1)], min_val=0, max_val=NX - 1)
                        return w1[bass.ds(e, 1), :, :].rearrange("a (k p) f -> p (a k) f", p=P)

                    for u in range(2):
                        sp.dma_start(w1_slot[:, u, :, :], load(u, u)).then_inc(w1_in[u], 16)

                    def step(u, k, ahead):
                        if ahead >= 2:
                            rows = load(u + 2, k)
                            sp.wait_ge(hidden_summed, 2 * u + 2)
                            sp.dma_start(w1_slot[:, k, :, :], rows).then_inc(w1_in[k], 16)

                    tiles(sp, step)

                @block.gpsimd
                def _(pool):
                    def read(u, k):
                        pool.wait_ge(read_ready, u + 1)
                        pool.sem_inc(waited, 1)
                        pool.indirect_dma_start(xg[:, k, :], None, xn_table,
                                                bass.IndirectOffsetOnAxis(ap=read_index[:, k:k + 1], axis=0)).then_inc(xg_in[k], 16)

                    def step(u, k, ahead):
                        if ahead >= 3:
                            read(u + 3, 1 - k)
                        if not isinstance(u, int) or u > 0:
                            pool.wait_ge(y_added, u * 16)
                            pool.sem_inc(waited, 1)
                        pool.wait_ge(y_ready, u + 1)
                        pool.sem_inc(waited, 1)
                        pool.indirect_dma_start(out, bass.IndirectOffsetOnAxis(ap=add_index[:, k:k + 1], axis=0),
                                                y[:, k, :], None, compute_op=ALU.add).then_inc(y_added, 16)

                    read(0, 0)
                    read(1, 1)
                    read(2, 0)
                    tiles(pool, step)
                    pool.wait_ge(y_added, UT * 16)

                @block.scalar
                def _(act):
                    def turned_in(u, k):
                        act.wait_ge(xg_turned, u + 1)
                        act.activation(xgT[:, k, :], bank[0][:, 0:D], ACT.Copy).then_inc(xgT_ready, 1)

                    def gelu(u, k):
                        act.wait_ge(b1_ready, u + 1)
                        for half in range(2):
                            act.wait_ge(hidden_summed, 2 * u + half + 1)
                            for f in range(KF // 2):
                                g = half * (KF // 2) + f
                                op = act.activation(hiddenT[:, k, g * P:(g + 1) * P], bank[1 + 2 * k + half][:, f * P:(f + 1) * P],
                                                    ACT.Gelu, bias=b1_slot[:, k, g:g + 1])
                            op.then_inc(hidden_ready, 1)

                    def step(u, k, ahead):
                        if ahead >= 1:
                            gelu(u + 1, 1 - k)
                        if ahead >= 2:
                            turned_in(u + 2, k)

                    turned_in(0, 0)
                    turned_in(1, 1)
                    gelu(0, 0)
                    tiles(act, step)

                @block.tensor
                def _(pe):
                    pe.wait_ge(w2_in, 16 * NX)

                    def turn_in(u, k):
                        if not isinstance(u, int) or u > 0:
                            pe.wait_ge(xgT_ready, u)
                        pe.wait_ge(xg_in[k], uses(u, k) * 16)
                        for c in range(KD):
                            tr = pe.transpose(bank[0][:, c * P:(c + 1) * P], xg[:, k, c * P:(c + 1) * P], ident[:, :])
                        tr.then_inc(xg_turned, 1)

                    def widen(u, k):
                        pe.wait_ge(xgT_ready, u + 1)
                        pe.wait_ge(w1_in[k], uses(u, k) * 16)
                        for f in range(KF):
                            for c in range(KD):
                                mm = pe.matmul(bank[1 + 2 * k + f // 4][:, f % 4 * P:(f % 4 + 1) * P],
                                               w1_slot[:, k, c, f * P:(f + 1) * P], xgT[:, k, c * P:(c + 1) * P],
                                               start=(c == 0), stop=(c == KD - 1))
                            if f % 4 == 3:
                                mm.then_inc(hidden_summed, 1)

                    def step(u, k, ahead):
                        e = pe.value_load(tile_expert[0:1, bass.ds(u, 1)], min_val=0, max_val=NX - 1)
                        if ahead >= 1:
                            widen(u + 1, 1 - k)
                        if ahead >= 2:
                            turn_in(u + 2, k)
                        for f in range(KF):
                            if f % 4 == 0:
                                pe.wait_ge(hidden_ready, 2 * u + f // 4 + 1)
                            if f == 0 and (not isinstance(u, int) or u >= 2):
                                pe.wait_ge(y_biased, u - 1)
                            mm = pe.matmul(bank[5 + k][:, 0:D], hiddenT[:, k, f * P:(f + 1) * P],
                                           flat(w2_sb[:, bass.ds(e * KF + f, 1), :]), start=(f == 0), stop=(f == KF - 1))
                        mm.then_inc(y_summed, 1)

                    turn_in(0, 0)
                    turn_in(1, 1)
                    widen(0, 0)
                    tiles(pe, step)

                @block.vector
                def _(dve):
                    def index(u, k):
                        if not isinstance(u, int) or u >= 2:
                            dve.wait_ge(xg_turned, u - 1)
                        dve.tensor_copy(read_index[:, k:k + 1], slot_read[:, bass.ds(u, 1)]).then_inc(read_ready, 1)

                    def biases(u, k):
                        e = dve.value_load(tile_expert[0:1, bass.ds(u, 1)], min_val=0, max_val=NX - 1)
                        if not isinstance(u, int) or u >= 2:
                            dve.wait_ge(hidden_ready, 2 * u - 2)
                        dve.tensor_copy(b1_slot[:, k, :], b1_cols[:, bass.ds(e * KF, KF)]).then_inc(b1_ready, 1)

                    def step(u, k, ahead):
                        if ahead >= 3:
                            index(u + 3, 1 - k)
                        if ahead >= 2:
                            biases(u + 2, k)
                        e = dve.value_load(tile_expert[0:1, bass.ds(u, 1)], min_val=0, max_val=NX - 1)
                        dve.wait_ge(y_summed, u + 1)
                        if not isinstance(u, int) or u >= 2:
                            dve.wait_ge(y_added, (u - 1) * 16)
                        dve.tensor_copy(add_index[:, k:k + 1], slot_token[:, bass.ds(u, 1)])
                        dve.tensor_tensor(y[:, k, :], bank[5 + k][:, 0:D], flat(b2_sb[:, bass.ds(e, 1), :]), ALU.add).then_inc(y_biased, 1)
                        dve.wait_ge(y_biased, u + 1)
                        dve.tensor_scalar(y[:, k, :], y[:, k, :], slot_share[:, bass.ds(u, 1)], None, ALU.mult).then_inc(y_ready, 1)

                    for u in range(2):
                        index(u, u)
                        biases(u, u)
                    index(2, 0)
                    tiles(dve, step)


_INS = ['x', 'src', 'dst', 'L0_gnn_W', 'L0_gnn_att_src', 'L0_gnn_att_dst', 'L0_gnn_bias', 'L0_mix_W_qkv', 'L0_mix_W_out',
        'L0_mix_b_out', 'L0_ffn_Wg', 'L0_ffn_bg', 'L0_ffn_W1', 'L0_ffn_b1', 'L0_ffn_W2', 'L0_ffn_b2']


def kernel(**inputs):
    import numpy as np
    import concourse.bacc as bacc
    from concourse.bass_utils import run_bass_kernel_spmd

    nc = bacc.Bacc("TRN2", target_bir_lowering=False, num_devices=1)
    arrays, args = {}, []
    for name in _INS:
        a = np.ascontiguousarray(inputs[name])
        arrays[f"in_{name}"] = a
        args.append(nc.dram_tensor(f"in_{name}", a.shape, mybir.dt.from_np(a.dtype), kind="ExternalInput").ap())
    out = nc.dram_tensor("out", (N + SPARE, D), F32, kind="ExternalOutput").ap()
    graph_layer(nc, *args, out)
    result = run_bass_kernel_spmd(nc, [arrays], core_ids=[0])
    return result.results[0]["out"][:N]
```

```python
from contextlib import ExitStack

import concourse.bass as bass
from concourse import mybir

F32 = mybir.dt.float32
I32 = mybir.dt.int32
U32 = mybir.dt.uint32
ALU = mybir.AluOpType
ACT = mybir.ActivationFunctionType
AX = mybir.AxisListType

P = 128
N = 3125
D = 256
NT = -(-N // P)
NPAD = NT * P
LAST = N - (NT - 1) * P
KD = D // P
HEADS = 4
C = D // HEADS
ROW = D + HEADS
HID = 128
DH = HID // HEADS
E = 53125
ET = -(-E // P)
EQ = ET // 4
NB = NT
BIG = 16384.0
CH = 448
G = 4
RING = 8
LEAD = 4
NGRP = CH // G
MAXCHUNK = -(-(ET * NB) // CH)
VCOL = 84
NX = 8
FF = 1024
KF = FF // P
NCHOICE = 2 * NT
UT = (2 * N + NX * (P - 1)) // P
MINPAIRS = -(-2 * N // (2 * P))
SPARE = P
UNROLL = 5
NR = NT // UNROLL
CONSTS = 6
EPS = 1e-5
SLOPE = 0.2
QSCALE = float(DH) ** -0.5

assert UT % 2 == 0 and ET % 4 == 0 and NT % UNROLL == 0 and P * VCOL >= MAXCHUNK * CH and NGRP % RING == 0 and EQ <= P


def flat(ap):
    return ap.rearrange("p a b -> p (a b)")


def ahead(n):
    return n + UNROLL


def from_one(n):
    return n + 1


class Chain:

    def __init__(self, sem):
        self.sem, self.n = sem, 0

    def done(self, instruction):
        self.n += 1
        instruction.then_inc(self.sem, 1)


def graph_layer(nc, x, src, dst, w_gat, att_src, att_dst, gat_bias, w_qkv, w_out, b_out,
                w_gate, b_gate, w1, b1, w2, b2, out):
    h_table = nc.dram_tensor("h_table", (NPAD, ROW), F32, kind="Internal").ap()
    visit_tile = nc.dram_tensor("visit_tile", (P * VCOL,), I32, kind="Internal").ap()
    visit_block = nc.dram_tensor("visit_block", (P * VCOL,), I32, kind="Internal").ap()
    xn_table = nc.dram_tensor("xn_table", (NPAD, D), F32, kind="Internal").ap()

    with ExitStack() as whole:
        def sem(name):
            return whole.enter_context(nc.semaphore(name))

        def sb(scope, name, shape, dtype=F32):
            return scope.enter_context(nc.sbuf_tensor(name, shape, dtype))

        bank = [whole.enter_context(nc.psum_tensor(f"bank{k}", [P, 512], F32)) for k in range(8)]

        ident = sb(whole, "ident", [P, P])
        ones = sb(whole, "ones", [P, P])
        xs = sb(whole, "xs", [P, NT, D])
        acc = sb(whole, "acc", [P, NB + 1, ROW])
        stats = sb(whole, "stats", [P, NT, 6])
        moments = sb(whole, "moments", [P, NT, 2])
        rstd = sb(whole, "rstd", [P, NT])
        gat_bias_sb = sb(whole, "gat_bias_sb", [P, D])
        iota_row = sb(whole, "iota_row", [P, P])
        adc = sb(whole, "adc", [P, NB + 1, 2 * HEADS])
        src_col = sb(whole, "src_col", [P, ET])
        dst_col = sb(whole, "dst_col", [P, ET])
        minus_base = sb(whole, "minus_base", [P, NB + 1])
        chunks_i = sb(whole, "chunks_i", [1, 1], I32)
        eps_col = sb(whole, "eps_col", [P, 1])
        xnT = sb(whole, "xnT", [P, NT, D])
        w_mix = sb(whole, "w_mix", [P, KD, D])

        weights_in = sem("weights_in")
        bias_in = sem("bias_in")
        self_ready = sem("self_ready")
        waited = sem("waited")

        with ExitStack() as early:
            hs = sb(early, "hs", [P, NT, D + 2 * HEADS])
            kv = sb(early, "kv", [P, NT, 2 * HID + 1])
            w_h = sb(early, "w_h", [P, KD, D + 2 * HEADS])
            w_kv = sb(early, "w_kv", [P, KD, 2 * HID])
            w_q = sb(early, "w_q", [P, KD, HID])
            w_o = sb(early, "w_o", [P, D])
            tile_min = sb(early, "tile_min", [EQ, 4])
            tile_max = sb(early, "tile_max", [EQ, 4])
            with ExitStack() as scope:
                xn = sb(scope, "xn", [P, UNROLL, D])
                xnT_slot = sb(scope, "xnT_slot", [P, UNROLL, D])
                att = sb(scope, "att", [P, 2, D])
                att_w = sb(scope, "att_w", [P, KD, D])
                b_o = sb(scope, "b_o", [P, D])
                edge_i = sb(scope, "edge_i", [EQ, 2, 4 * P], I32)
                edge_f = sb(scope, "edge_f", [EQ, 2, 4 * P])

                block_lo = sb(scope, "block_lo", [P, NB])
                tile_id = sb(scope, "tile_id", [P, 4])
                has = sb(scope, "has", [EQ, 4, NB])
                has2 = sb(scope, "has2", [EQ, 4, NB])
                first_q = sb(scope, "first_q", [EQ, NB])
                last_q = sb(scope, "last_q", [EQ, NB])
                span = sb(scope, "span", [NB, 4])
                upto = sb(scope, "upto", [P, P])
                span_rows = sb(scope, "span_rows", [NB, 3 * NB])
                rows = sb(scope, "rows", [P, 3 * NB])
                visit_id = sb(scope, "visit_id", [P, VCOL])
                past = sb(scope, "past", [P, VCOL, NB])
                within = sb(scope, "within", [P, VCOL, NB])
                from_visit = sb(scope, "from_visit", [P, NB + 1])
                change = sb(scope, "change", [P, NB])
                vb = sb(scope, "vb", [P, VCOL])
                vt = sb(scope, "vt", [P, VCOL])
                vb_i = sb(scope, "vb_i", [P, VCOL], I32)
                vt_i = sb(scope, "vt_i", [P, VCOL], I32)
                chunk_sum = sb(scope, "chunk_sum", [1, 1])
                chunk_lo = sb(scope, "chunk_lo", [1, MAXCHUNK])

                visit_consts = sem("visit_consts")
                spans_ready = sem("spans_ready")
                spans_turned = sem("spans_turned")
                rows_ready = sem("rows_ready")
                rows_spread = sem("rows_spread")
                visits_ready = sem("visits_ready")
                visits_stored = sem("visits_stored")
                x_in = [sem(f"x_in{k}") for k in range(3)]
                edges_in = sem("edges_in")
                x_padded = sem("x_padded")
                edges_padded = sem("edges_padded")
                consts = sem("consts")
                stats_ready = sem("stats_ready")
                std_ready = sem("std_ready")
                rstd_ready = sem("rstd_ready")
                x_biased = sem("x_biased")
                w_ready = sem("w_ready")
                xn_ready = sem("xn_ready")
                turned = sem("turned")
                xnT_kept = sem("xnT_kept")
                moments_ready = sem("moments_ready")
                xnT_ready = sem("xnT_ready")
                projected = sem("projected")
                h_copied = sem("h_copied")
                kv_copied = sem("kv_copied")
                h_stored = sem("h_stored")
                edges_f = sem("edges_f")
                edges_turned = sem("edges_turned")
                edges_done = sem("edges_done")
                v1 = Chain(sem("v1"))
                g1 = Chain(sem("g1"))

                PAIRS = ((3, 4), (5, 6), (2, 7), (3, 4), (5, 6))

                def rounds(eng, step, before=None, after_last=None):
                    def one(i, last=False):
                        if before:
                            before(i)
                        for k in range(UNROLL):
                            step(i, k, last)
                            if last and after_last:
                                after_last(k)

                    one(0)
                    if before:
                        before(1)
                    with eng.Fori(1, NR - 2) as i:
                        for k in range(UNROLL):
                            step(i, k, False)
                    one(NR - 2)
                    one(NR - 1, True)

                with nc.Block() as block:
                    @block.sync
                    def _(sp):
                        rows = x[0:(NT - 1) * P, :].rearrange("(t p) d -> p t d", p=P)
                        sp.dma_start(xs[:, 0:UNROLL, :], rows[:, 0:UNROLL, :]).then_inc(x_in[0], 16)
                        sp.wait_ge(edges_padded, 2)
                        full = E // (4 * P)
                        for j, edge in ((0, src), (1, dst)):
                            sp.dma_start(edge_i[0:full, j, :],
                                         edge[0:full * 4 * P].rearrange("(q e) -> q e", e=4 * P)).then_inc(edges_in, 16)
                            sp.dma_start(edge_i[full:full + 1, j, 0:E - full * 4 * P],
                                         edge[full * 4 * P:E].rearrange("(q e) -> q e", q=1)).then_inc(edges_in, 16)
                        sp.dma_start(xs[:, UNROLL:NT - 1, :], rows[:, UNROLL:, :]).then_inc(x_in[1], 16)
                        sp.wait_ge(x_padded, 1)
                        sp.dma_start(xs[0:LAST, NT - 1, :], x[(NT - 1) * P:N, :]).then_inc(x_in[2], 16)
                        with sp.Fori(0, NT) as t:
                            sp.wait_ge(h_copied, ahead(t + 1))
                            sp.dma_start(h_table.rearrange("(t p) r -> p t r", p=P)[:, bass.ds(t, 1), :],
                                         hs[:, bass.ds(t, 1), 0:ROW]).then_inc(h_stored, 16)
                        sp.wait_ge(visits_ready, 2)
                        sp.dma_start(visit_tile.rearrange("(p c) -> p c", c=VCOL), vt_i[:, :]).then_inc(visits_stored, 16)
                        sp.dma_start(visit_block.rearrange("(p c) -> p c", c=VCOL), vb_i[:, :]).then_inc(visits_stored, 16)
                        sp.wait_ge(visits_stored, 32)
                        sp.wait_ge(h_stored, 16 * NT)

                    @block.gpsimd
                    def _(pool):
                        for counts in (xnT_kept, h_copied, kv_copied, turned, projected):
                            pool.sem_inc(counts, UNROLL)
                        pool.memset(edge_i[:, 0, :], 0).then_inc(edges_padded, 1)
                        pool.memset(edge_i[:, 1, :], 4095).then_inc(edges_padded, 1)
                        pool.memset(xs[:, NT - 1, :], 0.0).then_inc(x_padded, 1)
                        g1.done(pool.memset(ident[:, :], 0.0))
                        pool.wait_ge(g1.sem, g1.n)
                        pool.affine_select(out=ident[:, :], in_=ident[:, :], compare_op=ALU.not_equal, fill=1.0,
                                           base=0, pattern=[[-1, P]], channel_multiplier=1).then_inc(consts, 1)
                        pool.memset(ones[:, :], 1.0).then_inc(consts, 1)
                        pool.memset(eps_col[:, :], EPS).then_inc(consts, 1)
                        pool.iota(iota_row[:, :], [[1, P]], base=0, channel_multiplier=0,
                                  allow_small_or_imprecise_dtypes=True).then_inc(consts, 1)
                        pool.iota(minus_base[:, :], [[-P, NB + 1]], base=0, channel_multiplier=0,
                                  allow_small_or_imprecise_dtypes=True).then_inc(consts, 1)
                        pool.memset(kv[:, :, 2 * HID:2 * HID + 1], 1.0).then_inc(consts, 1)
                        pool.iota(block_lo[:, :], [[P, NB]], base=0, channel_multiplier=0,
                                  allow_small_or_imprecise_dtypes=True).then_inc(visit_consts, 1)
                        pool.iota(tile_id[:, :], [[1, 4]], base=0, channel_multiplier=4,
                                  allow_small_or_imprecise_dtypes=True).then_inc(visit_consts, 1)
                        pool.iota(visit_id[:, :], [[1, VCOL]], base=0, channel_multiplier=VCOL,
                                  allow_small_or_imprecise_dtypes=True).then_inc(visit_consts, 1)
                        pool.iota(chunk_lo[:, :], [[CH, MAXCHUNK]], base=0, channel_multiplier=0,
                                  allow_small_or_imprecise_dtypes=True).then_inc(visit_consts, 1)
                        g1.done(pool.memset(upto[:, :], 1.0))
                        pool.wait_ge(g1.sem, g1.n)
                        pool.affine_select(out=upto[:, :], in_=upto[:, :], compare_op=ALU.is_ge, fill=0.0,
                                           base=0, pattern=[[1, P]], channel_multiplier=-1).then_inc(visit_consts, 1)
                        pool.memset(from_visit[:, NB:NB + 1], 0.0).then_inc(visit_consts, 1)
                        pool.wait_ge(bias_in, 48)
                        for i in range(NR):
                            pool.wait_ge(xn_ready, (i + 1) * UNROLL)
                            some = xs[:, i * UNROLL:(i + 1) * UNROLL, :]
                            pool.tensor_tensor(some, some, b_o[:, :].unsqueeze(1).broadcast_to((P, UNROLL, D)),
                                               ALU.add).then_inc(x_biased, 1)
                        pool.wait_ge(x_biased, NR)

                    @block.scalar
                    def _(act):
                        act.dma_start(w_h[:, :, 0:D], w_gat.rearrange("(k p) n -> p k n", p=P)).then_inc(weights_in, 16)
                        act.dma_start(w_q[:, :, :], w_qkv[:, 0:HID].rearrange("(k p) n -> p k n", p=P)).then_inc(weights_in, 16)
                        act.dma_start(w_kv[:, :, :], w_qkv[:, HID:3 * HID].rearrange("(k p) n -> p k n", p=P)).then_inc(weights_in, 16)
                        act.dma_start(att[:, 0, :], att_src.rearrange("h c -> (h c)").partition_broadcast(P)).then_inc(weights_in, 16)
                        act.dma_start(att[:, 1, :], att_dst.rearrange("h c -> (h c)").partition_broadcast(P)).then_inc(weights_in, 16)
                        act.dma_start(w_o[:, :], w_out).then_inc(bias_in, 16)
                        act.dma_start(b_o[:, :], b_out.partition_broadcast(P)).then_inc(bias_in, 16)
                        act.dma_start(gat_bias_sb[:, :], gat_bias.partition_broadcast(P)).then_inc(bias_in, 16)
                        act.wait_ge(consts, CONSTS)

                        def deviations(i):
                            act.wait_ge(moments_ready, i * UNROLL + UNROLL)
                            act.activation(rstd[:, 0:UNROLL], moments[:, 0:UNROLL, 1], ACT.Sqrt, bias=eps_col[:, :]).then_inc(std_ready, 1)

                        def keep(t, k):
                            act.wait_ge(turned, ahead(t + 1))
                            rows_T = bank[k % 2][:, 0:D]
                            act.activation(xnT_slot[:, k, :], rows_T, ACT.Copy).then_inc(xnT_ready, 1)
                            act.activation(flat(xnT[:, bass.ds(t, 1), :]), rows_T, ACT.Copy).then_inc(xnT_kept, 1)

                        def step(i, k, last):
                            t = i * UNROLL + k
                            if not (last and k == UNROLL - 1):
                                keep(t + 1, (k + 1) % UNROLL)
                            act.wait_ge(projected, ahead(t + 1))
                            act.activation(flat(kv[:, bass.ds(t, 1), 0:2 * HID]), bank[PAIRS[k][1]][:, 0:2 * HID],
                                           ACT.Copy).then_inc(kv_copied, 1)
                            if k == 2 and not last:
                                deviations(i + 1)

                        deviations(0)
                        keep(0, 0)
                        rounds(act, step)

                    @block.tensor
                    def _(pe):
                        pe.wait_ge(consts, CONSTS)
                        pe.wait_ge(edges_f, 2)
                        for j in range(2):
                            for q in range(4):
                                tr = pe.transpose(bank[j][:, q * EQ:(q + 1) * EQ], edge_f[:, j, q * P:(q + 1) * P],
                                                  ident[0:EQ, 0:EQ])
                            tr.then_inc(edges_turned, 1)

                        def turn(t, k):
                            pe.wait_ge(xn_ready, t + 1)
                            pe.wait_ge(xnT_kept, ahead(t if k == 0 else t - 1))
                            for c in range(KD):
                                tr = pe.transpose(bank[k % 2][:, c * P:(c + 1) * P],
                                                  xn[:, k, c * P:(c + 1) * P], ident[:, :])
                            tr.then_inc(turned, 1)

                        def step(i, k, last):
                            t = i * UNROLL + k
                            if not (last and k == UNROLL - 1):
                                turn(t + 1, (k + 1) % UNROLL)
                            pe.wait_ge(xnT_ready, t + 1)
                            pe.wait_ge(h_copied, ahead(t - 1))
                            pe.wait_ge(kv_copied, ahead(t - 1))
                            for c in range(KD):
                                pe.matmul(bank[PAIRS[k][0]][:, 0:D + 2 * HEADS], xnT_slot[:, k, c * P:(c + 1) * P],
                                          w_h[:, c, :], start=(c == 0), stop=(c == KD - 1))
                            for c in range(KD):
                                mm = pe.matmul(bank[PAIRS[k][1]][:, 0:2 * HID], xnT_slot[:, k, c * P:(c + 1) * P],
                                               w_kv[:, c, :], start=(c == 0), stop=(c == KD - 1))
                            mm.then_inc(projected, 1)

                        def before(i):
                            if i == 3:
                                pe.wait_ge(h_copied, ahead(3 * UNROLL - 2))
                                pe.wait_ge(spans_ready, 1)
                                pe.transpose(bank[2][0:NB, 0:EQ], first_q[:, :], ident[0:EQ, 0:EQ])
                                pe.transpose(bank[2][0:NB, P:P + EQ], last_q[:, :], ident[0:EQ, 0:EQ]).then_inc(spans_turned, 1)
                            if i == 4:
                                pe.wait_ge(h_copied, ahead(4 * UNROLL - 2))
                                pe.wait_ge(rows_ready, 1)
                                pe.matmul(bank[2][:, 0:3 * NB], ones[0:NB, :], span_rows[:, :], start=True, stop=True).then_inc(rows_spread, 1)

                        pe.wait_ge(edges_done, 4)
                        turn(0, 0)
                        pe.wait_ge(w_ready, 1)
                        rounds(pe, step, before)

                    @block.vector
                    def _(dve):

                        def statistics(i, k):
                            dve.bn_stats(stats[:, k, :], flat(xs[:, bass.ds(i * UNROLL + k, 1), :])).then_inc(stats_ready, 1)

                        def averages(i):
                            dve.wait_ge(stats_ready, i * UNROLL + UNROLL)
                            if not isinstance(i, int) or i > 0:
                                dve.wait_ge(xn_ready, i * UNROLL)
                                dve.sem_inc(waited, 1)
                            for k in range(UNROLL):
                                dve.bn_aggr(moments[:, k, :], stats[:, k, :]).then_inc(moments_ready, 1)

                        def invert(i):
                            dve.wait_ge(std_ready, i + 1)
                            dve.reciprocal(rstd[:, 0:UNROLL], rstd[:, 0:UNROLL]).then_inc(rstd_ready, 1)
                            dve.wait_ge(rstd_ready, i + 1)

                        def normalise(t, k):
                            dve.wait_ge(turned, ahead(t + 1 - UNROLL))
                            dve.tensor_scalar(xn[:, k, :], flat(xs[:, bass.ds(t, 1), :]), moments[:, k, 0:1],
                                              rstd[:, k:k + 1], ALU.subtract, ALU.mult).then_inc(xn_ready, 1)

                        dve.wait_ge(x_in[0], 16)
                        for k in range(UNROLL):
                            statistics(0, k)
                        averages(0)
                        dve.wait_ge(edges_in, 64)
                        for j in range(2):
                            dve.tensor_copy(edge_f[:, j, :], edge_i[:, j, :]).then_inc(edges_f, 1)
                        dve.wait_ge(edges_f, 2)
                        by_tile = edge_f[:, 1, :].rearrange("q (k e) -> q k e", e=P)
                        dve.tensor_reduce(tile_min[:, :], by_tile, AX.X, ALU.min).then_inc(edges_done, 1)
                        dve.tensor_reduce(tile_max[:, :], by_tile, AX.X, ALU.max).then_inc(edges_done, 1)
                        for j, column in ((0, src_col), (1, dst_col)):
                            dve.wait_ge(edges_turned, j + 1)
                            dve.tensor_copy(column[:, :].rearrange("p (q k) -> p k q", k=4),
                                            bank[j][:, 0:4 * EQ].rearrange("p (k q) -> p k q", k=4)).then_inc(edges_done, 1)
                        invert(0)
                        normalise(0, 0)
                        normalise(1, 1)
                        dve.wait_ge(weights_in, 80)
                        for j in range(2):
                            if j:
                                dve.wait_ge(v1.sem, v1.n)
                            v1.done(dve.tensor_tensor(att_w[:, :, :], w_h[:, :, 0:D],
                                                      att[:, j:j + 1, :].broadcast_to((P, KD, D)), ALU.mult))
                            dve.wait_ge(v1.sem, v1.n)
                            v1.done(dve.tensor_reduce(w_h[:, :, D + j * HEADS:D + (j + 1) * HEADS],
                                                      att_w[:, :, :].rearrange("p k (h c) -> p k h c", c=C), AX.X, ALU.add))
                        dve.wait_ge(v1.sem, v1.n)
                        dve.sem_inc(w_ready, 1)
                        dve.wait_ge(x_in[1], 16)
                        dve.wait_ge(x_in[2], 16)

                        def step(i, k, last):
                            t = i * UNROLL + k
                            if not last and k == UNROLL - 2:
                                invert(i + 1)
                            if not (last and k >= UNROLL - 2):
                                normalise(t + 2, (k + 2) % UNROLL)
                            if not last:
                                for n in {0: (0, 1), 1: (2, 3), 2: (4,)}.get(k, ()):
                                    statistics(i + 1, n)
                                if k == 2:
                                    averages(i + 1)
                            dve.wait_ge(projected, ahead(t + 1))
                            dve.tensor_copy(flat(hs[:, bass.ds(t, 1), :]), bank[PAIRS[k][0]][:, 0:D + 2 * HEADS]).then_inc(h_copied, 1)

                        upto_b, of_b, first_b = rows[:, 0:NB], rows[:, NB:2 * NB], rows[:, 2 * NB:3 * NB]
                        grid = (P, VCOL, NB)
                        ids = visit_id[:, :].unsqueeze(2).broadcast_to(grid)

                        def after(instruction):
                            v1.done(instruction)
                            dve.wait_ge(v1.sem, v1.n)

                        def before(i):
                            if i == 1:
                                dve.wait_ge(visit_consts, 6)
                                wide = (EQ, 4, NB)
                                blocks = block_lo[0:EQ, :].unsqueeze(1).broadcast_to(wide)
                                after(dve.tensor_scalar(tile_min[:, :], tile_min[:, :], -float(P - 1), None, ALU.add))
                                dve.tensor_tensor(has[:, :, :], blocks, tile_min[:, :].unsqueeze(2).broadcast_to(wide), ALU.is_ge)
                                after(dve.tensor_tensor(has2[:, :, :], blocks, tile_max[:, :].unsqueeze(2).broadcast_to(wide), ALU.is_le))
                                after(dve.tensor_tensor(has[:, :, :], has[:, :, :], has2[:, :, :], ALU.mult))
                                after(dve.tensor_scalar(tile_id[:, :], tile_id[:, :], 1.0, None, ALU.add))
                                after(dve.tensor_tensor(has2[:, :, :], has[:, :, :], tile_id[0:EQ, :].unsqueeze(2).broadcast_to(wide), ALU.mult))
                                dve.tensor_reduce(last_q[:, :], has2[:, :, :].rearrange("q k b -> q b k"), AX.X, ALU.max)
                                after(dve.tensor_scalar(has[:, :, :], has[:, :, :], -BIG, BIG - 1.0, ALU.mult, ALU.add))
                                after(dve.tensor_tensor(has2[:, :, :], has[:, :, :], tile_id[0:EQ, :].unsqueeze(2).broadcast_to(wide), ALU.add))
                                dve.tensor_reduce(first_q[:, :], has2[:, :, :].rearrange("q k b -> q b k"), AX.X, ALU.min).then_inc(spans_ready, 1)
                            if i == 3:
                                dve.wait_ge(spans_turned, 1)
                                after(dve.tensor_reduce(span[:, 0:1], bank[2][0:NB, 0:EQ], AX.X, ALU.min))
                                after(dve.tensor_reduce(span[:, 1:2], bank[2][0:NB, P:P + EQ], AX.X, ALU.max))
                                after(dve.tensor_tensor(span[:, 2:3], span[:, 1:2], span[:, 0:1], ALU.subtract))
                                after(dve.tensor_scalar(span[:, 3:4], span[:, 2:3], 0.0, None, ALU.max))
                                dve.tensor_scalar(span_rows[:, 0:NB], upto[0:NB, 0:NB], span[:, 3:4], None, ALU.mult)
                                dve.tensor_scalar(span_rows[:, NB:2 * NB], ident[0:NB, 0:NB], span[:, 3:4], None, ALU.mult)
                                dve.tensor_scalar(span_rows[:, 2 * NB:3 * NB], ident[0:NB, 0:NB], span[:, 0:1], None, ALU.mult).then_inc(rows_ready, 1)
                            if i == 4:
                                dve.wait_ge(rows_spread, 1)
                                after(dve.tensor_copy(rows[:, :], bank[2][:, 0:3 * NB]))
                                after(dve.tensor_scalar(chunk_lo[:, :], chunk_lo[:, :], rows[0:1, NB - 1:NB], None, ALU.is_lt))
                                after(dve.tensor_reduce(chunk_sum[:, :], chunk_lo[:, :], AX.X, ALU.add))
                                after(dve.tensor_copy(chunks_i[:, :], chunk_sum[:, :]))
                                after(dve.tensor_tensor(of_b, upto_b, of_b, ALU.subtract))
                                after(dve.tensor_tensor(from_visit[:, 0:NB], first_b, of_b, ALU.subtract))
                                after(dve.tensor_tensor(change[:, :], from_visit[:, 1:NB + 1], from_visit[:, 0:NB], ALU.subtract))

                        def after_last(k):
                            if k == 0:
                                after(dve.tensor_tensor(past[:, :, :], ids, upto_b.unsqueeze(1).broadcast_to(grid), ALU.is_ge))
                            if k == 1:
                                dve.tensor_reduce(vb[:, :], past[:, :, :], AX.X, ALU.add)
                            if k == 2:
                                after(dve.tensor_tensor(within[:, :, :], past[:, :, :], change[:, :].unsqueeze(1).broadcast_to(grid), ALU.mult))
                            if k == 3:
                                after(dve.tensor_reduce(vt[:, :], within[:, :, :], AX.X, ALU.add))
                            if k == 4:
                                after(dve.tensor_tensor(vt[:, :], vt[:, :], visit_id[:, :], ALU.add))
                                after(dve.tensor_scalar(vt[:, :], vt[:, :], from_visit[:, 0:1], None, ALU.add))
                                after(dve.tensor_scalar(vt[:, :], vt[:, :], float(ET - 1), None, ALU.min))
                                dve.tensor_copy(vt_i[:, :], vt[:, :]).then_inc(visits_ready, 1)
                                dve.tensor_copy(vb_i[:, :], vb[:, :]).then_inc(visits_ready, 1)

                        rounds(dve, step, before, after_last)
                        dve.wait_ge(h_copied, ahead(NT))

            with ExitStack() as scope:
                kmax = sb(scope, "kmax", [P, HID])
                kcol = sb(scope, "kcol", [P, 1])
                kdiag = sb(scope, "kdiag", [P, P])
                head_mask = sb(scope, "head_mask", [P, HID])
                key_sum = sb(scope, "key_sum", [P, 1])
                ctx = sb(scope, "ctx", [P, HID])
                ctxT = sb(scope, "ctxT", [P, HID])
                ctx_out = sb(scope, "ctx_out", [P, D])
                w_qT = sb(scope, "w_qT", [P, D])
                amax_p = sb(scope, "amax_p", [P, HEADS])
                amax_c = sb(scope, "amax_c", [HEADS, 1])
                amax_d = sb(scope, "amax_d", [HEADS, HEADS])
                amax = sb(scope, "amax", [P, HEADS])
                self_z = sb(scope, "self_z", [P, NT, HEADS])

                pool_ready = sem("pool_ready")
                kmax_ready = sem("kmax_ready")
                kmax_turned = sem("kmax_turned")
                kdiag_ready = sem("kdiag_ready")
                kmax_spread = sem("kmax_spread")
                keys_shifted = sem("keys_shifted")
                keys_exp = sem("keys_exp")
                ctx_summed = sem("ctx_summed")
                ctx_ready = sem("ctx_ready")
                ctx_turned = sem("ctx_turned")
                ctxT_ready = sem("ctxT_ready")
                ctx_out_summed = sem("ctx_out_summed")
                ctx_out_ready = sem("ctx_out_ready")
                w_q_turned = sem("w_q_turned")
                w_qT_ready = sem("w_qT_ready")
                w_mix_summed = sem("w_mix_summed")
                w_mix_ready = sem("w_mix_ready")
                amax_ready = sem("amax_ready")
                amax_turned = sem("amax_turned")
                amax_diag = sem("amax_diag")
                amax_spread = sem("amax_spread")
                self_logits = sem("self_logits")
                self_exp = sem("self_exp")


                v2 = Chain(sem("v2"))
                g2 = Chain(sem("g2"))

                with nc.Block() as block:
                    @block.gpsimd
                    def _(pool):
                        g2.done(pool.memset(head_mask[:, :], 0.0))
                        pool.wait_ge(g2.sem, g2.n)
                        for h in range(HEADS):
                            g2.done(pool.memset(head_mask[h * DH:(h + 1) * DH, h * DH:(h + 1) * DH], 1.0))
                            pool.wait_ge(g2.sem, g2.n)
                        pool.memset(acc[:, NB, :], 0.0).then_inc(pool_ready, 1)
                        pool.memset(adc[:, NB, :], 0.0).then_inc(pool_ready, 1)
                        pool.wait_ge(self_exp, 1)
                        pool.tensor_tensor(acc[:, 0:NB, 0:D].rearrange("p t (h c) -> p t h c", c=C),
                                           hs[:, :, 0:D].rearrange("p t (h c) -> p t h c", c=C),
                                           acc[:, 0:NB, D:ROW].unsqueeze(3).broadcast_to((P, NB, HEADS, C)), ALU.mult).then_inc(self_ready, 1)

                    @block.vector
                    def _(dve):
                        def after(instruction):
                            v2.done(instruction)
                            dve.wait_ge(v2.sem, v2.n)

                        dve.tensor_reduce(amax_p[:, :], hs[:, :, D:D + HEADS].rearrange("p t h -> p h t"), AX.X, ALU.max).then_inc(amax_ready, 1)
                        after(dve.tensor_reduce(kmax[:, :], kv[:, 0:NT - 1, 0:HID].rearrange("p t c -> p c t"), AX.X, ALU.max))
                        dve.tensor_tensor(kmax[0:LAST, :], kmax[0:LAST, :], kv[0:LAST, NT - 1, 0:HID], ALU.max).then_inc(kmax_ready, 1)
                        dve.wait_ge(amax_turned, 1)
                        after(dve.tensor_reduce(amax_c[:, :], bank[1][0:HEADS, 0:P], AX.X, ALU.max))
                        dve.tensor_scalar(amax_d[:, :], ident[0:HEADS, 0:HEADS], amax_c[:, 0:1], None, ALU.mult).then_inc(amax_diag, 1)
                        dve.wait_ge(kmax_turned, 1)
                        after(dve.tensor_reduce(kcol[:, :], bank[0][:, 0:P], AX.X, ALU.max))
                        dve.tensor_scalar(kdiag[:, :], ident[:, :], kcol[:, 0:1], None, ALU.mult).then_inc(kdiag_ready, 1)
                        dve.wait_ge(amax_spread, 1)
                        after(dve.tensor_copy(amax[:, :], bank[3][:, 0:HEADS]))
                        a_src, a_dst = hs[:, :, D:D + HEADS], hs[:, :, D + HEADS:D + 2 * HEADS]
                        logit, shift = adc[:, 0:NB, 0:HEADS], adc[:, 0:NB, HEADS:2 * HEADS]
                        dve.tensor_copy(logit, a_dst)
                        after(dve.tensor_tensor(shift, a_dst, amax[:, :].unsqueeze(1).broadcast_to((P, NT, HEADS)), ALU.add))
                        after(dve.scalar_tensor_tensor(out=shift, in0=shift, scalar=SLOPE, in1=shift, op0=ALU.mult, op1=ALU.max))
                        after(dve.tensor_tensor(self_z[:, :, :], a_src, a_dst, ALU.add))
                        after(dve.scalar_tensor_tensor(out=self_z[:, :, :], in0=self_z[:, :, :], scalar=SLOPE, in1=self_z[:, :, :],
                                                       op0=ALU.mult, op1=ALU.max))
                        dve.tensor_tensor(self_z[:, :, :], self_z[:, :, :], shift, ALU.subtract).then_inc(self_logits, 1)

                        dve.wait_ge(kmax_spread, 1)
                        for i in range(NR):
                            keys = kv[:, i * UNROLL:(i + 1) * UNROLL, 0:HID]
                            dve.tensor_tensor(keys, keys, bank[2][:, 0:HID].unsqueeze(1).broadcast_to((P, UNROLL, HID)),
                                              ALU.subtract).then_inc(keys_shifted, 1)

                        dve.wait_ge(ctx_summed, 1)
                        after(dve.reciprocal(key_sum[:, :], bank[0][:, HID:HID + 1]))
                        after(dve.tensor_scalar(ctx[:, :], bank[0][:, 0:HID], key_sum[:, 0:1], QSCALE, ALU.mult, ALU.mult))
                        dve.wait_ge(pool_ready, 2)
                        dve.tensor_tensor(ctx[:, :], ctx[:, :], head_mask[:, :], ALU.mult).then_inc(ctx_ready, 1)
                        dve.wait_ge(w_q_turned, 1)
                        dve.tensor_copy(w_qT[:, :], bank[6][:, 0:D]).then_inc(w_qT_ready, 1)
                        dve.wait_ge(ctx_turned, 1)
                        dve.tensor_copy(ctxT[:, :], bank[1][:, 0:P]).then_inc(ctxT_ready, 1)
                        dve.wait_ge(ctx_out_summed, 1)
                        dve.tensor_copy(ctx_out[:, :], bank[2][:, 0:D]).then_inc(ctx_out_ready, 1)
                        dve.wait_ge(w_mix_summed, 1)
                        dve.tensor_copy(w_mix[:, :, :], bank[3][:, :].rearrange("p (k d) -> p k d", k=KD)).then_inc(w_mix_ready, 1)
                        dve.wait_ge(w_mix_ready, 1)

                    @block.scalar
                    def _(act):
                        act.wait_ge(self_logits, 1)
                        act.activation(acc[:, 0:NB, D:ROW], self_z[:, :, :], ACT.Exp).then_inc(self_exp, 1)
                        for i in range(NR):
                            keys = kv[:, i * UNROLL:(i + 1) * UNROLL, 0:HID]
                            act.wait_ge(keys_shifted, i + 1)
                            act.activation(keys, keys, ACT.Exp).then_inc(keys_exp, 1)

                    @block.tensor
                    def _(pe):
                        pe.wait_ge(amax_ready, 1)
                        pe.transpose(bank[1][0:HEADS, 0:P], amax_p[:, :], ident[:, :]).then_inc(amax_turned, 1)
                        pe.wait_ge(kmax_ready, 1)
                        pe.transpose(bank[0][:, 0:P], kmax[:, :], ident[:, :]).then_inc(kmax_turned, 1)
                        pe.wait_ge(amax_diag, 1)
                        pe.matmul(bank[3][:, 0:HEADS], ones[0:HEADS, :], amax_d[:, :], start=True, stop=True).then_inc(amax_spread, 1)
                        pe.wait_ge(kdiag_ready, 1)
                        pe.matmul(bank[2][:, 0:P], ones[:, :], kdiag[:, :], start=True, stop=True).then_inc(kmax_spread, 1)
                        for c in range(KD):
                            tr = pe.transpose(bank[6][:, c * P:(c + 1) * P], w_q[:, c, :], ident[:, :])
                        tr.then_inc(w_q_turned, 1)
                        for t in range(NT):
                            if t % UNROLL == 0:
                                pe.wait_ge(keys_exp, t // UNROLL + 1)
                            n = P if t < NT - 1 else LAST
                            mm = pe.matmul(bank[0][:, 0:HID + 1], kv[0:n, t, 0:HID], kv[0:n, t, HID:2 * HID + 1],
                                           start=(t == 0), stop=(t == NT - 1))
                        mm.then_inc(ctx_summed, 1)
                        pe.wait_ge(ctx_ready, 1)
                        pe.transpose(bank[1][:, 0:P], ctx[:, :], ident[:, :]).then_inc(ctx_turned, 1)
                        pe.wait_ge(ctxT_ready, 1)
                        pe.wait_ge(bias_in, 48)
                        pe.matmul(bank[2][:, 0:D], ctxT[:, :], w_o[:, :], start=True, stop=True).then_inc(ctx_out_summed, 1)
                        pe.wait_ge(ctx_out_ready, 1)
                        pe.wait_ge(w_qT_ready, 1)
                        for c in range(KD):
                            mm = pe.matmul(bank[3][:, c * D:(c + 1) * D], w_qT[:, c * P:(c + 1) * P], ctx_out[:, :],
                                           start=True, stop=True)
                        mm.then_inc(w_mix_summed, 1)


        w2_in = sem("w2_in")
        w2_sb = sb(whole, "w2_sb", [P, NX * KF, D])
        with ExitStack() as scope:
            table = sb(scope, "table", [1, 2, CH], I32)
            gathered = sb(scope, "gathered", [P, RING, G, ROW])
            index = sb(scope, "index", [P, RING, G], U32)
            local = sb(scope, "local", [P, RING, G])
            one_hot = sb(scope, "one_hot", [P, RING, G, P])
            one_hotT = sb(scope, "one_hotT", [P, 2, G, P])
            z = sb(scope, "z", [P, G, HEADS])
            turned_bank, ad_bank, sum_bank = bank[0:2], bank[2:4], bank[4:8]

            table_in = sem("table_in")
            cols_ready = sem("cols_ready")
            gather_done = [sem(f"gather_done{r}") for r in range(RING)]
            hot_ready = sem("hot_ready")
            hot_turned = sem("hot_turned")
            hotT_ready = sem("hotT_ready")
            ad_ready = sem("ad_ready")
            logit_step = sem("logit_step")
            logits_ready = sem("logits_ready")
            exp_ready = sem("exp_ready")
            weighted = sem("weighted")
            summed = sem("summed")
            added = sem("added")

            def steps(eng, c, step):
                for r in range(RING):
                    step(c * NGRP + r, r, r, RING)
                with eng.Fori(1, NGRP // RING - 1) as i:
                    for r in range(RING):
                        step(c * NGRP + i * RING + r, i * RING + r, r, RING)
                for r in range(RING):
                    step(c * NGRP + NGRP - RING + r, NGRP - RING + r, r, RING - 1 - r)

            with nc.Block() as block:
                @block.sync
                def _(sp):
                    chunks = sp.value_load(chunks_i[0:1, 0:1], min_val=1, max_val=MAXCHUNK)
                    with sp.Fori(0, chunks) as c:
                        first = sp.snap(c * CH)
                        sp.wait_ge(added, from_one(first))
                        sp.sem_inc(waited, 1)
                        sp.dma_start(table[0:1, 0, :], visit_tile[bass.ds(first, CH)].unsqueeze(0)).then_inc(table_in, 16)
                        sp.dma_start(table[0:1, 1, :], visit_block[bass.ds(first, CH)].unsqueeze(0)).then_inc(table_in, 16)
                        with sp.If(c == 0):
                            for e in range(NX):
                                sp.wait_ge(added, from_one(2 * G * (e + 1)))
                                sp.dma_start(w2_sb[:, e * KF:(e + 1) * KF, :],
                                             w2[e:e + 1, :, :].rearrange("e (k p) d -> p (e k) d", p=P)).then_inc(w2_in, 16)

                @block.gpsimd
                def _(pool):
                    for counts in (summed, added, logits_ready):
                        pool.sem_inc(counts, 1)
                    chunks = pool.value_load(chunks_i[0:1, 0:1], min_val=1, max_val=MAXCHUNK)
                    with pool.Fori(0, chunks) as c:
                        with pool.Fori(0, NGRP // RING) as i:
                            for r in range(RING):
                                pool.wait_ge(cols_ready, c * NGRP + i * RING + r + 1)
                                pool.sem_inc(waited, 1)
                                for j in range(G):
                                    pool.indirect_dma_start(gathered[:, r, j, :], None, h_table,
                                                            bass.IndirectOffsetOnAxis(ap=index[:, r, j:j + 1], axis=0)
                                                            ).then_inc(gather_done[r], 16)

                @block.scalar
                def _(act):
                    chunks = act.value_load(chunks_i[0:1, 0:1], min_val=1, max_val=MAXCHUNK)
                    tile_regs = [act.alloc_register(f"act_tile{j}") for j in range(G)]
                    block_regs = [act.alloc_register(f"act_block{j}") for j in range(G)]

                    def columns(s, r, free):
                        act.load(tile_regs, table[0:1, 0, bass.ds(s * G, G)])
                        act.load(block_regs, table[0:1, 1, bass.ds(s * G, G)])
                        act.wait_ge(summed, from_one(free))
                        for j in range(G):
                            t = act.snap(tile_regs[j], min_val=0, max_val=ET - 1)
                            b = act.snap(block_regs[j], min_val=0, max_val=NB)
                            act.activation(index[:, r, j:j + 1], src_col[:, bass.ds(t, 1)], ACT.Copy)
                            op = act.activation(local[:, r, j:j + 1], dst_col[:, bass.ds(t, 1)], ACT.Identity,
                                                bias=minus_base[:, bass.ds(b, 1)])
                        op.then_inc(cols_ready, 1)

                    def turned_out(n, half):
                        act.wait_ge(hot_turned, n)
                        act.activation(one_hotT[:, half, :, :].rearrange("p a b -> p (a b)"), turned_bank[half][:, :],
                                       ACT.Copy).then_inc(hotT_ready, 1)

                    def exps(n, r):
                        act.wait_ge(logits_ready, from_one(n))
                        act.activation(gathered[:, r, :, D:ROW], z[:, :, :], ACT.Exp).then_inc(exp_ready, 1)

                    def step(n, s, r, ahead):
                        if ahead >= 2:
                            act.wait_ge(ad_ready, from_one(n + 1))
                            turned_out(n + 3, r % 2)
                        if ahead >= LEAD:
                            free = n + LEAD - RING + 1 if not isinstance(s, int) or s >= RING else n - r + max(r + LEAD - RING + 1, 0)
                            columns(s + LEAD, (r + LEAD) % RING, free)
                        if ahead >= 1:
                            exps(n + 2, (r + 1) % RING)

                    with act.Fori(0, chunks) as c:
                        act.wait_ge(table_in, c * 32 + 32)
                        act.sem_inc(waited, 1)
                        for r in range(LEAD):
                            columns(r, r, c * NGRP)
                        turned_out(c * NGRP + 1, 0)
                        turned_out(c * NGRP + 2, 1)
                        exps(c * NGRP + 1, 0)
                        steps(act, c, step)

                @block.tensor
                def _(pe):
                    chunks = pe.value_load(chunks_i[0:1, 0:1], min_val=1, max_val=MAXCHUNK)
                    block_regs = [pe.alloc_register(f"pe_block{j}") for j in range(G)]
                    pe.sem_inc(ad_ready, 1)

                    def turn(n, r, half):
                        pe.wait_ge(hot_ready, n)
                        for j in range(G):
                            tr = pe.transpose(turned_bank[half][:, j * P:(j + 1) * P], one_hot[:, r, j, :], ident[:, :])
                        tr.then_inc(hot_turned, 1)

                    def spread(n, half):
                        pe.wait_ge(hotT_ready, n)
                        for j in range(G):
                            b = pe.snap(block_regs[j], min_val=0, max_val=NB)
                            mm = pe.matmul(ad_bank[half][:, j * 2 * HEADS:(j + 1) * 2 * HEADS], one_hotT[:, half, j, :],
                                           flat(adc[:, bass.ds(b, 1), :]), start=True, stop=True)
                        mm.then_inc(ad_ready, 1)

                    def step(n, s, r, ahead):
                        if ahead >= 2:
                            pe.load(block_regs, table[0:1, 1, bass.ds((s + 2) * G, G)])
                            pe.wait_ge(logits_ready, from_one(n + 1))
                            spread(n + 3, r % 2)
                        pe.wait_ge(weighted, n + 1)
                        for j in range(G):
                            pe.wait_ge(added, from_one((n - 1) * G + j + 1 if not isinstance(s, int) or s > 0 else n * G))
                            mm = pe.matmul(sum_bank[j][:, 0:ROW], one_hot[:, r, j, :], gathered[:, r, j, :],
                                           start=True, stop=True)
                        mm.then_inc(summed, 1)
                        if ahead >= 3:
                            turn(n + 4, (r + 3) % RING, (r + 1) % 2)

                    with pe.Fori(0, chunks) as c:
                        pe.wait_ge(table_in, c * 32 + 32)
                        pe.sem_inc(waited, 1)
                        pe.load(block_regs, table[0:1, 1, 0:G])
                        turn(c * NGRP + 1, 0, 0)
                        spread(c * NGRP + 1, 0)
                        turn(c * NGRP + 2, 1, 1)
                        pe.load(block_regs, table[0:1, 1, G:2 * G])
                        spread(c * NGRP + 2, 1)
                        turn(c * NGRP + 3, 2, 0)
                        steps(pe, c, step)

                @block.vector
                def _(dve):
                    chunks = dve.value_load(chunks_i[0:1, 0:1], min_val=1, max_val=MAXCHUNK)
                    block_regs = [dve.alloc_register(f"dve_block{j}") for j in range(G)]

                    def hot(r, j):
                        return dve.tensor_scalar(one_hot[:, r, j, :], iota_row[:, :], local[:, r, j:j + 1], None, ALU.is_equal)

                    def add_sum(n, j):
                        b = dve.snap(block_regs[j], min_val=0, max_val=NB)
                        dve.wait_ge(added, from_one(n * G + j))
                        dve.tensor_tensor(flat(acc[:, bass.ds(b, 1), :]), flat(acc[:, bass.ds(b, 1), :]),
                                          sum_bank[j][:, 0:ROW], ALU.add).then_inc(added, 1)

                    def logits(n, r, half, part):
                        ad = ad_bank[half][:, 0:G * 2 * HEADS].rearrange("p (j a) -> p j a", j=G)
                        if part == 0:
                            dve.wait_ge(ad_ready, from_one(n + 1))
                            dve.tensor_tensor(z[:, :, :], gathered[:, r, :, D:ROW], ad[:, :, 0:HEADS], ALU.add).then_inc(logit_step, 1)
                        elif part == 1:
                            dve.wait_ge(logit_step, n * 2 + 1)
                            dve.scalar_tensor_tensor(out=z[:, :, :], in0=z[:, :, :], scalar=SLOPE, in1=z[:, :, :],
                                                     op0=ALU.mult, op1=ALU.max).then_inc(logit_step, 1)
                        else:
                            dve.wait_ge(logit_step, n * 2 + 2)
                            dve.tensor_tensor(z[:, :, :], z[:, :, :], ad[:, :, HEADS:2 * HEADS], ALU.subtract).then_inc(logits_ready, 1)

                    def weigh(n, r):
                        dve.wait_ge(exp_ready, n + 1)
                        message = gathered[:, r, :, 0:D].rearrange("p j (h c) -> p j h c", c=C)
                        dve.tensor_tensor(message, message,
                                          gathered[:, r, :, D:ROW].unsqueeze(3).broadcast_to((P, G, HEADS, C)),
                                          ALU.mult).then_inc(weighted, 1)

                    with dve.Fori(0, chunks) as c:
                        rounds = c * (NGRP // RING)

                        def step(n, s, r, ahead):
                            before = not isinstance(s, int) or s > 0
                            if before:
                                dve.load(block_regs, table[0:1, 1, bass.ds(s * G - G, G)])
                            weigh(n, r)
                            if ahead >= 3:
                                dve.wait_ge(cols_ready, n + 4)
                            if before:
                                dve.wait_ge(summed, from_one(n))
                            for j in range(G):
                                if before:
                                    add_sum(n - 1, j)
                                if j == 2 and ahead >= 1:
                                    logits(n + 1, (r + 1) % RING, (r + 1) % 2, 2)
                                if ahead >= 3:
                                    op = hot((r + 3) % RING, j)
                                if j == 0 and ahead >= 1:
                                    dve.wait_ge(gather_done[(r + 1) % RING], ring_count(n, s, r))
                                    logits(n + 1, (r + 1) % RING, (r + 1) % 2, 0)
                                if j == 1 and ahead >= 1:
                                    logits(n + 1, (r + 1) % RING, (r + 1) % 2, 1)
                            if ahead >= 3:
                                op.then_inc(hot_ready, 1)

                        def ring_count(n, s, r):
                            uses = (n + 1 - (r + 1) % RING)
                            return uses * (16 * G // RING) + 16 * G

                        dve.wait_ge(table_in, c * 32 + 32)
                        for r in range(3):
                            dve.wait_ge(cols_ready, c * NGRP + r + 1)
                            for j in range(G):
                                op = hot(r, j)
                            op.then_inc(hot_ready, 1)
                        dve.wait_ge(gather_done[0], rounds * 16 * G + 16 * G)
                        for part in range(3):
                            logits(c * NGRP, 0, 0, part)
                        steps(dve, c, step)
                        dve.load(block_regs, table[0:1, 1, CH - G:CH])
                        dve.wait_ge(summed, from_one(c * NGRP + NGRP))
                        for j in range(G):
                            add_sum(c * NGRP + NGRP - 1, j)
        b1_cols = sb(whole, "b1_cols", [P, NX * KF])
        b2_sb = sb(whole, "b2_sb", [P, NX, D])
        middle_pairs = sb(whole, "middle_pairs", [1, 1], I32)
        tile_expert = sb(whole, "tile_expert", [P, UT], I32)
        slot_token = sb(whole, "slot_token", [P, UT])
        slot_read = sb(whole, "slot_read", [P, UT])
        slot_share = sb(whole, "slot_share", [P, UT])
        with ExitStack() as scope:
            w_g = sb(scope, "w_g", [P, KD, NX])
            b_g = sb(scope, "b_g", [P, NX])
            rden = sb(scope, "rden", [P, NT, HEADS])
            xn = sb(scope, "xn2", [P, UNROLL, D])
            xnT_slot = sb(scope, "xn2T_slot", [P, UNROLL, D])
            gate = sb(scope, "gate", [P, NT, NX])
            top = sb(scope, "top", [P, NT, NX])
            top_i = sb(scope, "top_i", [P, NT, NX], U32)
            top_f = sb(scope, "top_f", [P, 2, NT])
            expert_id = sb(scope, "expert_id", [P, NX])
            row_id = sb(scope, "row_id", [P, 1])
            node_id = sb(scope, "node_id", [P, NT])
            valid = sb(scope, "valid", [P, 1])
            absent = sb(scope, "absent", [P, 1])
            b1_rows = sb(scope, "b1_rows", [NX * KF, P])
            zeros = sb(scope, "zeros", [P, D])
            share = sb(scope, "share", [P, 2, NT])
            slot_i = sb(scope, "slot_i", [P, 2, NCHOICE], I32)
            slot_at = sb(scope, "slot_at", [P, 2, NCHOICE])
            spare = flat(xnT[:, :, :])
            sizes = UNROLL * P, UNROLL * UT, UNROLL * 2 * UT
            place, in_tile, what = [], [], []
            for k in range(2):
                at = k * sum(sizes)
                place.append(spare[:, at:at + sizes[0]].rearrange("p (n c) -> p n c", c=P))
                in_tile.append(spare[:, at + sizes[0]:at + sizes[0] + sizes[1]].rearrange("p (n u) -> p n u", u=UT))
                what.append(spare[:, at + sizes[0] + sizes[1]:at + sum(sizes)].rearrange("p (n w u) -> p n w u", w=2, u=UT))
            empty = sb(scope, "empty", [P, UT])
            tile_no = sb(scope, "tile_no", [P, UT])
            before_row = sb(scope, "before_row", [P, P])
            choice = sb(scope, "choice", [P, NCHOICE, NX])
            count = src_col[:, 0:NCHOICE * NX].rearrange("p (n e) -> p n e", e=NX)
            upto_count = dst_col[:, 0:NCHOICE * NX].rearrange("p (n e) -> p n e", e=NX)
            room = sb(scope, "room", [P, NX])
            room_i = sb(scope, "room_i", [P, NX], I32)
            tiles_upto = sb(scope, "tiles_upto", [P, NX])
            start = sb(scope, "start", [P, NX])
            slot_f = sb(scope, "slot_f", [P, NCHOICE])
            past_e = flat(xnT_slot[:, :, :])[:, 0:UT * NX].rearrange("p (u e) -> p u e", e=NX)
            expert_f = sb(scope, "expert_f", [P, UT])
            ratio = sb(scope, "ratio", [P, NT])

            mix_slot = sb(scope, "mix_slot", [P, UNROLL, D])

            slot_ready = sem("slot_ready")
            mixed = sem("mixed")
            mix_added = sem("mix_added")
            gat_scaled = sem("gat_scaled")
            gate_in = sem("gate_in")
            ffn_bias_in = sem("ffn_bias_in")
            den_ready = sem("den_ready")
            gat_ready = sem("gat_ready")
            stats2_ready = sem("stats2_ready")
            x_step = sem("x_step")
            moments2_ready = sem("moments2_ready")
            std2_ready = sem("std2_ready")
            xn2_ready = sem("xn2_ready")
            rstd2_ready = sem("rstd2_ready")
            turned2 = sem("turned2")
            xn2T_ready = sem("xn2T_ready")
            gated = sem("gated")
            pool3 = sem("pool3")
            ratio_ready = sem("ratio_ready")
            exp2_ready = sem("exp2_ready")
            choice_ready = sem("choice_ready")
            b1_in = sem("b1_in")
            b1_turned = sem("b1_turned")
            xn_stored = sem("xn_stored")
            out_started = sem("out_started")
            places_ready = sem("places_ready")
            placed = sem("placed")
            tiles_found = sem("tiles_found")
            what_ready = sem("what_ready")
            zeros_ready = sem("zeros_ready")
            counted = sem("counted")
            v3 = Chain(sem("v3"))
            TURN_BANKS = -(-UNROLL // 2)

            def rounds(eng, step):
                step(1)
                with eng.Fori(2, NR) as i:
                    step(i)

            g3 = Chain(sem("g3"))

            with nc.Block() as block:
                @block.sync
                def _(sp):
                    sp.dma_start(w_g[:, :, :], w_gate.rearrange("(k p) e -> p k e", p=P)).then_inc(gate_in, 16)
                    sp.dma_start(b_g[:, :], b_gate.partition_broadcast(P)).then_inc(gate_in, 16)
                    sp.dma_start(b1_rows[:, :], b1.rearrange("e (k p) -> (e k) p", p=P)).then_inc(b1_in, 16)
                    sp.dma_start(b2_sb[:, :, :], b2.partition_broadcast(P)).then_inc(ffn_bias_in, 16)
                    sp.wait_ge(zeros_ready, 1)
                    sp.dma_start(out[N:N + SPARE, :], zeros[:, :]).then_inc(out_started, 16)
                    for i in range(NR):
                        tiles = slice(i * UNROLL, min((i + 1) * UNROLL, NT - 1))
                        sp.wait_ge(x_step, i + 1)
                        sp.dma_start(out[tiles.start * P:tiles.stop * P, :].rearrange("(t p) d -> p t d", p=P),
                                     xs[:, tiles, :]).then_inc(out_started, 16)
                        sp.wait_ge(xn2_ready, (i + 1) * UNROLL)
                        sp.dma_start(xn_table[i * UNROLL * P:(i + 1) * UNROLL * P, :].rearrange("(t p) d -> p t d", p=P),
                                     xn[:, :, :]).then_inc(xn_stored, 16)
                    sp.dma_start(out[(NT - 1) * P:N, :], xs[0:LAST, NT - 1, :]).then_inc(out_started, 16)
                    sp.wait_ge(xn_stored, 16 * NR)
                    sp.wait_ge(out_started, 16 * (NR + 2))

                @block.gpsimd
                def _(pool):
                    pool.sem_inc(mix_added, 1)
                    pool.sem_inc(mixed, UNROLL)
                    pool.memset(zeros[:, :], 0.0).then_inc(zeros_ready, 1)
                    pool.iota(node_id[:, :], [[P, NT]], base=1, channel_multiplier=1,
                              allow_small_or_imprecise_dtypes=True).then_inc(pool3, 1)
                    pool.iota(expert_id[:, :], [[1, NX]], base=0, channel_multiplier=0,
                              allow_small_or_imprecise_dtypes=True).then_inc(pool3, 1)
                    pool.iota(row_id[:, :], [[0, 1]], base=N + 1, channel_multiplier=1,
                              allow_small_or_imprecise_dtypes=True).then_inc(pool3, 1)
                    pool.iota(tile_no[:, :], [[1, UT]], base=0, channel_multiplier=0,
                              allow_small_or_imprecise_dtypes=True).then_inc(pool3, 1)
                    g3.done(pool.memset(before_row[:, :], 1.0))
                    pool.wait_ge(g3.sem, g3.n)
                    pool.affine_select(out=before_row[:, :], in_=before_row[:, :], compare_op=ALU.is_ge, fill=0.0,
                                       base=-1, pattern=[[1, P]], channel_multiplier=-1).then_inc(pool3, 1)
                    pool.wait_ge(den_ready, 1)
                    pool.wait_ge(bias_in, 48)
                    for i in range(NR):
                        tiles = slice(i * UNROLL, (i + 1) * UNROLL)
                        sums = acc[:, tiles, 0:D].rearrange("p t (h c) -> p t h c", c=C)
                        pool.tensor_tensor(sums, sums, rden[:, tiles, :].unsqueeze(3).broadcast_to((P, UNROLL, HEADS, C)),
                                           ALU.mult).then_inc(gat_scaled, 1)
                        pool.wait_ge(gat_scaled, i + 1)
                        sums = acc[:, tiles, 0:D]
                        pool.tensor_tensor(sums, sums, gat_bias_sb[:, :].unsqueeze(1).broadcast_to((P, UNROLL, D)),
                                           ALU.add).then_inc(gat_ready, 1)
                    for m in range(NCHOICE // UNROLL):
                        pool.wait_ge(tiles_found, m + 1)
                        nodes = slice(m * UNROLL % NT, m * UNROLL % NT + UNROLL)
                        grid = (P, UNROLL, UT)
                        pool.tensor_tensor(what[m % 2][:, :, 0, :], in_tile[m % 2],
                                           node_id[:, nodes].unsqueeze(2).broadcast_to(grid), ALU.mult)
                        pool.tensor_tensor(what[m % 2][:, :, 1, :], in_tile[m % 2],
                                           share[:, m * UNROLL // NT, nodes].unsqueeze(2).broadcast_to(grid), ALU.mult).then_inc(what_ready, 1)

                @block.scalar
                def _(act):
                    def slots(i):
                        for k in range(UNROLL):
                            act.wait_ge(mixed, ahead(i * UNROLL + k + 1 - UNROLL))
                            act.activation(mix_slot[:, k, :], flat(xnT[:, bass.ds(i * UNROLL + k, 1), :]),
                                           ACT.Copy).then_inc(slot_ready, 1)

                    def finish(i):
                        act.wait_ge(moments2_ready, i * UNROLL + UNROLL)
                        act.activation(rstd[:, 0:UNROLL], moments[:, 0:UNROLL, 1], ACT.Sqrt, bias=eps_col[:, :]).then_inc(std2_ready, 1)
                        if not isinstance(i, int) or i > 0:
                            act.wait_ge(gated, i * UNROLL)
                        for b in range(TURN_BANKS):
                            act.wait_ge(turned2, i * TURN_BANKS + b + 1)
                            width = min(2, UNROLL - 2 * b) * D
                            act.activation(flat(xnT_slot[:, :, :])[:, 2 * b * D:2 * b * D + width], bank[b][:, 0:width],
                                           ACT.Copy).then_inc(xn2T_ready, 1)

                    def step(i):
                        slots(i)
                        finish(i - 1)

                    slots(0)
                    rounds(act, step)
                    finish(NR - 1)
                    act.wait_ge(ratio_ready, 1)
                    act.activation(ratio[:, :], ratio[:, :], ACT.Exp).then_inc(exp2_ready, 1)

                @block.tensor
                def _(pe):
                    def mix(i):
                        for k in range(UNROLL):
                            t = i * UNROLL + k
                            pe.wait_ge(slot_ready, t + 1)
                            pe.wait_ge(mix_added, from_one(i * UNROLL if k < 4 else t - 3))
                            for c in range(KD):
                                mm = pe.matmul(bank[3 + k % 4][:, 0:D], mix_slot[:, k, c * P:(c + 1) * P], w_mix[:, c, :],
                                               start=(c == 0), stop=(c == KD - 1))
                            mm.then_inc(mixed, 1)

                    def gates(i):
                        for k in range(UNROLL):
                            pe.wait_ge(xn2_ready, i * UNROLL + k + 1)
                            for c in range(KD):
                                at = (k % 2) * D + c * P
                                tr = pe.transpose(bank[k // 2][:, at:at + P], xn[:, k, c * P:(c + 1) * P], ident[:, :])
                            if k % 2 == 1 or k == UNROLL - 1:
                                tr.then_inc(turned2, 1)
                        for k in range(UNROLL):
                            if k % 2 == 0:
                                pe.wait_ge(xn2T_ready, i * TURN_BANKS + k // 2 + 1)
                            logits = bank[7][:, bass.ds((i * UNROLL + k) * NX, NX)]
                            for c in range(KD):
                                mm = pe.matmul(logits, xnT_slot[:, k, c * P:(c + 1) * P], w_g[:, c, :],
                                               start=(c == 0), stop=(c == KD - 1))
                            mm.then_inc(gated, 1)

                    def step(i):
                        mix(i)
                        gates(i - 1)

                    mix(0)
                    pe.wait_ge(gate_in, 32)
                    rounds(pe, step)
                    gates(NR - 1)
                    pe.wait_ge(choice_ready, 1)
                    pe.wait_ge(b1_in, 16)
                    pe.transpose(bank[2][:, 0:NX * KF], b1_rows[:, :], ident[0:NX * KF, 0:NX * KF]).then_inc(b1_turned, 1)
                    flat_choice = choice[:, :, :].rearrange("p n e -> p (n e)")
                    pe.matmul(bank[0][:, 0:NCHOICE * NX], before_row[:, :], flat_choice, start=True, stop=True)
                    pe.matmul(bank[1][:, 0:NCHOICE * NX], ones[:, :], flat_choice, start=True, stop=True).then_inc(counted, 1)
                    for n in range(NCHOICE):
                        pe.wait_ge(places_ready, n // UNROLL + 1)
                        pe.wait_ge(what_ready, n // UNROLL + 1)
                        m, k = n // UNROLL, n % UNROLL
                        pe.matmul(bank[3][:, 0:2 * UT], place[m % 2][:, k, :], what[m % 2][:, k, :, :].rearrange("p a b -> p (a b)"),
                                  start=(n == 0), stop=(n == NCHOICE - 1)).then_inc(placed, 1)

                @block.vector
                def _(dve):
                    def after(instruction):
                        v3.done(instruction)
                        dve.wait_ge(v3.sem, v3.n)

                    dve.reciprocal(rden[:, :, :], acc[:, 0:NB, D:ROW]).then_inc(den_ready, 1)

                    def add_mix(i):
                        for k in range(UNROLL):
                            t = i * UNROLL + k
                            dve.wait_ge(mixed, ahead(t + 1))
                            row = flat(xs[:, bass.ds(t, 1), :])
                            dve.tensor_tensor(row, row, bank[3 + k % 4][:, 0:D], ALU.add).then_inc(mix_added, 1)

                    def moments_of(i):
                        dve.wait_ge(gat_ready, i + 1)
                        dve.wait_ge(mix_added, from_one(i * UNROLL + UNROLL))
                        some = xs[:, bass.ds(i * UNROLL, UNROLL), :]
                        dve.scalar_tensor_tensor(out=some, in0=acc[:, bass.ds(i * UNROLL, UNROLL), 0:D], scalar=0.0, in1=some,
                                                 op0=ALU.max, op1=ALU.add).then_inc(x_step, 1)
                        dve.wait_ge(x_step, i + 1)
                        dve.sem_inc(waited, 1)
                        for k in range(UNROLL):
                            dve.bn_stats(stats[:, k, :], flat(xs[:, bass.ds(i * UNROLL + k, 1), :])).then_inc(stats2_ready, 1)
                        dve.wait_ge(stats2_ready, i * UNROLL + UNROLL)
                        dve.sem_inc(waited, 1)
                        if not isinstance(i, int) or i > 0:
                            dve.wait_ge(xn2_ready, i * UNROLL)
                            dve.sem_inc(waited, 1)
                        for k in range(UNROLL):
                            dve.bn_aggr(moments[:, k, :], stats[:, k, :]).then_inc(moments2_ready, 1)

                    def normalise(i):
                        dve.wait_ge(std2_ready, i + 1)
                        dve.reciprocal(rstd[:, 0:UNROLL], rstd[:, 0:UNROLL]).then_inc(rstd2_ready, 1)
                        dve.wait_ge(rstd2_ready, i + 1)
                        if not isinstance(i, int) or i > 0:
                            dve.wait_ge(turned2, i * TURN_BANKS)
                            dve.wait_ge(xn_stored, i * 16)
                        for k in range(UNROLL):
                            dve.tensor_scalar(xn[:, k, :], flat(xs[:, bass.ds(i * UNROLL + k, 1), :]), moments[:, k, 0:1],
                                              rstd[:, k:k + 1], ALU.subtract, ALU.mult).then_inc(xn2_ready, 1)

                    def step(i):
                        normalise(i - 1)
                        add_mix(i)
                        moments_of(i)

                    add_mix(0)
                    moments_of(0)
                    rounds(dve, step)
                    normalise(NR - 1)
                    dve.wait_ge(gated, NT)
                    dve.wait_ge(gate_in, 32)
                    after(dve.tensor_tensor(gate[:, :, :], bank[7][:, 0:NT * NX].rearrange("p (t e) -> p t e", e=NX),
                                            b_g[:, :].unsqueeze(1).broadcast_to((P, NT, NX)), ALU.add))
                    for t in range(NT):
                        dve.max(top[:, t, :], gate[:, t, :]).then_inc(v3.sem, 1)
                    v3.n += NT
                    dve.wait_ge(v3.sem, v3.n)
                    for t in range(NT):
                        dve.max_index(top_i[:, t, :], top[:, t, :], gate[:, t, :]).then_inc(v3.sem, 1)
                    v3.n += NT
                    dve.tensor_tensor(ratio[:, :], top[:, :, 1], top[:, :, 0], ALU.subtract).then_inc(ratio_ready, 1)
                    dve.wait_ge(v3.sem, v3.n)
                    after(dve.tensor_copy(top_f[:, :, :], top_i[:, :, 0:2].rearrange("p t k -> p k t")))
                    dve.wait_ge(pool3, 5)
                    for k in range(2):
                        after(dve.tensor_tensor(choice[:, k * NT:(k + 1) * NT, :], top_f[:, k, :].unsqueeze(2).broadcast_to((P, NT, NX)),
                                                expert_id[:, :].unsqueeze(1).broadcast_to((P, NT, NX)), ALU.is_equal))
                    after(dve.tensor_scalar(valid[:, :], node_id[:, NT - 1:NT], float(N), None, ALU.is_le))
                    both = choice[:, NT - 1:NCHOICE:NT, :]
                    dve.tensor_scalar(both, both, valid[:, 0:1], None, ALU.mult).then_inc(choice_ready, 1)
                    dve.tensor_scalar(absent[:, :], valid[:, :], -float(UT * P), float(UT * P), ALU.mult, ALU.add)
                    dve.wait_ge(exp2_ready, 1)
                    after(dve.tensor_scalar(share[:, 1, :], ratio[:, :], 1.0, None, ALU.add))
                    after(dve.reciprocal(share[:, 0, :], share[:, 1, :]))
                    after(dve.tensor_tensor(share[:, 1, :], ratio[:, :], share[:, 0, :], ALU.mult))
                    dve.wait_ge(counted, 1)
                    after(dve.tensor_copy(count[:, :, :], bank[1][:, 0:NCHOICE * NX].rearrange("p (n e) -> p n e", e=NX)))
                    for e in range(NX):
                        op = dve.tensor_tensor_scan(upto_count[:, :, e], ones[:, 0:NCHOICE], count[:, :, e], 0.0, ALU.mult, ALU.add)
                    after(op)
                    after(dve.tensor_scalar(room_i[:, :], upto_count[:, NCHOICE - 1, :], float(P - 1), None, ALU.add))
                    after(dve.tensor_scalar(room_i[:, :], room_i[:, :], P.bit_length() - 1, None, ALU.arith_shift_right))
                    after(dve.tensor_copy(room[:, :], room_i[:, :]))
                    after(dve.tensor_tensor_scan(tiles_upto[:, :], ones[:, 0:NX], room[:, :], 0.0, ALU.mult, ALU.add))
                    after(dve.tensor_tensor(start[:, :], tiles_upto[:, :], room[:, :], ALU.subtract))
                    after(dve.tensor_scalar(middle_pairs[:, :], tiles_upto[0:1, NX - 1:NX], -5.0, None, ALU.add))
                    after(dve.tensor_scalar(middle_pairs[:, :], middle_pairs[:, :], 1, None, ALU.arith_shift_right))
                    after(dve.tensor_scalar(start[:, :], start[:, :], float(P), None, ALU.mult))
                    after(dve.tensor_tensor(upto_count[:, :, :], upto_count[:, :, :], count[:, :, :], ALU.subtract))
                    after(dve.tensor_tensor(upto_count[:, :, :], upto_count[:, :, :],
                                            start[:, :].unsqueeze(1).broadcast_to((P, NCHOICE, NX)), ALU.add))
                    after(dve.tensor_tensor(upto_count[:, :, :], upto_count[:, :, :],
                                            bank[0][:, 0:NCHOICE * NX].rearrange("p (n e) -> p n e", e=NX), ALU.add))
                    after(dve.tensor_tensor(upto_count[:, :, :], upto_count[:, :, :], choice[:, :, :], ALU.mult))
                    after(dve.tensor_reduce(slot_f[:, :], upto_count[:, :, :], AX.X, ALU.add))
                    last = slot_f[:, NT - 1:NCHOICE:NT]
                    after(dve.tensor_scalar(last, last, absent[:, 0:1], None, ALU.add))
                    after(dve.tensor_copy(slot_i[:, 0, :], slot_f[:, :]))
                    after(dve.tensor_scalar(slot_i[:, 1, :], slot_i[:, 0, :], P.bit_length() - 1, None, ALU.arith_shift_right))
                    after(dve.tensor_scalar(slot_i[:, 0, :], slot_i[:, 0, :], P - 1, None, ALU.bitwise_and))
                    after(dve.tensor_copy(slot_at[:, :, :], slot_i[:, :, :]))
                    for m in range(NCHOICE // UNROLL):
                        if m >= 2:
                            dve.wait_ge(placed, (m - 1) * UNROLL)
                        some = slice(m * UNROLL, (m + 1) * UNROLL)
                        grid = (P, UNROLL, UT)
                        dve.tensor_tensor(in_tile[m % 2], tile_no[:, :].unsqueeze(1).broadcast_to(grid),
                                          slot_at[:, 1, some].unsqueeze(2).broadcast_to(grid), ALU.is_equal).then_inc(tiles_found, 1)
                        dve.tensor_tensor(place[m % 2], iota_row[:, :].unsqueeze(1).broadcast_to((P, UNROLL, P)),
                                          slot_at[:, 0, some].unsqueeze(2).broadcast_to((P, UNROLL, P)), ALU.is_equal).then_inc(places_ready, 1)
                    grid = (P, UT, NX)
                    after(dve.tensor_tensor(past_e[:, :, :], tile_no[:, :].unsqueeze(2).broadcast_to(grid),
                                            tiles_upto[:, :].unsqueeze(1).broadcast_to(grid), ALU.is_ge))
                    after(dve.tensor_reduce(expert_f[:, :], past_e[:, :, :], AX.X, ALU.add))
                    after(dve.tensor_scalar(expert_f[:, :], expert_f[:, :], float(NX - 1), None, ALU.min))
                    after(dve.tensor_copy(tile_expert[:, :], expert_f[:, :]))
                    dve.wait_ge(b1_turned, 1)
                    dve.tensor_copy(b1_cols[:, :], bank[2][:, 0:NX * KF])
                    dve.wait_ge(placed, NCHOICE)
                    after(dve.tensor_copy(slot_token[:, :], bank[3][:, 0:UT]))
                    dve.tensor_copy(slot_share[:, :], bank[3][:, UT:2 * UT])
                    after(dve.tensor_scalar(empty[:, :], slot_token[:, :], 0.0, None, ALU.is_equal))
                    after(dve.tensor_scalar(empty[:, :], empty[:, :], row_id[:, 0:1], -1.0, ALU.mult, ALU.add))
                    after(dve.tensor_tensor(slot_token[:, :], slot_token[:, :], empty[:, :], ALU.add))
                    after(dve.tensor_scalar(slot_read[:, :], slot_token[:, :], float(N - 1), None, ALU.min))

        with ExitStack() as scope:
            w1_slot = sb(scope, "w1_slot", [P, 2, KD, FF])
            xg = sb(scope, "xg", [P, 2, D])
            xgT = sb(scope, "xgT", [P, 2, D])
            hiddenT = sb(scope, "hiddenT", [P, 2, FF])
            y = sb(scope, "y", [P, 2, D])
            b1_slot = sb(scope, "b1_slot", [P, 2, KF])
            read_index = sb(scope, "read_index", [P, 2], U32)
            add_index = sb(scope, "add_index", [P, 2], U32)

            w1_in = [sem(f"w1_in{k}") for k in range(2)]
            xg_in = [sem(f"xg_in{k}") for k in range(2)]
            read_ready = sem("read_ready")
            xg_turned = sem("xg_turned")
            xgT_ready = sem("xgT_ready")
            b1_ready = sem("b1_ready")
            hidden_summed = sem("hidden_summed")
            hidden_ready = sem("hidden_ready")
            y_summed = sem("y_summed")
            y_biased = sem("y_biased")
            y_ready = sem("y_ready")
            y_added = sem("y_added")

            def tiles(eng, step):
                middle = eng.value_load(middle_pairs[0:1, 0:1], min_val=MINPAIRS - 3, max_val=UT // 2 - 3) + 1
                for u in range(2):
                    step(u, u, 9)
                with eng.Fori(1, middle) as i:
                    for k in range(2):
                        step(i * 2 + k, k, 9)
                for u in range(4):
                    step(middle * 2 + u, u % 2, 3 - u)
                return middle

            def uses(u, k):
                return u // 2 + 1 if isinstance(u, int) else (u - k) // 2 + 1

            with nc.Block() as block:
                @block.sync
                def _(sp):
                    def load(u, k):
                        e = sp.value_load(tile_expert[0:1, bass.ds(u, 1)], min_val=0, max_val=NX - 1)
                        return w1[bass.ds(e, 1), :, :].rearrange("a (k p) f -> p (a k) f", p=P)

                    for u in range(2):
                        sp.dma_start(w1_slot[:, u, :, :], load(u, u)).then_inc(w1_in[u], 16)

                    def step(u, k, ahead):
                        if ahead >= 2:
                            rows = load(u + 2, k)
                            sp.wait_ge(hidden_summed, 2 * u + 2)
                            sp.dma_start(w1_slot[:, k, :, :], rows).then_inc(w1_in[k], 16)

                    tiles(sp, step)

                @block.gpsimd
                def _(pool):
                    def read(u, k):
                        pool.wait_ge(read_ready, u + 1)
                        pool.sem_inc(waited, 1)
                        pool.indirect_dma_start(xg[:, k, :], None, xn_table,
                                                bass.IndirectOffsetOnAxis(ap=read_index[:, k:k + 1], axis=0)).then_inc(xg_in[k], 16)

                    def step(u, k, ahead):
                        if ahead >= 3:
                            read(u + 3, 1 - k)
                        if not isinstance(u, int) or u > 0:
                            pool.wait_ge(y_added, u * 16)
                            pool.sem_inc(waited, 1)
                        pool.wait_ge(y_ready, u + 1)
                        pool.sem_inc(waited, 1)
                        pool.indirect_dma_start(out, bass.IndirectOffsetOnAxis(ap=add_index[:, k:k + 1], axis=0),
                                                y[:, k, :], None, compute_op=ALU.add).then_inc(y_added, 16)

                    read(0, 0)
                    read(1, 1)
                    read(2, 0)
                    middle = tiles(pool, step)
                    pool.wait_ge(y_added, (middle + 2) * 32)

                @block.scalar
                def _(act):
                    def turned_in(u, k):
                        act.wait_ge(xg_turned, u + 1)
                        act.activation(xgT[:, k, :], bank[0][:, 0:D], ACT.Copy).then_inc(xgT_ready, 1)

                    def gelu(u, k):
                        act.wait_ge(b1_ready, u + 1)
                        for half in range(2):
                            act.wait_ge(hidden_summed, 2 * u + half + 1)
                            for f in range(KF // 2):
                                g = half * (KF // 2) + f
                                op = act.activation(hiddenT[:, k, g * P:(g + 1) * P], bank[1 + 2 * k + half][:, f * P:(f + 1) * P],
                                                    ACT.Gelu, bias=b1_slot[:, k, g:g + 1])
                            op.then_inc(hidden_ready, 1)

                    def step(u, k, ahead):
                        if ahead >= 1:
                            gelu(u + 1, 1 - k)
                        if ahead >= 2:
                            turned_in(u + 2, k)

                    turned_in(0, 0)
                    turned_in(1, 1)
                    gelu(0, 0)
                    tiles(act, step)

                @block.tensor
                def _(pe):
                    pe.wait_ge(w2_in, 16 * NX)

                    def turn_in(u, k):
                        if not isinstance(u, int) or u > 0:
                            pe.wait_ge(xgT_ready, u)
                        pe.wait_ge(xg_in[k], uses(u, k) * 16)
                        for c in range(KD):
                            tr = pe.transpose(bank[0][:, c * P:(c + 1) * P], xg[:, k, c * P:(c + 1) * P], ident[:, :])
                        tr.then_inc(xg_turned, 1)

                    def widen(u, k):
                        pe.wait_ge(xgT_ready, u + 1)
                        pe.wait_ge(w1_in[k], uses(u, k) * 16)
                        for f in range(KF):
                            for c in range(KD):
                                mm = pe.matmul(bank[1 + 2 * k + f // 4][:, f % 4 * P:(f % 4 + 1) * P],
                                               w1_slot[:, k, c, f * P:(f + 1) * P], xgT[:, k, c * P:(c + 1) * P],
                                               start=(c == 0), stop=(c == KD - 1))
                            if f % 4 == 3:
                                mm.then_inc(hidden_summed, 1)

                    def step(u, k, ahead):
                        e = pe.value_load(tile_expert[0:1, bass.ds(u, 1)], min_val=0, max_val=NX - 1)
                        if ahead >= 1:
                            widen(u + 1, 1 - k)
                        if ahead >= 2:
                            turn_in(u + 2, k)
                        for f in range(KF):
                            if f % 4 == 0:
                                pe.wait_ge(hidden_ready, 2 * u + f // 4 + 1)
                            if f == 0 and (not isinstance(u, int) or u >= 2):
                                pe.wait_ge(y_biased, u - 1)
                            mm = pe.matmul(bank[5 + k][:, 0:D], hiddenT[:, k, f * P:(f + 1) * P],
                                           flat(w2_sb[:, bass.ds(e * KF + f, 1), :]), start=(f == 0), stop=(f == KF - 1))
                        mm.then_inc(y_summed, 1)

                    turn_in(0, 0)
                    turn_in(1, 1)
                    widen(0, 0)
                    tiles(pe, step)

                @block.vector
                def _(dve):
                    def index(u, k):
                        if not isinstance(u, int) or u >= 2:
                            dve.wait_ge(xg_turned, u - 1)
                        dve.tensor_copy(read_index[:, k:k + 1], slot_read[:, bass.ds(u, 1)]).then_inc(read_ready, 1)

                    def biases(u, k):
                        e = dve.value_load(tile_expert[0:1, bass.ds(u, 1)], min_val=0, max_val=NX - 1)
                        if not isinstance(u, int) or u >= 2:
                            dve.wait_ge(hidden_ready, 2 * u - 2)
                        dve.tensor_copy(b1_slot[:, k, :], b1_cols[:, bass.ds(e * KF, KF)]).then_inc(b1_ready, 1)

                    def step(u, k, ahead):
                        if ahead >= 3:
                            index(u + 3, 1 - k)
                        if ahead >= 2:
                            biases(u + 2, k)
                        e = dve.value_load(tile_expert[0:1, bass.ds(u, 1)], min_val=0, max_val=NX - 1)
                        dve.wait_ge(y_summed, u + 1)
                        if not isinstance(u, int) or u >= 2:
                            dve.wait_ge(y_added, (u - 1) * 16)
                        dve.tensor_copy(add_index[:, k:k + 1], slot_token[:, bass.ds(u, 1)])
                        dve.tensor_tensor(y[:, k, :], bank[5 + k][:, 0:D], flat(b2_sb[:, bass.ds(e, 1), :]), ALU.add).then_inc(y_biased, 1)
                        dve.wait_ge(y_biased, u + 1)
                        dve.tensor_scalar(y[:, k, :], y[:, k, :], slot_share[:, bass.ds(u, 1)], None, ALU.mult).then_inc(y_ready, 1)

                    for u in range(2):
                        index(u, u)
                        biases(u, u)
                    index(2, 0)
                    tiles(dve, step)


_INS = ['x', 'src', 'dst', 'L0_gnn_W', 'L0_gnn_att_src', 'L0_gnn_att_dst', 'L0_gnn_bias', 'L0_mix_W_qkv', 'L0_mix_W_out',
        'L0_mix_b_out', 'L0_ffn_Wg', 'L0_ffn_bg', 'L0_ffn_W1', 'L0_ffn_b1', 'L0_ffn_W2', 'L0_ffn_b2']


def kernel(**inputs):
    import numpy as np
    import concourse.bacc as bacc
    from concourse.bass_utils import run_bass_kernel_spmd

    nc = bacc.Bacc("TRN2", target_bir_lowering=False, num_devices=1)
    arrays, args = {}, []
    for name in _INS:
        a = np.ascontiguousarray(inputs[name])
        arrays[f"in_{name}"] = a
        args.append(nc.dram_tensor(f"in_{name}", a.shape, mybir.dt.from_np(a.dtype), kind="ExternalInput").ap())
    out = nc.dram_tensor("out", (N + SPARE, D), F32, kind="ExternalOutput").ap()
    graph_layer(nc, *args, out)
    result = run_bass_kernel_spmd(nc, [arrays], core_ids=[0])
    return result.results[0]["out"][:N]
```
